# Optimizing a Trainium2 kernel written in Bass

```python
import numpy as np
import jax
import jax.numpy as jnp

def _softmax(x, axis=-1):
    return jax.nn.softmax(x, axis=axis)

def _gelu(x):
    return jax.nn.gelu(x, approximate=True)

def _silu(x):
    return jax.nn.silu(x)

def _sigmoid(x):
    return jax.nn.sigmoid(x)

def _layernorm(x, axis=-1, eps=1e-05):
    m = jnp.mean(x, axis=axis, keepdims=True)
    v = jnp.var(x, axis=axis, keepdims=True)
    return (x - m) / jnp.sqrt(v + eps)

def _scatter_add(tgt, idx, src, axis=0):
    return tgt.at[idx].add(src)

def _segment_sum(src, seg, n):
    return jax.ops.segment_sum(src, seg, n)
kernel_name = 'mk_perceiver_d2_seqx_r4_647717'

def setup_inputs(seed: int=0):
    np.random.seed(seed)
    _w = jnp.asarray

    def _rec_inputs():
        import jax
        import jax.numpy as jnp
        _rk = jax.random.key(seed)
        x = 7.22e-05 + 1 * jax.random.normal(jax.random.fold_in(_rk, 1), (1, 256, 256), jnp.float32)
        _lenS = 256 - jax.random.randint(jax.random.fold_in(_rk, 7), (1,), 0, max(1, 256 // 4) + 1, jnp.int32)
        _lenS2 = 4096 - jax.random.randint(jax.random.fold_in(_rk, 8), (1,), 0, max(1, 4096 // 4) + 1, jnp.int32)
        _ctx_1024P = jax.random.normal(jax.random.fold_in(_rk, 11), (1, 16, 256), jnp.float32)
        _ctx_1024c = jax.random.dirichlet(jax.random.fold_in(_rk, 511), 0.3 * jnp.ones((16,), jnp.float32), (1, 4096))
        _ctx_1024t = jnp.einsum('bsk,bkd->bsd', _ctx_1024c, _ctx_1024P)
        _ctx_1024t = _ctx_1024t * jax.lax.rsqrt(jnp.mean(jnp.square(_ctx_1024t)) + 1e-12) * 0.953939
        ctx_1024 = 4.13588e-05 + 0.999923 * (_ctx_1024t + 0.3 * jax.random.normal(jax.random.fold_in(_rk, 611), (1, 4096, 256), jnp.float32))
        _validS = jnp.arange(256)[None, :] < _lenS[:, None]
        _validS2 = jnp.arange(4096)[None, :] < _lenS2[:, None]
        _causal = jnp.tril(jnp.ones((256, 256), dtype=bool))
        mask_Bx1xS2_bk0 = jnp.logical_not(jnp.broadcast_to(_validS2[:, None, :], (1, 1, 4096)))
        mask_Bx1xSxS2_bf1 = jnp.ones((1, 1, 256, 4096), dtype=bool)
        return (x, ctx_1024, mask_Bx1xS2_bk0, mask_Bx1xSxS2_bf1)
    x, ctx_1024, mask_Bx1xS2_bk0, mask_Bx1xSxS2_bf1 = _rec_inputs()

    def _L0_xattn_setup():
        import jax, jax.numpy as jnp
        import numpy as np
        B, S, E, H = (4, 512, 256, 16)
        DH = E // H

        def _make_heads(v, n_heads):
            b, n, e = v.shape
            return jnp.moveaxis(v.reshape(b, n, n_heads, e // n_heads), -2, 0)
        key = jax.random.key(seed)
        k1, k2, k3, k4, k5 = jax.random.split(key, 5)
        return {'query': jax.random.normal(k1, (B, S, E), dtype=jnp.float32), 'key': jax.random.normal(k2, (B, S, E), dtype=jnp.float32), 'value': jax.random.normal(k3, (B, S, E), dtype=jnp.float32), 'mask': jax.random.randint(k4, (B, 1, S), 0, 2).astype(bool), 'W_out': jax.random.normal(k5, (E, E), dtype=jnp.float32) / np.sqrt(E), 'scale': jnp.asarray(1.0, dtype=jnp.float32), 'log_C': jnp.asarray(np.log(10.0), dtype=jnp.float32)}
    _L0_xattn_all = _L0_xattn_setup()
    _L0_xattn_in = {k: v for k, v in _L0_xattn_all.items() if k in ('W_out', 'scale', 'log_C')}
    del _L0_xattn_all

    def _L0_attn_setup():
        import jax, jax.numpy as jnp
        import numpy as np
        EPS = 1e-06
        NUM_HEADS = 16

        def rms_norm(x, w):
            var = jnp.mean(jnp.square(x), axis=-1, keepdims=True)
            return x * jax.lax.rsqrt(var + EPS) * w
        key = jax.random.key(seed)
        ks = jax.random.split(key, 6)
        B, N, C = (8, 256, 256)
        return {'x': jax.random.normal(ks[0], (B, N, C), dtype=jnp.float32), 'w_qkv': jax.random.normal(ks[1], (3 * C, C), dtype=jnp.float32) * (1.0 / np.sqrt(C)), 'b_qkv': jax.random.normal(ks[2], (3 * C,), dtype=jnp.float32) * 0.02, 'qn_w': jnp.ones((C // NUM_HEADS,), dtype=jnp.float32), 'kn_w': jnp.ones((C // NUM_HEADS,), dtype=jnp.float32), 'w_proj': jax.random.normal(ks[3], (C, C), dtype=jnp.float32) * (1.0 / np.sqrt(C)), 'b_proj': jax.random.normal(ks[4], (C,), dtype=jnp.float32) * 0.02}
    _L0_attn_all = _L0_attn_setup()
    _L0_attn_in = {k: v for k, v in _L0_attn_all.items() if k in ('w_qkv', 'b_qkv', 'qn_w', 'kn_w', 'w_proj', 'b_proj')}
    del _L0_attn_all

    def _L0_ffn_setup():
        import jax, jax.numpy as jnp
        import numpy as np
        EPS = 1e-08
        key = jax.random.key(seed)
        kx, kw = jax.random.split(key)
        x = jax.random.normal(kx, (8, 1024, 256), dtype=jnp.float32)
        weight = jax.random.normal(kw, (256, 256), dtype=jnp.float32) * (1.0 / np.sqrt(256))
        return {'x': x, 'weight': weight}
    _L0_ffn_all = _L0_ffn_setup()
    _L0_ffn_in = {k: v for k, v in _L0_ffn_all.items() if k in ('weight',)}
    del _L0_ffn_all

    def _L1_xattn_setup():
        import jax, jax.numpy as jnp
        import numpy as np
        B, S, D, H = (4, 512, 256, 16)
        DK = D // H

        def _split_heads(x):
            b, s, _ = x.shape
            return x.reshape(b, s, H, DK).transpose(0, 2, 1, 3)
        key = jax.random.key(seed)
        ks = jax.random.split(key, 12)
        s = 0.02
        return {'query': jax.random.normal(ks[0], (B, S, D), jnp.float32), 'key': jax.random.normal(ks[1], (B, S, D), jnp.float32), 'value': jax.random.normal(ks[2], (B, S, D), jnp.float32), 'mask': jnp.ones((B, 1, S, S), dtype=bool), 'Wq': jax.random.normal(ks[3], (D, D), jnp.float32) * s, 'bq': jnp.zeros((D,), jnp.float32), 'Wk': jax.random.normal(ks[4], (D, D), jnp.float32) * s, 'bk': jnp.zeros((D,), jnp.float32), 'Wv': jax.random.normal(ks[5], (D, D), jnp.float32) * s, 'bv': jnp.zeros((D,), jnp.float32), 'Wo': jax.random.normal(ks[6], (D, D), jnp.float32) * s, 'bo': jnp.zeros((D,), jnp.float32)}
    _L1_xattn_all = _L1_xattn_setup()
    _L1_xattn_in = {k: v for k, v in _L1_xattn_all.items() if k in ('Wq', 'bq', 'Wk', 'bk', 'Wv', 'bv', 'Wo', 'bo')}
    del _L1_xattn_all

    def _L1_attn_setup():
        import jax, jax.numpy as jnp
        import numpy as np
        B, S, E, H, Dh = (2, 512, 256, 16, 64)
        key = jax.random.key(seed)
        ks = jax.random.split(key, 8)
        w = 0.02
        return {'x': jax.random.normal(ks[0], (B, S, E), jnp.float32), 'Wq': jax.random.normal(ks[1], (H, Dh, E), jnp.float32) * w, 'bq': jax.random.normal(ks[2], (H, Dh), jnp.float32) * w, 'Wk': jax.random.normal(ks[3], (H, Dh, E), jnp.float32) * w, 'bk': jax.random.normal(ks[4], (H, Dh), jnp.float32) * w, 'Wv': jax.random.normal(ks[5], (H, Dh, E), jnp.float32) * w, 'bv': jax.random.normal(ks[6], (H, Dh), jnp.float32) * w, 'proj': jax.random.normal(ks[7], (H * Dh, E), jnp.float32) * w}
    _L1_attn_all = _L1_attn_setup()
    _L1_attn_in = {k: v for k, v in _L1_attn_all.items() if k in ('Wq', 'bq', 'Wk', 'bk', 'Wv', 'bv', 'proj')}
    del _L1_attn_all

    def _L1_ffn_setup():
        import jax, jax.numpy as jnp
        import numpy as np
        D_MODEL = 256
        NUM_HEADS = 4
        NUM_EXPERTS = 8
        TOP_K = 2
        D_FF = 256
        EPS = 1e-06

        def _rmsnorm(x, g):
            return x * jax.lax.rsqrt(jnp.mean(x * x, axis=-1, keepdims=True) + EPS) * g

        def _swiglu(x, w1, w2, w3):
            return jax.nn.silu(x @ w1.T) * (x @ w3.T) @ w2.T
        key = jax.random.key(seed)
        ks = jax.random.split(key, 16)
        d, e, f = (D_MODEL, NUM_EXPERTS, D_FF)
        dc = d // 4
        s = 0.02
        return {'X': jax.random.normal(ks[0], (2, 256, d), dtype=jnp.float32), 'g1': jnp.ones((d,), jnp.float32), 'g2': jnp.ones((d,), jnp.float32), 'Wq': jax.random.normal(ks[1], (d, d), jnp.float32) * s, 'Wkc': jax.random.normal(ks[2], (dc, d), jnp.float32) * s, 'Wvc': jax.random.normal(ks[3], (dc, d), jnp.float32) * s, 'Wo': jax.random.normal(ks[4], (d, d), jnp.float32) * s, 'Wr': jax.random.normal(ks[5], (e, d), jnp.float32) * s, 'expert_bias': jnp.zeros((e,), jnp.float32), 'sW1': jax.random.normal(ks[6], (f, d), jnp.float32) * s, 'sW2': jax.random.normal(ks[7], (d, f), jnp.float32) * s, 'sW3': jax.random.normal(ks[8], (f, d), jnp.float32) * s, 'eW1': jax.random.normal(ks[9], (e, f, d), jnp.float32) * s, 'eW2': jax.random.normal(ks[10], (e, d, f), jnp.float32) * s, 'eW3': jax.random.normal(ks[11], (e, f, d), jnp.float32) * s}
    _L1_ffn_all = _L1_ffn_setup()
    _L1_ffn_in = {k: v for k, v in _L1_ffn_all.items() if k in ('g1', 'g2', 'Wq', 'Wkc', 'Wvc', 'Wo', 'Wr', 'expert_bias', 'sW1', 'sW2', 'sW3', 'eW1', 'eW2', 'eW3')}
    del _L1_ffn_all
    return {'x': x, 'ctx_1024': ctx_1024, 'mask_Bx1xS2_bk0': mask_Bx1xS2_bk0, 'mask_Bx1xSxS2_bf1': mask_Bx1xSxS2_bf1, 'L0_xattn_W_out': _L0_xattn_in['W_out'], 'L0_xattn_scale': _L0_xattn_in['scale'], 'L0_xattn_log_C': _L0_xattn_in['log_C'], 'L0_attn_w_qkv': _L0_attn_in['w_qkv'], 'L0_attn_b_qkv': _L0_attn_in['b_qkv'], 'L0_attn_qn_w': _L0_attn_in['qn_w'], 'L0_attn_kn_w': _L0_attn_in['kn_w'], 'L0_attn_w_proj': _L0_attn_in['w_proj'], 'L0_attn_b_proj': _L0_attn_in['b_proj'], 'L0_ffn_weight': _L0_ffn_in['weight'], 'L1_xattn_Wq': _L1_xattn_in['Wq'], 'L1_xattn_bq': _L1_xattn_in['bq'], 'L1_xattn_Wk': _L1_xattn_in['Wk'], 'L1_xattn_bk': _L1_xattn_in['bk'], 'L1_xattn_Wv': _L1_xattn_in['Wv'], 'L1_xattn_bv': _L1_xattn_in['bv'], 'L1_xattn_Wo': _L1_xattn_in['Wo'], 'L1_xattn_bo': _L1_xattn_in['bo'], 'L1_attn_Wq': _L1_attn_in['Wq'], 'L1_attn_bq': _L1_attn_in['bq'], 'L1_attn_Wk': _L1_attn_in['Wk'], 'L1_attn_bk': _L1_attn_in['bk'], 'L1_attn_Wv': _L1_attn_in['Wv'], 'L1_attn_bv': _L1_attn_in['bv'], 'L1_attn_proj': _L1_attn_in['proj'], 'L1_ffn_g1': _L1_ffn_in['g1'], 'L1_ffn_g2': _L1_ffn_in['g2'], 'L1_ffn_Wq': _L1_ffn_in['Wq'], 'L1_ffn_Wkc': _L1_ffn_in['Wkc'], 'L1_ffn_Wvc': _L1_ffn_in['Wvc'], 'L1_ffn_Wo': _L1_ffn_in['Wo'], 'L1_ffn_Wr': _L1_ffn_in['Wr'], 'L1_ffn_expert_bias': _L1_ffn_in['expert_bias'], 'L1_ffn_sW1': _L1_ffn_in['sW1'], 'L1_ffn_sW2': _L1_ffn_in['sW2'], 'L1_ffn_sW3': _L1_ffn_in['sW3'], 'L1_ffn_eW1': _L1_ffn_in['eW1'], 'L1_ffn_eW2': _L1_ffn_in['eW2'], 'L1_ffn_eW3': _L1_ffn_in['eW3']}

def reference(x, ctx_1024, mask_Bx1xS2_bk0, mask_Bx1xSxS2_bf1, L0_xattn_W_out, L0_xattn_scale, L0_xattn_log_C, L0_attn_w_qkv, L0_attn_b_qkv, L0_attn_qn_w, L0_attn_kn_w, L0_attn_w_proj, L0_attn_b_proj, L0_ffn_weight, L1_xattn_Wq, L1_xattn_bq, L1_xattn_Wk, L1_xattn_bk, L1_xattn_Wv, L1_xattn_bv, L1_xattn_Wo, L1_xattn_bo, L1_attn_Wq, L1_attn_bq, L1_attn_Wk, L1_attn_bk, L1_attn_Wv, L1_attn_bv, L1_attn_proj, L1_ffn_g1, L1_ffn_g2, L1_ffn_Wq, L1_ffn_Wkc, L1_ffn_Wvc, L1_ffn_Wo, L1_ffn_Wr, L1_ffn_expert_bias, L1_ffn_sW1, L1_ffn_sW2, L1_ffn_sW3, L1_ffn_eW1, L1_ffn_eW2, L1_ffn_eW3):
    import jax
    import jax.numpy as jnp

    def _L0_xattn_ref(query, key, value, mask, W_out, scale, log_C):
        import jax, jax.numpy as jnp
        import numpy as np
        B, S, E, H = (4, 512, 256, 16)
        DH = E // H

        def _make_heads(v, n_heads):
            b, n, e = v.shape
            return jnp.moveaxis(v.reshape(b, n, n_heads, e // n_heads), -2, 0)
        q = _make_heads(query, H)
        k = _make_heads(key, H)
        v = _make_heads(value, H)
        d_k = q.shape[-1]
        u = jnp.einsum('hbqd,hbkd->hbqk', q, k) * scale / np.sqrt(d_k)
        logits = jnp.tanh(u) * jnp.exp(log_C)
        logits = jnp.where(mask, -jnp.inf, logits)
        attn = jax.nn.softmax(logits, axis=-1)
        out_heads = jnp.einsum('hbqk,hbkd->hbqd', attn, v)
        out = jnp.moveaxis(out_heads, 0, -2).reshape(query.shape)
        return out @ W_out.T

    def _L0_attn_ref(x, w_qkv, b_qkv, qn_w, kn_w, w_proj, b_proj):
        import jax, jax.numpy as jnp
        import numpy as np
        EPS = 1e-06
        NUM_HEADS = 16

        def rms_norm(x, w):
            var = jnp.mean(jnp.square(x), axis=-1, keepdims=True)
            return x * jax.lax.rsqrt(var + EPS) * w
        B, N, C = x.shape
        H = NUM_HEADS
        D = C // H
        qkv = x @ w_qkv.T + b_qkv
        qkv = qkv.reshape(B, N, 3, H, D).transpose(2, 0, 3, 1, 4)
        q, k, v = (qkv[0], qkv[1], qkv[2])
        q = rms_norm(q, qn_w)
        k = rms_norm(k, kn_w)
        scale = 1.0 / np.sqrt(D).astype(np.float32)
        attn = jnp.einsum('bhld,bhsd->bhls', q, k) * scale
        attn = jax.nn.softmax(attn, axis=-1)
        out = jnp.einsum('bhls,bhsd->bhld', attn, v)
        out = out.transpose(0, 2, 1, 3).reshape(B, N, C)
        return out @ w_proj.T + b_proj

    def _L0_ffn_ref(x, weight):
        import jax, jax.numpy as jnp
        import numpy as np
        EPS = 1e-08
        w_scale = jnp.mean(jnp.abs(weight)) + EPS
        u = weight / w_scale
        w_quant = u + jax.lax.stop_gradient(jnp.clip(jnp.round(u), -1.0, 1.0) - u)
        a_scale = jnp.max(jnp.abs(x), axis=-1, keepdims=True) + EPS
        z = jnp.clip(x / a_scale * 127.0, -128.0, 127.0)
        a_quant = z + jax.lax.stop_gradient(jnp.round(z) - z)
        y = jnp.einsum('bsi,oi->bso', a_quant, w_quant)
        y = y * (w_scale * a_scale / 127.0)
        return y

    def _L1_xattn_ref(query, key, value, mask, Wq, bq, Wk, bk, Wv, bv, Wo, bo):
        import jax, jax.numpy as jnp
        import numpy as np
        B, S, D, H = (4, 512, 256, 16)
        DK = D // H

        def _split_heads(x):
            b, s, _ = x.shape
            return x.reshape(b, s, H, DK).transpose(0, 2, 1, 3)
        q = _split_heads(query @ Wq.T + bq)
        k = _split_heads(key @ Wk.T + bk)
        v = _split_heads(value @ Wv.T + bv)
        scores = jnp.einsum('bhqd,bhkd->bhqk', q, k) / jnp.sqrt(jnp.float32(DK))
        scores = jnp.where(mask, scores, jnp.float32(-1000000000.0))
        p = jax.nn.softmax(scores, axis=-1)
        out = jnp.einsum('bhqk,bhkd->bhqd', p, v)
        out = out.transpose(0, 2, 1, 3).reshape(query.shape[0], -1, D)
        return out @ Wo.T + bo

    def _L1_attn_ref(x, Wq, bq, Wk, bk, Wv, bv, proj):
        import jax, jax.numpy as jnp
        import numpy as np
        B, S, E, H, Dh = (2, 512, 256, 16, 64)
        b, s, e = x.shape
        h, dh, _ = Wq.shape
        scale = jnp.sqrt(jnp.asarray(dh, x.dtype))
        q = jnp.einsum('bse,hde->bhsd', x, Wq) + bq[None, :, None, :]
        k = jnp.einsum('bse,hde->bhsd', x, Wk) + bk[None, :, None, :]
        v = jnp.einsum('bse,hde->bhsd', x, Wv) + bv[None, :, None, :]
        causal = jnp.triu(jnp.ones((s, s), bool), 1)
        scores = jnp.einsum('bhsd,bhtd->bhst', q, k) / scale
        scores = jnp.where(causal[None, None], -jnp.inf, scores)
        att = jax.nn.softmax(scores, axis=-1) / scale
        z = jnp.einsum('bhst,bhtd->bhsd', att, v)
        z = z.reshape(b, s, h * dh)
        return z @ proj

    def _L1_ffn_ref(X, g1, g2, Wq, Wkc, Wvc, Wo, Wr, expert_bias, sW1, sW2, sW3, eW1, eW2, eW3):
        import jax, jax.numpy as jnp
        import numpy as np
        D_MODEL = 256
        NUM_HEADS = 4
        NUM_EXPERTS = 8
        TOP_K = 2
        D_FF = 256
        EPS = 1e-06

        def _rmsnorm(x, g):
            return x * jax.lax.rsqrt(jnp.mean(x * x, axis=-1, keepdims=True) + EPS) * g

        def _swiglu(x, w1, w2, w3):
            return jax.nn.silu(x @ w1.T) * (x @ w3.T) @ w2.T
        B, S, d = X.shape
        H = NUM_HEADS
        dk = d // H
        scale = 1.0 / jnp.sqrt(jnp.float32(dk))
        nx = _rmsnorm(X, g1)
        Q = (nx @ Wq.T).reshape(B, S, H, dk).transpose(0, 2, 1, 3)
        Kc = nx @ Wkc.T
        Vc = nx @ Wvc.T
        scores = jnp.einsum('bhsd,btd->bhst', Q, Kc) * scale
        attn = jax.nn.softmax(scores, axis=-1)
        out = jnp.einsum('bhst,btd->bhsd', attn, Vc)
        out = out.transpose(0, 2, 1, 3).reshape(B, S, d) @ Wo.T
        X = X + out
        nx = _rmsnorm(X, g2)
        xf = nx.reshape(-1, d)
        logits = xf @ Wr.T + expert_bias
        rw = jax.nn.softmax(logits, axis=-1)
        topw, topi = jax.lax.top_k(rw, TOP_K)
        topw = jax.nn.softmax(topw, axis=-1)
        combine = jnp.sum(jax.nn.one_hot(topi, NUM_EXPERTS, dtype=xf.dtype) * topw[..., None], axis=1)
        shared = _swiglu(xf, sW1, sW2, sW3)
        h = jax.nn.silu(jnp.einsum('td,efd->etf', xf, eW1)) * jnp.einsum('td,efd->etf', xf, eW3)
        eo = jnp.einsum('etf,edf->etd', h, eW2)
        specialist = jnp.einsum('te,etd->td', combine, eo)
        moe_out = (shared + specialist).reshape(B, S, d)
        return X + moe_out
    x = x + _L0_xattn_ref(_layernorm(x, axis=-1), ctx_1024, ctx_1024, mask_Bx1xS2_bk0, L0_xattn_W_out, L0_xattn_scale, L0_xattn_log_C)
    x = x + _L0_attn_ref(_layernorm(x, axis=-1), L0_attn_w_qkv, L0_attn_b_qkv, L0_attn_qn_w, L0_attn_kn_w, L0_attn_w_proj, L0_attn_b_proj)
    x = x + _L0_ffn_ref(_layernorm(x, axis=-1), L0_ffn_weight)
    x = x + _L1_xattn_ref(_layernorm(x, axis=-1), ctx_1024, ctx_1024, mask_Bx1xSxS2_bf1, L1_xattn_Wq, L1_xattn_bq, L1_xattn_Wk, L1_xattn_bk, L1_xattn_Wv, L1_xattn_bv, L1_xattn_Wo, L1_xattn_bo)
    x = x + _L1_attn_ref(_layernorm(x, axis=-1), L1_attn_Wq, L1_attn_bq, L1_attn_Wk, L1_attn_bk, L1_attn_Wv, L1_attn_bv, L1_attn_proj)
    x = x + _L1_ffn_ref(_layernorm(x, axis=-1), L1_ffn_g1, L1_ffn_g2, L1_ffn_Wq, L1_ffn_Wkc, L1_ffn_Wvc, L1_ffn_Wo, L1_ffn_Wr, L1_ffn_expert_bias, L1_ffn_sW1, L1_ffn_sW2, L1_ffn_sW3, L1_ffn_eW1, L1_ffn_eW2, L1_ffn_eW3)
    return x

_drawn_inputs = setup_inputs


def setup_inputs(seed=0):
    import zlib

    import numpy as np

    out = dict(_drawn_inputs(seed))
    spreads = {'L0_attn_qn_w': (1.0, 0.6),
     'L0_attn_kn_w': (1.0, 0.6),
     'L1_xattn_bq': (0.0, 0.8),
     'L1_xattn_bk': (0.0, 0.8),
     'L1_xattn_bv': (0.0, 0.408),
     'L1_xattn_bo': (0.0, 0.1),
     'L1_ffn_g1': (1.0, 0.6),
     'L1_ffn_g2': (1.0, 0.6),
     'L1_ffn_expert_bias': (0.0, 0.8)}
    factors = {'L0_attn_b_qkv': 3.538,
     'L0_attn_b_proj': 3.961,
     'L1_xattn_Wq': 8.0,
     'L1_xattn_Wk': 8.0,
     'L1_attn_Wq': 8.0,
     'L1_attn_bq': 8.0,
     'L1_attn_Wk': 8.0,
     'L1_attn_bk': 8.0,
     'L1_attn_Wv': 6.946,
     'L1_attn_bv': 8.0,
     'L1_attn_proj': 6.92,
     'L1_ffn_Wq': 8.0,
     'L1_ffn_Wkc': 8.0,
     'L1_ffn_Wvc': 2.728,
     'L1_ffn_Wo': 2.689,
     'L1_ffn_Wr': 8.0,
     'L1_ffn_sW1': 8.0,
     'L1_ffn_sW2': 8.0,
     'L1_ffn_sW3': 7.958,
     'L1_ffn_eW1': 8.0,
     'L1_ffn_eW2': 8.0,
     'L1_ffn_eW3': 8.0}
    for name, (base, spread) in spreads.items():
        noise = np.random.default_rng([zlib.crc32(name.encode()), seed]).standard_normal(out[name].shape)
        drawn = base * np.exp(spread * noise) if base else spread * noise
        out[name] = jnp.asarray(drawn.astype(out[name].dtype))
    for name, factor in factors.items():
        out[name] = (out[name] * factor).astype(out[name].dtype)
    return out
```

```python
from contextlib import ExitStack

import numpy as np

import concourse.bass as bass
from concourse import mybir

F32 = mybir.dt.float32
BF16 = mybir.dt.bfloat16
I32 = mybir.dt.int32
U8 = mybir.dt.uint8
ALU = mybir.AluOpType
ACT = mybir.ActivationFunctionType
AX = mybir.AxisListType

P = 128
S = 256
D = 256
S2 = 4096
H = 16
DH = D // H
QT = S // P
KT = D // P
NCH = S2 // P
UNIT_CH = NCH // 2
UNIT_KEYS = UNIT_CH * P
GROUP_CH = 4
GROUPS = UNIT_CH // GROUP_CH
PARTS = 3
MAXROW = 96
LOROW = MAXROW + PARTS
STACK = LOROW + DH
KSPLIT = 1024
CBLK = 512
E_T = 8
E_DH = 64
N_EXP = 8
F_H = 4
ROUND = 12582912.0
RSQRT_MAGIC = float(0x5F3759DF)


class Kern:

    def __init__(self, nc, ctx, ins, out):
        self.nc, self.ctx, self.i, self.out = nc, ctx, ins, out
        self.sems = {}
        self.dve_ordered = [0]
        self.small_pairs = 0
        self.pool_ordered = [0]

    def sb(self, name, shape, dt=F32):
        t = self.ctx.enter_context(self.nc.sbuf_tensor("sb_" + name, shape, dt))
        return t

    def sem(self, name):
        if name not in self.sems:
            self.sems[name] = self.ctx.enter_context(self.nc.semaphore(name))
        return self.sems[name]


class Order:

    def __init__(self, eng, sem, count):
        self.eng, self.sem, self.count = eng, sem, count

    def link(self, ins):
        self.count[0] += 1
        ins.then_inc(self.sem, 1)
        self.eng.wait_ge(self.sem, self.count[0])
        return self.count[0]


def allocate(k):
    nc = k.nc
    k.kd0 = nc.dram_tensor("k_parts_l0", [H, PARTS * DH, S2], BF16, kind="Internal").ap()
    k.kd1 = nc.dram_tensor("k_parts_l1", [H, PARTS * DH, S2], BF16, kind="Internal").ap()
    k.qd = nc.dram_tensor("q_parts", [2, H, PARTS * DH, S], BF16, kind="Internal").ap()

    k.ps = k.ctx.enter_context(nc.psum_tensor("ps", [P, 8, 512], F32))

    k.x = k.sb("x", [P, QT, D])
    k.ident = k.sb("ident", [P, P])
    k.ident_bf = k.sb("ident_bf", [P, P], BF16)
    k.quad_sum = k.sb("quad_sum", [P, 32])
    k.ones_row = k.sb("ones_row", [1, CBLK])
    k.ln_stats = k.sb("ln_stats", [P, QT, 6])
    k.ln_mv = k.sb("ln_mv", [P, QT, 2])
    k.rs_v = k.sb("rs_v", [P, 64])
    k.rs_y = k.sb("rs_y", [P, 64])
    k.rs_t = k.sb("rs_t", [P, 64])
    k.xn = k.sb("xn", [P, QT, D])
    k.xnT = k.sb("xnT", [P, KT, S])
    k.o_nat = k.sb("o_nat", [P, QT, D])
    k.oT = k.sb("oT", [P, KT, S])
    k.q_f = k.sb("q_f", [P, KT, S])
    k.q_r = k.sb("q_r", [P, KT, S])
    k.q_p = k.sb("q_p", [P, PARTS, KT, S], BF16)
    k.q_all = k.sb("q_all", [P, H, S], BF16)
    k.q_st = k.sb("q_st", [P, 2, S], BF16)
    k.k_st = k.sb("k_st", [P, 4, UNIT_KEYS], BF16)
    k.v_st = k.sb("v_st", [P, 2, NCH, 32])
    k.v_rows = k.sb("v_rows", [P, NCH, D])
    k.v_proj = k.sb("v_proj", [P, NCH, D])
    k.probs = k.sb("probs", [P, 2, UNIT_KEYS // P, S])
    k.acc_sb = k.sb("acc_sb", [P, 2, S])
    k.rec = k.sb("rec", [P, 2, QT])
    k.keep = k.sb("keep", [P, NCH])
    k.keep_u8 = k.sb("keep_u8", [P, NCH], U8)
    k.l0_scale = k.sb("l0_scale", [P, 1])
    k.l0_logc = k.sb("l0_logc", [P, 1])
    k.cap = k.sb("cap", [P, 1])
    k.neg_cap = k.sb("neg_cap", [P, 1])
    k.bkv1 = k.sb("bkv1", [1, 2, D])
    k.w1_q = k.sb("w1_q", [P, KT, D])
    k.w1_o = k.sb("w1_o", [P, KT, D])
    k.b1_qo = k.sb("b1_qo", [1, 2, D])
    k.any_keep = k.sb("any_keep", [P, QT])
    k.mask_sum = k.sb("mask_sum", [P, QT])
    k.masked_f = k.sb("masked_f", [P, 1])
    k.masked_i = k.sb("masked_i", [1, 1], I32)
    k.m_blk = k.sb("m_blk", [P, QT, S2 // 512])
    k.m_neg = k.sb("m_neg", [P, QT])
    k.m_res = k.sb("m_res", [P, 2, QT])
    k.m_parts = k.sb("m_parts", [P, QT, PARTS], BF16)
    k.q_m = k.sb("q_m", [P, 2, S], BF16)
    vf = k.v_rows[:, :, :].rearrange("p c d -> p (c d)")
    k.mask_bias = vf[:, 0:4096].bitcast(BF16).rearrange("p (t n) -> p t n", t=QT)
    k.mask_u8 = vf[:, 4096:6144].bitcast(U8).rearrange("p (t n) -> p t n", t=QT)
    k.early = k.sb("early", [P, 8192])
    k.bias_rows = k.sb("bias_rows", [1, 4 * D])
    at = [0]

    def carve(n):
        at[0] += n
        return k.early[:, at[0] - n:at[0]]

    k.w_out0, k.wk1, k.wv1, k.w_ffn0 = [carve(KT * D).rearrange("p (t n) -> p t n", t=KT) for _ in range(4)]
    k.w_qkv0 = carve(KT * 3 * D).rearrange("p (t n) -> p t n", t=KT)
    k.w_proj0 = carve(H // 4 * D).rearrange("p (t n) -> p t n", t=H // 4)
    k.ctx_blk = carve(KT * CBLK).rearrange("p (t n) -> p t n", t=KT)
    k.kd_r = carve(2 * CBLK).rearrange("p (t n) -> p t n", t=2)
    k.kd_bf = carve(PARTS * CBLK).bitcast(BF16).rearrange("p (b s n) -> p b s n", b=2, s=PARTS)
    k.b_qkv0, k.b_proj0 = k.bias_rows[:, 0:3 * D], k.bias_rows[:, 3 * D:4 * D]
    k.e_w = k.early[:, 0:6144].rearrange("p (s t n) -> p s t n", s=3, t=KT)
    k.e_proj = k.early[:, 6144:8192].rearrange("p (t n) -> p t n", t=E_T)
    k.e_bv = k.bias_rows[:, :]
    k.e_bqk = k.sb("e_bqk", [P, 2, E_T])
    k.causal = k.sb("causal", [P, P], BF16)
    k.f_comb = k.sb("f_comb", [P, QT, N_EXP + 1])
    k.f_lg = k.sb("f_lg", [P, QT, N_EXP])
    k.f_rw = k.sb("f_rw", [P, QT, N_EXP])
    k.f_gt = k.sb("f_gt", [P, QT, N_EXP, N_EXP])
    k.f_eq = k.sb("f_eq", [P, QT, N_EXP, N_EXP])
    k.f_low = k.sb("f_low", [P, N_EXP, N_EXP])
    k.f_rank = k.sb("f_rank", [P, QT, N_EXP])
    k.f_sel = k.sb("f_sel", [P, 2, QT, N_EXP])
    k.f_pick = k.sb("f_pick", [P, 2, QT, N_EXP])
    k.f_p = k.sb("f_p", [P, 2, QT])
    k.f_w = k.sb("f_w", [P, 4, QT])
    k.head_mask = k.sb("head_mask", [P, P // DH])
    k.ones_sq = k.sb("ones_sq", [P, P])
    k.w_qkn = k.sb("w_qkn", [P, 2, DH])
    k.nmax = k.sb("nmax", [P, 2 * H])
    k.sums = k.sb("sums", [P, 2 * H])
    k.inv = k.sb("inv", [P, 2 * H])
    k.w_tern = k.sb("w_tern", [P, KT, D], BF16)
    k.w_sum = k.sb("w_sum", [P, 1])
    k.w_scale = k.sb("w_scale", [P, 1])
    k.w_inv = k.sb("w_inv", [P, 1])
    k.a_scale = k.sb("a_scale", [P, QT])
    k.a_inv = k.sb("a_inv", [P, QT])
    k.a_q = k.sb("a_q", [P, QT, D], BF16)
    k.a_qT = k.sb("a_qT", [P, KT, S], BF16)
    flat = lambda t, dims: t.rearrange(f"p {dims} -> p ({dims})")
    pf = flat(k.probs[:, :, :, :], "b c q")
    k.q_mask = pf[:, 0:H * S].rearrange("p (h q) -> p h q", q=S)
    k.qk = pf[:, 4096:5120].rearrange("p (t n) -> p t n", t=QT)
    k.qk_sq = pf[:, 5120:6144].rearrange("p (t n) -> p t n", t=QT)
    k.kT_self = pf[:, 6144:6656].rearrange("p (t n) -> p t n", t=KT)
    k.v_self = pf[:, 6656:7680].rearrange("p (t h n) -> p t h n", t=KT, h=H)
    qa = flat(k.q_all[:, :, :], "h q").bitcast(F32)
    k.sp_rows = qa[:, 0:1024].rearrange("p (b e n) -> p b e n", b=2, e=2)
    k.sp_T = qa[:, 1024:2048].rearrange("p (b n) -> p b n", b=2)
    k.e_qT = pf[:, 0:2048].rearrange("p (t q) -> p t q", t=E_T)
    k.e_kT = pf[:, 2048:4096].rearrange("p (t q) -> p t q", t=E_T)
    k.e_v = pf[:, 4096:6144].rearrange("p (t n) -> p t n", t=KT)
    k.e_oT = pf[:, 6144:8192].rearrange("p (h i c) -> p h i c", h=2 * E_T, c=E_T)
    k.x_ffn = k.o_nat
    k.f_qT = pf[:, 0:512].rearrange("p (t q) -> p t q", t=KT)
    k.f_kT = pf[:, 512:768]
    k.f_v = pf[:, 768:896].rearrange("p (t n) -> p t n", t=KT)
    k.f_tanh = pf[:, 1024:2048].rearrange("p (b n) -> p b n", b=2)
    k.f_gate = pf[:, 2048:3072].rearrange("p (b n) -> p b n", b=2)
    k.f_hT = pf[:, 3072:4096].rearrange("p (b t q) -> p b t q", b=2, t=KT)
    fs = vf[:, 6144:8192]
    k.f_wq = fs[:, 0:512].rearrange("p (t n) -> p t n", t=KT)
    k.f_wo = fs[:, 512:1024].rearrange("p (t n) -> p t n", t=KT)
    k.f_wkc = fs[:, 1024:1280].rearrange("p (t n) -> p t n", t=KT)
    k.f_wvc = fs[:, 1280:1408].rearrange("p (t n) -> p t n", t=KT)
    k.f_wr = fs[:, 1408:1424].rearrange("p (t n) -> p t n", t=KT)
    k.f_g = fs[:, 1424:1428].rearrange("p (s t) -> p s t", s=2)
    k.f_be = fs[0:1, 1428:1436]
    vp = k.v_proj[:, :, :].rearrange("p c d -> p (c d)")
    place = [vp[:, n * 512:(n + 1) * 512] for n in range(16)] + [vf[:, n * 512:(n + 1) * 512] for n in range(11)]
    k.f_exp = [[place[3 * e + w].rearrange("p (t n) -> p t n", t=KT) for w in range(3)] for e in range(N_EXP + 1)]
    k.oT_pad = flat(k.v_st[:, :, :, :], "b c n")[:, 0:1024].rearrange("p (g q) -> p g q", g=4)


def layer_norm(k, dve, link, src, dst, done):
    v = k.nc.vector
    for t in range(QT):
        link(v.bn_stats(k.ln_stats[:, t, :], src[:, t, :]))
        link(v.bn_aggr(k.ln_mv[:, t, :], k.ln_stats[:, t, :]))
    link(v.tensor_scalar(k.rs_v[:, 0:QT], k.ln_mv[:, :, 1], 1e-5, None, ALU.add))
    rsqrt(k, link, QT)
    for t in range(QT):
        v.tensor_scalar(dst[:, t, :], src[:, t, :], k.ln_mv[:, t, 0:1], k.rs_y[:, t:t + 1],
                        ALU.subtract, ALU.mult).then_inc(done, 1)


def rsqrt(k, link, n):
    v, y, t = k.rs_v[:, 0:n], k.rs_y[:, 0:n], k.rs_t[:, 0:n]
    vec = k.nc.vector
    link(vec.tensor_scalar(y.bitcast(I32), v.bitcast(I32), -0.5, RSQRT_MAGIC, ALU.mult, ALU.add))
    for _ in range(3):
        link(vec.tensor_tensor(t, y, y, ALU.mult))
        link(vec.scalar_tensor_tensor(out=t, in0=t, scalar=-0.5, in1=v, op0=ALU.mult, op1=ALU.mult))
        link(vec.scalar_tensor_tensor(out=y, in0=t, scalar=1.5, in1=y, op0=ALU.add, op1=ALU.mult))


def transpose_rows(k, src, banks, done):
    for t in range(QT):
        for c in range(KT):
            last = k.nc.tensor.transpose(k.ps[:, banks, c * S + t * P:c * S + (t + 1) * P],
                                         src[:, t, c * P:(c + 1) * P], k.ident[:, :])
    last.then_inc(done, 1)


def split_q(k, link):
    v = k.nc.vector
    link(v.tensor_copy(k.q_p[:, 0], k.q_f[:, :, :]))
    link(v.tensor_tensor(k.q_r[:, :, :], k.q_f[:, :, :], k.q_p[:, 0], ALU.subtract))
    link(v.tensor_copy(k.q_p[:, 1], k.q_r[:, :, :]))
    return v.tensor_tensor(k.q_p[:, 2], k.q_r[:, :, :], k.q_p[:, 1], ALU.subtract)


def store_q_parts(k, sp, layer):
    split, stored, loaded = k.sem("q_split"), k.sem("q_stored"), k.sem("q_loaded")
    sp.wait_ge(split, layer + 1)
    for p in range(PARTS):
        for t in range(KT):
            sp.dma_start(k.qd[layer, t * 8:(t + 1) * 8, p * DH:(p + 1) * DH, :],
                         k.q_p[:, p, t, :]).then_inc(stored, 16)
    sp.wait_ge(stored, 16 * PARTS * KT * (layer + 1))
    rows = [(r * DH, r // 2) for r in range(2 * PARTS)] + [(LOROW, 0)]
    for row, p in rows:
        sp.dma_start(k.q_all[row:row + DH, :, :],
                     k.qd[layer, :, p * DH:(p + 1) * DH, :].rearrange("h d q -> d h q")).then_inc(loaded, 16)
    sp.wait_ge(loaded, 16 * len(rows) * (layer + 1))


def load_k_unit(k, sp, kd, h, half, slot, loaded):
    ks = slice(half * UNIT_KEYS, (half + 1) * UNIT_KEYS)
    for r in range(PARTS):
        sp.dma_start(k.k_st[2 * DH * r:2 * DH * (r + 1), slot, :], kd[h, 0:2 * DH, ks]).then_inc(loaded, 16)
    sp.dma_start(k.k_st[LOROW:STACK, slot, :], kd[h, 2 * DH:3 * DH, ks]).then_inc(loaded, 16)


K_LOADS = PARTS + 1


def stage_prepare(k):
    nc, i = k.nc, k.i
    n_blk = S2 // KSPLIT
    blk = k.probs[:, 0].rearrange("p c q -> p (c q)").rearrange("p (b n) -> p b n", n=KSPLIT)
    res = k.probs[:, 1].rearrange("p c q -> p (c q)")[:, 0:2 * KSPLIT].rearrange("p (b n) -> p b n", n=KSPLIT)
    parts = k.v_proj[:, 0:12].rearrange("p c q -> p (c q)").bitcast(BF16).rearrange("p (b s n) -> p b s n", b=2, s=PARTS)

    with nc.Block() as block:
        @block.sync
        def _(sp):
            sp.dma_start(k.x[:, :, :], i["x"].rearrange("a (t p) d -> p (a t) d", p=P)).then_inc(k.sem("x_in"), 16)
            for n in range(KT * n_blk):
                t, b = divmod(n, n_blk)
                if n >= 4:
                    sp.wait_ge(k.sem("k0_split"), n - 3)
                sp.dma_start(blk[:, n % 4], i["ctxT"][t * P:(t + 1) * P, b * KSPLIT:(b + 1) * KSPLIT]
                             ).then_inc(k.sem(f"ctxT_in{n % 4}"), 16)
            store_q_parts(k, sp, 0)

        @block.gpsimd
        def _(pool):
            g = nc.gpsimd
            link = Order(pool, k.sem("pool_order"), k.pool_ordered).link
            link(g.memset(k.ident[:, :], 0.0))
            link(g.affine_select(out=k.ident[:, :], in_=k.ident[:, :], compare_op=ALU.not_equal, fill=1.0, base=0,
                                 pattern=[[-1, P]], channel_multiplier=1))
            link(g.memset(k.w_proj0[:, :, :], 0.0))
            link(g.memset(k.ones_row[:, :], 1.0))
            link(g.memset(k.ones_sq[:, :], 1.0))
            link(g.memset(k.v_st[:, :, :, :], 0.0))
            link(g.memset(k.k_st[MAXROW:LOROW, :, :], 1.0))
            link(g.memset(k.q_all[MAXROW:LOROW, :, :], 0.0))
            for n in range(KT * n_blk):
                t, b = divmod(n, n_blk)
                pool.wait_ge(k.sem("k0_split"), n + 1)
                for p in range(PARTS):
                    g.dma_start(k.kd0[t * 8:(t + 1) * 8, p * DH:(p + 1) * DH, b * KSPLIT:(b + 1) * KSPLIT],
                                parts[:, n % 2, p, :]).then_inc(k.sem(f"k0_stored{n % 2}"), 16)
            for b in range(2):
                pool.wait_ge(k.sem(f"k0_stored{b}"), 16 * PARTS * KT * n_blk // 2)

        @block.scalar
        def _(act):
            a = nc.scalar
            one = k.sem("small_in")
            act.dma_start(k.l0_scale[:, :], i["L0_xattn_scale"].to_broadcast([P, 1])).then_inc(one, 16)
            act.dma_start(k.l0_logc[:, :], i["L0_xattn_log_C"].to_broadcast([P, 1])).then_inc(one, 16)
            act.dma_start(k.keep_u8[:, :], i["mask_bk0_by_chunk"]).then_inc(one, 16)
            act.dma_start(k.v_rows[:, :, :], i["ctx_1024"].rearrange("a (c p) d -> p (a c) d", p=P)).then_inc(k.sem("ctx_in"), 16)
            act.dma_start(k.w_out0[:, :, :], i["L0_xattn_W_outT"].rearrange("(t p) n -> p t n", p=P)).then_inc(k.sem("w1_in"), 16)
            act.dma_start(k.wk1[:, :, :], i["L1_xattn_WkT"].rearrange("(t p) n -> p t n", p=P)).then_inc(k.sem("w1_in"), 16)
            act.dma_start(k.wv1[:, :, :], i["L1_xattn_WvT"].rearrange("(t p) n -> p t n", p=P)).then_inc(k.sem("w1_in"), 16)
            act.dma_start(k.bkv1[0:1, 0, :], i["L1_xattn_bk"].unsqueeze(0)).then_inc(k.sem("w1_in"), 16)
            act.dma_start(k.bkv1[0:1, 1, :], i["L1_xattn_bv"].unsqueeze(0)).then_inc(k.sem("w1_in"), 16)
            w2 = k.sem("w2_in")
            act.dma_start(k.w_qkv0[:, :, :], i["L0_attn_w_qkvT"].rearrange("(t p) n -> p t n", p=P)).then_inc(w2, 16)
            act.dma_start(k.b_qkv0[:, :], i["L0_attn_b_qkv"].unsqueeze(0)).then_inc(w2, 16)
            act.dma_start(k.b_proj0[:, :], i["L0_attn_b_proj"].unsqueeze(0)).then_inc(w2, 16)
            act.dma_start(k.w_qkn[:, 0, :], i["L0_attn_qn_w"].unsqueeze(0).to_broadcast([P, DH])).then_inc(w2, 16)
            act.dma_start(k.w_qkn[:, 1, :], i["L0_attn_kn_w"].unsqueeze(0).to_broadcast([P, DH])).then_inc(w2, 16)
            act.dma_start(k.w_ffn0[:, :, :], i["L0_ffn_weightT"].rearrange("(t p) n -> p t n", p=P)).then_inc(w2, 16)
            act.dma_start(k.w1_q[:, :, :], i["L1_xattn_WqT"].rearrange("(t p) n -> p t n", p=P)).then_inc(w2, 16)
            act.dma_start(k.w1_o[:, :, :], i["L1_xattn_WoT"].rearrange("(t p) n -> p t n", p=P)).then_inc(w2, 16)
            act.dma_start(k.b1_qo[0:1, 0, :], i["L1_xattn_bq"].unsqueeze(0)).then_inc(w2, 16)
            act.dma_start(k.b1_qo[0:1, 1, :], i["L1_xattn_bo"].unsqueeze(0)).then_inc(w2, 16)
            act.wait_ge(k.sem("pool_order"), 3)
            for m in range(4):
                act.dma_start(k.w_proj0[32 * m:32 * m + DH, :, :],
                              i["L0_attn_w_projT"].rearrange("(g m d) n -> m d g n", m=4, d=DH)[m]).then_inc(w2, 16)
            act.wait_ge(one, 48)
            a.activation(k.cap[:, :], k.l0_logc[:, :], ACT.Exp).then_inc(k.sem("cap"), 1)
            act.wait_ge(k.sem("cap"), 1)
            a.activation(k.neg_cap[:, :], k.cap[:, :], ACT.Copy, scale=-1.0).then_inc(k.sem("cap"), 1)
            for n in range(KT * n_blk):
                act.wait_ge(k.sem(f"ctxT_in{n % 4}"), 16 * (n // 4 + 1))
                if n >= 2:
                    act.wait_ge(k.sem(f"k0_stored{n % 2}"), 16 * PARTS * (n // 2))
                a.activation(parts[:, n % 2, 0, :], blk[:, n % 4], ACT.Copy).then_inc(k.sem("k0_hi"), 1)
                act.wait_ge(k.sem("k0_res"), n + 1)
                a.activation(parts[:, n % 2, 1, :], res[:, n % 2], ACT.Copy).then_inc(k.sem("k0_mid"), 1)
            act.wait_ge(k.sem("w1_in"), 80)
            act.wait_ge(k.sem("w2_in"), 16 * 14)
            act.wait_ge(k.sem("ctx_in"), 16)

        @block.vector
        def _(dve):
            v = nc.vector
            link = Order(dve, k.sem("dve_order"), k.dve_ordered).link
            dve.wait_ge(k.sem("x_in"), 16)
            layer_norm(k, dve, link, k.x, k.xn, k.sem("xn0"))
            dve.wait_ge(k.sem("pool_order"), 2)
            link(v.tensor_copy(k.ident_bf[:, :], k.ident[:, :]))
            link(v.tensor_reduce(k.quad_sum[:, :], k.ident[:, :].rearrange("p (g j) -> p j g", g=4), AX.X, ALU.add))
            link(v.tensor_reduce(k.head_mask[:, :], k.ident[:, :].rearrange("p (j d) -> p j d", d=DH), AX.X, ALU.add))
            dve.wait_ge(k.sem("small_in"), 48)
            link(v.tensor_scalar(k.keep[:, :], k.keep_u8[:, :], -1.0, 1.0, ALU.mult, ALU.add))
            dve.wait_ge(k.sem("pool_order"), 6)
            for b in range(2):
                link(v.tensor_copy(k.v_st[:, b, :, DH], k.keep[:, :]))
            dve.wait_ge(k.sem("xnT_ps"), 1)
            link(v.tensor_scalar(k.q_f[:, :, :].rearrange("p c q -> p (c q)"), k.ps[:, 0, :], k.l0_scale[:, 0:1],
                                 1.0 / np.sqrt(DH), ALU.mult, ALU.mult))
            split_q(k, link).then_inc(k.sem("q_split"), 1)
            for n in range(KT * n_blk):
                dve.wait_ge(k.sem("k0_hi"), n + 1)
                if n >= 2:
                    dve.wait_ge(k.sem("k0_split"), n - 1)
                v.tensor_tensor(res[:, n % 2], blk[:, n % 4], parts[:, n % 2, 0, :], ALU.subtract
                                ).then_inc(k.sem("k0_res"), 1)
                dve.wait_ge(k.sem("k0_mid"), n + 1)
                v.tensor_tensor(parts[:, n % 2, 2, :], res[:, n % 2], parts[:, n % 2, 1, :], ALU.subtract
                                ).then_inc(k.sem("k0_split"), 1)

        @block.tensor
        def _(pe):
            pe.wait_ge(k.sem("pool_order"), 2)
            pe.wait_ge(k.sem("xn0"), QT)
            transpose_rows(k, k.xn, 0, k.sem("xnT_ps"))


def stage_cross0(k):
    nc, i = k.nc, k.i
    probs = k.probs[:, :, :, :]
    s = {n: k.sem("a_" + n) for n in (
        "scores", "tanh", "exp", "pv", "staged", "acc_copied", "sel", "o_read", "rec", "blk_in",
        "proj", "v_copied", "kd_ops", "kd_split")}
    k_in = [k.sem(f"a_k_in{j}") for j in range(4)]
    kd_out = [k.sem(f"a_kd_out{j}") for j in range(2)]

    def scores_bank(g):
        return k.ps[:, 2 * (g % 2):2 * (g % 2) + 2, :].rearrange("p b (c q) -> p (b c) q", q=S)

    with nc.Block() as block:
        @block.sync
        def _(sp):
            def body(it, first):
                key0 = it * CBLK if first else sp.snap(it * CBLK)
                block = i["ctxT"].rearrange("(t p) n -> p t n", p=P)[:, :, bass.ds(key0, CBLK)]
                if not first:
                    sp.wait_ge(s["proj"], 4 * it)
                sp.dma_start(k.ctx_blk[:, :, :], block
                             ).then_inc(s["blk_in"], 16)
                for j in range(4):
                    if not first:
                        sp.wait_ge(s["scores"], (it - 1) * 16 + 4 * (j + 1))
                    load_k_unit(k, sp, k.kd0, 2 * it + j // 2, j % 2, j, k_in[j])
                for j in range(2):
                    sp.wait_ge(s["kd_split"], 2 * it + j + 1)
                    for p in (1, 2, 0):
                        sp.dma_start(k.kd1[8 * j:8 * j + 8, p * DH:(p + 1) * DH, bass.ds(key0, CBLK)],
                                     k.kd_bf[:, j, p, :]).then_inc(kd_out[j], 16)

            body(0, True)
            with sp.Fori(1, H // 2) as it:
                body(it, False)
            for j in range(2):
                sp.wait_ge(kd_out[j], 16 * PARTS * (H // 2))

        @block.gpsimd
        def _(pool):
            g = nc.gpsimd

            def stage(h, b, fresh):
                if not fresh:
                    pool.wait_ge(s["pv"], 2 * h - 2)
                g.tensor_tensor(k.v_st[:, b, :, 0:DH], k.v_rows[:, :, bass.ds(h * DH, DH)],
                                k.keep[:, :].unsqueeze(2).to_broadcast([P, NCH, DH]), ALU.mult).then_inc(s["staged"], 1)
                g.tensor_copy(k.q_st[0:STACK, b, :], k.q_all[0:STACK, h, :]).then_inc(s["staged"], 1)

            stage(0, 0, True)
            stage(1, 1, True)
            with pool.Fori(1, H // 2) as it:
                stage(2 * it, 0, False)
                stage(2 * it + 1, 1, False)

        @block.scalar
        def _(act):
            a = nc.scalar

            def body(it, first):
                for j in range(4):
                    u = 4 * it + j
                    for g in range(GROUPS):
                        act.wait_ge(s["scores"], 4 * u + g + 1)
                        if g == 0 and not (first and j < 2):
                            act.wait_ge(s["pv"], u - 1)
                        a.activation(probs[:, j % 2, 4 * g:4 * g + 4, :], scores_bank(g), ACT.Tanh).then_inc(s["tanh"], 1)
                    act.wait_ge(s["tanh"], 4 * u + 4)
                    a.activation(probs[:, j % 2], probs[:, j % 2], ACT.Exp, bias=k.neg_cap[:, 0:1], scale=k.cap[:, 0:1]
                                 ).then_inc(s["exp"], 1)

            body(0, True)
            with act.Fori(1, H // 2) as it:
                body(it, False)

        @block.tensor
        def _(pe):
            t = nc.tensor

            def qk(it, j, g, first):
                u = 4 * it + j
                if g == 0:
                    pe.wait_ge(k_in[j], 16 * K_LOADS * (it + 1))
                    if j % 2 == 0:
                        pe.wait_ge(s["staged"], u + 2)
                if not (first and j == 0 and g < 2):
                    pe.wait_ge(s["tanh"], 4 * u + g - 1)
                out = scores_bank(g)
                for c in range(GROUP_CH):
                    n = GROUP_CH * g + c
                    last = t.matmul(out[:, c, :], k.k_st[0:STACK, j, n * P:(n + 1) * P], k.q_st[0:STACK, j // 2, :],
                                    start=True, stop=True)
                last.then_inc(s["scores"], 1)

            def pv(it, j, c, first):
                b = j // 2
                if c == 0:
                    pe.wait_ge(s["exp"], 4 * it + j + 1)
                    if j % 2 == 0 and not first:
                        pe.wait_ge(s["o_read"], 2 * it + b - 1)
                for m in range(4):
                    ch = 4 * c + m
                    last = t.matmul(k.ps[32 * m:32 * m + 32, 4 + b, 0:S], k.v_st[:, b, (j % 2) * UNIT_CH + ch, :],
                                    probs[:, j % 2, ch, :], start=(j % 2 == 0 and c == 0), stop=(j % 2 == 1 and c == 3))
                if c == 3:
                    last.then_inc(s["pv"], 1)

            def sel(h, b):
                pe.wait_ge(s["acc_copied"], h + 1)
                for q in range(QT):
                    last = t.matmul(k.ps[:, 4 + b, S + 32 * q:S + 32 * (q + 1)], k.acc_sb[:, b, q * P:(q + 1) * P],
                                    k.quad_sum[:, :], start=True, stop=True)
                last.then_inc(s["sel"], 1)

            def project(it, j, first):
                if j == 0:
                    pe.wait_ge(s["blk_in"], 16 * (it + 1))
                if j >= 2:
                    pe.wait_ge(s["kd_split"], 2 * it + j - 1)
                elif not first:
                    pe.wait_ge(s["v_copied"], 2 * it + j - 1)
                bank = 6 + j % 2
                if j < 2:
                    o = k.ps[:, bank, :]
                    for c in range(KT):
                        t.matmul(o, k.wk1[:, c, j * P:(j + 1) * P], k.ctx_blk[:, c, :], start=(c == 0), stop=False)
                    last = t.matmul(o, k.bkv1[0:1, 0, j * P:(j + 1) * P], k.ones_row[0:1, 0:CBLK], start=False, stop=True)
                else:
                    for m in range(2):
                        ch = 2 * (j - 2) + m
                        o = k.ps[:, bank, m * D:(m + 1) * D]
                        for c in range(KT):
                            t.matmul(o, k.ctx_blk[:, c, ch * P:(ch + 1) * P], k.wv1[:, c, :], start=(c == 0), stop=False)
                        last = t.matmul(o, k.ones_row[0:1, 0:P], k.bkv1[0:1, 1, :], start=False, stop=True)
                last.then_inc(s["proj"], 1)

            def body(it, first):
                for j in range(4):
                    pit, pj = (it - 1, 3) if j == 0 else (it, j - 1)
                    for g, cs in enumerate([[], [0, 1], [2], [3]]):
                        qk(it, j, g, first)
                        for c in cs:
                            if not (first and j == 0):
                                pv(pit, pj, c, first)
                    if j == 1 and not first:
                        sel(2 * it - 1, 1)
                    if j == 3:
                        sel(2 * it, 0)
                    project(it, j, first)

            body(0, True)
            with pe.Fori(1, H // 2) as it:
                body(it, False)
            for c in range(4):
                pv(H // 2 - 1, 3, c, False)
            sel(H - 1, 1)

        @block.vector
        def _(dve):
            v = nc.vector

            def split_k(it, j, first):
                n = 4 * it + j
                base = 6 * it + 3 * j
                src = k.ps[:, 6 + j, :]
                dve.wait_ge(s["proj"], n + 1)
                if not first:
                    dve.wait_ge(kd_out[j], 16 * PARTS * it)
                v.tensor_copy(k.kd_bf[:, j, 0, :], src).then_inc(s["kd_ops"], 1)
                dve.wait_ge(s["kd_ops"], base + 1)
                v.tensor_tensor(k.kd_r[:, j, :], src, k.kd_bf[:, j, 0, :], ALU.subtract).then_inc(s["kd_ops"], 1)
                dve.wait_ge(s["kd_ops"], base + 2)
                v.tensor_copy(k.kd_bf[:, j, 1, :], k.kd_r[:, j, :]).then_inc(s["kd_ops"], 1)
                dve.wait_ge(s["kd_ops"], base + 3)
                v.tensor_tensor(k.kd_bf[:, j, 2, :], k.kd_r[:, j, :], k.kd_bf[:, j, 1, :], ALU.subtract).then_inc(s["kd_split"], 1)

            def body(it, first):
                for j in range(4):
                    if j % 2 == 0 and not (first and j == 0):
                        copy_acc(2 * it - 1 + j // 2, (j // 2 + 1) % 2)
                    if j == 1 and not first:
                        normalise(2 * it - 1, 1)
                    if j == 3:
                        normalise(2 * it, 0)
                    if j < 2:
                        split_k(it, j, first)
                    else:
                        dve.wait_ge(s["proj"], 4 * it + j + 1)
                        v.tensor_copy(k.v_proj[:, bass.ds(4 * it + 2 * (j - 2), 2), :],
                                      k.ps[:, 6 + j % 2, :].rearrange("p (c d) -> p c d", d=D)).then_inc(s["v_copied"], 1)

            def copy_acc(h, b):
                dve.wait_ge(s["pv"], 2 * h + 2)
                v.tensor_copy(k.acc_sb[:, b, :], k.ps[:, 4 + b, 0:S]).then_inc(s["acc_copied"], 1)

            def normalise(h, b):
                o = k.ps[:, 4 + b, S:S + 32 * QT].rearrange("p (q n) -> p q n", q=QT)
                dve.wait_ge(s["sel"], h + 1)
                v.reciprocal(k.rec[:, b, :], o[:, :, DH]).then_inc(s["rec"], 1)
                dve.wait_ge(s["rec"], h + 1)
                v.tensor_tensor(k.o_nat[:, :, bass.ds(h * DH, DH)], o[:, :, 0:DH],
                                k.rec[:, b, :].unsqueeze(2).to_broadcast([P, QT, DH]), ALU.mult).then_inc(s["o_read"], 1)

            body(0, True)
            with dve.Fori(1, H // 2) as it:
                body(it, False)
            copy_acc(H - 1, 1)
            normalise(H - 1, 1)



def rows_linear(k, src, n_k, w, bias, bank, done):
    t = k.nc.tensor
    for q in range(QT):
        o = k.ps[:, bank, q * D:(q + 1) * D]
        for c in range(n_k):
            last = t.matmul(o, src[:, c, q * P:(q + 1) * P], w[:, c, :], start=(c == 0),
                            stop=(bias is None and c == n_k - 1))
        if bias is not None:
            last = t.matmul(o, k.ones_row[0:1, 0:P], bias, start=False, stop=True)
    last.then_inc(done, 1)


def update_pe(k, pe, tag, src, n_k, w, bias, turn, norm=True):
    if turn:
        transpose_rows(k, k.o_nat, 0, k.sem(tag + "_oT_ps"))
    pe.wait_ge(k.sem(tag + "_oT"), 1)
    rows_linear(k, src, n_k, w, bias, 1, k.sem(tag + "_y"))
    if norm:
        pe.wait_ge(k.sem(tag + "_xn"), QT)
        transpose_rows(k, k.xn, 2, k.sem(tag + "_xnT_ps"))


def update_dve(k, dve, link, tag, turn, norm=True):
    v = k.nc.vector
    if turn:
        dve.wait_ge(k.sem(tag + "_oT_ps"), 1)
        v.tensor_copy(k.oT[:, :, :].rearrange("p c q -> p (c q)"), k.ps[:, 0, :]).then_inc(k.sem(tag + "_oT"), 1)
    dve.wait_ge(k.sem(tag + "_y"), 1)
    xf = k.x[:, :, :].rearrange("p t d -> p (t d)")
    link(v.tensor_tensor(xf, xf, k.ps[:, 1, :], ALU.add))
    if norm:
        layer_norm(k, dve, link, k.x, k.xn, k.sem(tag + "_xn"))
        dve.wait_ge(k.sem(tag + "_xnT_ps"), 1)
        v.tensor_copy(k.xnT[:, :, :].rearrange("p c q -> p (c q)"), k.ps[:, 2, :]).then_inc(k.sem(tag + "_xnT"), 1)


class Small:

    def __init__(self, k, heads, step, causal, q_of, k_of, v_of, out_of, interleave=1):
        self.causal = causal
        self.interleave = interleave
        self.q_of, self.k_of, self.v_of, self.out_of = q_of, k_of, v_of, out_of
        self.base = k.small_pairs
        self.step = step
        self.pairs = [(h0 + r, q) for h0 in range(0, heads, 2 * step) for r in range(step) for q in range(QT)]

        k.small_pairs += len(self.pairs)

    def tiles(self, q):
        return q + 1 if self.causal else QT


def small_pe(k, pe, a):
    t = k.nc.tensor
    s = {n: k.sem("small_" + n) for n in ("S", "exp", "pn", "PT", "PT_copied", "out")}

    def scores(n):
        h0, q = a.pairs[n]
        nk = a.tiles(q) * P
        if n >= 2:
            pe.wait_ge(s["exp"], 2 * (a.base + n - 1))
        for e in range(2):
            o = k.ps[:, n % 2, e * S:e * S + nk]
            last = t.matmul(o, a.q_of(h0 + e * a.step, q), a.k_of(h0 + e * a.step, nk), start=True, stop=not a.causal)
            if a.causal:
                last = t.matmul(o[:, nk - P:nk], k.ident_bf[:, :], k.causal[:, :], start=False, stop=True)
        last.then_inc(s["S"], 1)

    def turn(n):
        h0, q = a.pairs[n]
        pe.wait_ge(s["pn"], 2 * (a.base + n + 1))
        if n >= 2:
            pe.wait_ge(s["PT_copied"], a.base + n - 1)
        for e in range(2):
            for c in range(a.tiles(q)):
                last = t.transpose(k.ps[:, 2 + n % 2, (2 * e + c) * P:(2 * e + c + 1) * P],
                                   k.sp_rows[:, n % 2, e, c * P:(c + 1) * P], k.ident[:, :])
        last.then_inc(s["PT"], 1)

    def values(n):
        h0, q = a.pairs[n]
        pe.wait_ge(s["PT_copied"], a.base + n + 1)
        for e in range(2):
            for r in range(a.interleave):
                for c in range(a.tiles(q)):
                    cols = k.sp_T[:, n % 2, (2 * e + c) * P:(2 * e + c + 1) * P].rearrange("p (m r) -> p m r", r=a.interleave)
                    last = t.matmul(a.out_of(h0 + e * a.step, q, r), a.v_of(h0 + e * a.step, c), cols[:, :, r],
                                    start=(c == 0), stop=(c == a.tiles(q) - 1))
        last.then_inc(s["out"], 1)

    n_pairs = len(a.pairs)
    scores(0)
    for n in range(n_pairs):
        if n + 1 < n_pairs:
            scores(n + 1)
        if n >= 1:
            values(n - 1)
        turn(n)
    values(n_pairs - 1)


def small_act(k, act, a):
    sc = k.nc.scalar
    s = {n: k.sem("small_" + n) for n in ("max", "exp", "PT", "PT_copied", "out")}

    def copy_turned(n):
        q = a.pairs[n][1]
        nk = a.tiles(q) * P
        act.wait_ge(s["PT"], a.base + n + 1)
        if n >= 2:
            act.wait_ge(s["out"], a.base + n - 1)
        sc.activation(k.sp_T[:, n % 2, :].rearrange("p (e m) -> p e m", e=2)[:, :, 0:nk],
                      k.ps[:, 2 + n % 2, :].rearrange("p (e m) -> p e m", e=2)[:, :, 0:nk], ACT.Copy).then_inc(s["PT_copied"], 1)

    for n, (h0, q) in enumerate(a.pairs):
        nk = a.tiles(q) * P
        act.wait_ge(s["max"], a.base + n + 1)
        if n >= 2:
            act.wait_ge(s["PT"], a.base + n - 1)
        for e in range(2):
            sc.activation(k.sp_rows[:, n % 2, e, 0:nk], k.ps[:, n % 2, e * S:e * S + nk], ACT.Exp,
                          bias=k.nmax[:, 2 * n + e:2 * n + e + 1],
                          accum_out=k.sums[:, 2 * n + e:2 * n + e + 1]).then_inc(s["exp"], 1)
        if n >= 1:
            copy_turned(n - 1)
    copy_turned(len(a.pairs) - 1)


def small_dve(k, dve, a):
    v = k.nc.vector
    s = {n: k.sem("small_" + n) for n in ("S", "max", "exp", "pn", "inv")}

    def row_max(n):
        q = a.pairs[n][1]
        nk = a.tiles(q) * P
        dve.wait_ge(s["S"], a.base + n + 1)
        v.tensor_reduce(k.nmax[:, 2 * n:2 * n + 2], k.ps[:, n % 2, :].rearrange("p (e m) -> p e m", e=2)[:, :, 0:nk],
                        AX.X, ALU.max, negate=True).then_inc(s["max"], 1)

    row_max(0)
    for n, (h0, q) in enumerate(a.pairs):
        nk = a.tiles(q) * P
        if n + 1 < len(a.pairs):
            row_max(n + 1)
        dve.wait_ge(s["exp"], 2 * (a.base + n + 1))
        v.reciprocal(k.inv[:, 2 * n:2 * n + 2], k.sums[:, 2 * n:2 * n + 2]).then_inc(s["inv"], 1)
        dve.wait_ge(s["inv"], a.base + n + 1)
        for e in range(2):
            v.tensor_scalar(k.sp_rows[:, n % 2, e, 0:nk], k.sp_rows[:, n % 2, e, 0:nk],
                            k.inv[:, 2 * n + e:2 * n + e + 1], None, ALU.mult).then_inc(s["pn"], 1)


def stage_self0(k):
    nc = k.nc
    vec, sc, t = nc.vector, nc.scalar, nc.tensor
    att = Small(k, H, 1, False,
                q_of=lambda h, q: k.q_mask[:, h, q * P:(q + 1) * P],
                k_of=lambda h, nk: k.kT_self[:, h // 8, 0:nk],
                v_of=lambda h, c: k.v_self[:, c, h, :],
                out_of=lambda h, q, r: k.ps[32 * (h % 4):32 * (h % 4) + 32, 4 + h // 8, (h // 4 % 2) * S + q * P:(h // 4 % 2) * S + (q + 1) * P])
    with nc.Block() as block:
        @block.gpsimd
        def _(pool):
            nc.gpsimd.memset(k.v_self[:, :, :, :], 0.0).then_inc(k.sem("b_v_z"), 1)

        @block.tensor
        def _(pe):
            update_pe(k, pe, "a", k.oT, KT, k.w_out0, None, True)
            pe.wait_ge(k.sem("a_xnT"), 1)
            for q in range(QT):
                for c in range(KT):
                    t.matmul(k.ps[:, 3 + q, :], k.xnT[:, c, q * P:(q + 1) * P], k.w_qkv0[:, c, 0:2 * D], start=(c == 0), stop=False)
                last = t.matmul(k.ps[:, 3 + q, :], k.ones_row[0:1, 0:P], k.b_qkv0[0:1, 0:2 * D], start=False, stop=True)
            last.then_inc(k.sem("b_qk"), 1)
            rows_linear(k, k.xnT, KT, k.w_qkv0[:, :, 2 * D:3 * D], k.b_qkv0[0:1, 2 * D:3 * D], 5, k.sem("b_v"))
            pe.wait_ge(k.sem("c_w_sum"), 1)
            t.matmul(k.ps[:, 7, 0:1], k.ones_sq[:, :], k.w_sum[:, :], start=True, stop=True).then_inc(k.sem("c_w_total"), 1)
            pe.wait_ge(k.sem("b_qkn"), QT)
            for q in range(QT):
                for half in range(2):
                    for c in range(KT):
                        last = t.transpose(k.ps[:, half, c * S + q * P:c * S + (q + 1) * P],
                                           k.qk[:, q, half * D + c * P:half * D + (c + 1) * P], k.ident[:, :])
            last.then_inc(k.sem("b_qkT"), 1)
            pe.wait_ge(k.sem("b_kT"), 1)
            pe.wait_ge(k.sem("b_qm_dve"), H // 2)
            pe.wait_ge(k.sem("b_qm_act"), H // 2)
            pe.wait_ge(k.sem("b_v_in"), 1)
            small_pe(k, pe, att)
            update_pe(k, pe, "b", k.oT_pad, 4, k.w_proj0, k.b_proj0[0:1, :], False, norm=False)
            pe.wait_ge(k.sem("c_aq"), 1)
            o = k.ps[:, 2, :].bitcast(BF16)
            for q in range(QT):
                for c in range(KT):
                    last = t.transpose(o[:, c * S + q * P:c * S + (q + 1) * P], k.a_q[:, q, c * P:(c + 1) * P], k.ident_bf[:, :])
            last.then_inc(k.sem("c_aqT_ps"), 1)
            pe.wait_ge(k.sem("c_aqT"), 1)
            rows_linear(k, k.a_qT, KT, k.w_tern, None, 3, k.sem("c_y"))
            pe.wait_ge(k.sem("c_xn"), QT)
            transpose_rows(k, k.xn, 2, k.sem("c_xnT_ps"))

        @block.scalar
        def _(act):
            act.wait_ge(k.sem("b_qk_rows"), 1)
            sc.activation(k.qk_sq[:, :, :], k.qk[:, :, :], ACT.Square).then_inc(k.sem("b_sq"), 1)
            act.wait_ge(k.sem("b_qkT"), 1)
            for h in range(8, H):
                sc.activation(k.q_mask[:, h, :], k.ps[:, 0, S:2 * S], ACT.Copy, scale=k.head_mask[:, h - 8:h - 7]).then_inc(k.sem("b_qm_act"), 1)
            small_act(k, act, att)

        @block.vector
        def _(dve):
            link = Order(dve, k.sem("dve_order"), k.dve_ordered).link
            update_dve(k, dve, link, "a", True)
            vec.tensor_reduce(k.w_sum[:, :], k.w_ffn0[:, :, :].rearrange("p t n -> p (t n)"), AX.X, ALU.add,
                              apply_absolute_value=True).then_inc(k.sem("c_w_sum"), 1)
            dve.wait_ge(k.sem("b_qk"), 1)
            vec.tensor_copy(k.qk[:, :, :], k.ps[:, 3:5, :]).then_inc(k.sem("b_qk_rows"), 1)
            dve.wait_ge(k.sem("b_v"), 1)
            dve.wait_ge(k.sem("b_v_z"), 1)
            vec.tensor_copy(k.v_self[:, :, :, 0:DH], k.ps[:, 5, :].rearrange("p (t h d) -> p t h d", t=KT, d=DH)).then_inc(k.sem("b_v_in"), 1)
            dve.wait_ge(k.sem("b_sq"), 1)
            link(vec.tensor_reduce(k.rs_v[:, :], k.qk_sq[:, :, :].rearrange("p t (h d) -> p (t h) d", d=DH), AX.X, ALU.add))
            link(vec.tensor_scalar(k.rs_v[:, :], k.rs_v[:, :], 1.0 / DH, 1e-6, ALU.mult, ALU.add))
            rsqrt(k, link, 64)
            link(vec.tensor_scalar(k.w_qkn[:, 0, :], k.w_qkn[:, 0, :], 1.0 / np.sqrt(DH), None, ALU.mult))
            heads = k.qk[:, :, :].rearrange("p t (h d) -> p (t h) d", d=DH)
            link(vec.tensor_tensor(heads, heads, k.rs_y[:, :].unsqueeze(2).to_broadcast([P, 4 * H, DH]), ALU.mult))
            for q in range(QT):
                row = k.qk[:, q, :].rearrange("p (s h d) -> p s h d", s=2, d=DH)
                vec.tensor_tensor(row, row, k.w_qkn[:, :, :].unsqueeze(2).to_broadcast([P, 2, H, DH]), ALU.mult).then_inc(k.sem("b_qkn"), 1)
            dve.wait_ge(k.sem("b_qkT"), 1)
            vec.tensor_copy(k.kT_self[:, :, :].rearrange("p t n -> p (t n)"), k.ps[:, 1, :]).then_inc(k.sem("b_kT"), 1)
            dve.wait_ge(k.sem("b_qm_act"), H // 2)
            for h in range(8):
                vec.tensor_scalar(k.q_mask[:, h, :], k.ps[:, 0, 0:S], k.head_mask[:, h:h + 1], None, ALU.mult).then_inc(k.sem("b_qm_dve"), 1)
            dve.wait_ge(k.sem("c_w_total"), 1)
            link(vec.tensor_scalar(k.w_scale[:, :], k.ps[:, 7, 0:1], 1.0 / (D * D), 1e-8, ALU.mult, ALU.add))
            link(vec.reciprocal(k.w_inv[:, :], k.w_scale[:, :]))
            link(vec.tensor_scalar(k.w_ffn0[:, :, :], k.w_ffn0[:, :, :], k.w_inv[:, 0:1], ROUND, ALU.mult, ALU.add))
            link(vec.tensor_scalar(k.w_ffn0[:, :, :], k.w_ffn0[:, :, :], -ROUND, 1.0, ALU.add, ALU.min))
            link(vec.tensor_scalar(k.w_tern[:, :, :], k.w_ffn0[:, :, :], -1.0, None, ALU.max))
            small_dve(k, dve, att)
            dve.wait_ge(k.sem("small_out"), att.base + len(att.pairs))
            vec.tensor_copy(k.oT_pad[:, :, :].rearrange("p (b g) q -> p b (g q)", b=2), k.ps[:, 4:6, :]).then_inc(k.sem("b_oT"), 1)
            update_dve(k, dve, link, "b", False, norm=False)
            layer_norm(k, dve, link, k.x, k.xn, k.sem("c_xn0"))
            dve.wait_ge(k.sem("c_xn0"), QT)
            link(vec.tensor_reduce(k.a_scale[:, :], k.xn[:, :, :], AX.X, ALU.max, apply_absolute_value=True))
            link(vec.tensor_scalar(k.a_scale[:, :], k.a_scale[:, :], 1e-8, None, ALU.add))
            link(vec.reciprocal(k.a_inv[:, :], k.a_scale[:, :]))
            for q in range(QT):
                link(vec.tensor_scalar(k.xn[:, q, :], k.xn[:, q, :], k.a_inv[:, q:q + 1], 127.0, ALU.mult, ALU.mult))
            link(vec.tensor_scalar(k.xn[:, :, :], k.xn[:, :, :], 127.0, -128.0, ALU.min, ALU.max))
            vec.tensor_scalar(k.a_q[:, :, :], k.xn[:, :, :], ROUND, -ROUND, ALU.add, ALU.add).then_inc(k.sem("c_aq"), 1)
            dve.wait_ge(k.sem("c_aqT_ps"), 1)
            vec.tensor_copy(k.a_qT[:, :, :].rearrange("p c q -> p (c q)"), k.ps[:, 2, :].bitcast(BF16)[:, 0:KT * S]).then_inc(k.sem("c_aqT"), 1)
            link(vec.tensor_scalar(k.a_scale[:, :], k.a_scale[:, :], k.w_scale[:, 0:1], 1.0 / 127.0, ALU.mult, ALU.mult))
            dve.wait_ge(k.sem("c_y"), 1)
            for q in range(QT):
                link(vec.scalar_tensor_tensor(out=k.x[:, q, :], in0=k.ps[:, 3, q * D:(q + 1) * D], scalar=k.a_scale[:, q:q + 1],
                                              in1=k.x[:, q, :], op0=ALU.mult, op1=ALU.add))
            layer_norm(k, dve, link, k.x, k.xn, k.sem("c_xn"))
            dve.wait_ge(k.sem("c_xnT_ps"), 1)
            vec.tensor_copy(k.xnT[:, :, :].rearrange("p c q -> p (c q)"), k.ps[:, 2, :]).then_inc(k.sem("c_xnT"), 1)


MASKED = -float(2 ** 30)


def stage_cross1_prepare(k):
    nc = k.nc
    with nc.Block() as block:
        @block.sync
        def _(sp):
            sp.dma_start(k.mask_u8, k.i["mask_Bx1xSxS2_bf1"].rearrange("a b (t p) n -> p (a b t) n", p=P)).then_inc(k.sem("d_mask_in"), 16)
            store_q_parts(k, sp, 1)

        @block.gpsimd
        def _(pool):
            g = nc.gpsimd
            link = Order(pool, k.sem("pool_order"), k.pool_ordered).link
            link(g.memset(k.q_all[MAXROW:LOROW, :, :], 0.0))
            link(g.memset(k.v_st[:, :, :, :], 0.0))
            link(g.memset(k.v_st[:, :, :, DH], 1.0))

        @block.scalar
        def _(act):
            act.wait_ge(k.sem("d_mask_in"), 16)
            for q in range(QT):
                nc.scalar.activation(k.mask_bias[:, q, :], k.mask_u8[:, q, :], ACT.Copy, scale=-MASKED, bias=MASKED,
                                     accum_out=k.mask_sum[:, q:q + 1]).then_inc(k.sem("d_bias"), 1)

        @block.vector
        def _(dve):
            v = nc.vector
            link = Order(dve, k.sem("dve_order"), k.dve_ordered).link
            dve.wait_ge(k.sem("d_bias"), QT)
            link(v.tensor_scalar(k.any_keep[:, :], k.mask_sum[:, :], MASKED * (S2 - 0.5), 1.0 / np.sqrt(DH), ALU.is_gt, ALU.mult))
            v.tensor_reduce(k.masked_f[:, :], k.mask_sum[:, :], AX.X, ALU.add).then_inc(k.sem("d_masked_sum"), 1)
            dve.wait_ge(k.sem("d_total"), 1)
            v.tensor_scalar(k.masked_i[:, :], k.ps[0:1, 6, 0:1], 0.0, None, ALU.is_lt).then_inc(k.sem("d_masked"), 1)
            dve.wait_ge(k.sem("d_q"), 1)
            for q in range(QT):
                v.tensor_scalar(k.xn[:, q, :], k.ps[:, 3, q * D:(q + 1) * D], k.any_keep[:, q:q + 1], None, ALU.mult).then_inc(k.sem("d_q_rows"), 1)
            dve.wait_ge(k.sem("d_qT"), 1)
            link(v.tensor_copy(k.q_f[:, :, :].rearrange("p c q -> p (c q)"), k.ps[:, 4, :]))
            split_q(k, link).then_inc(k.sem("q_split"), 1)

        @block.tensor
        def _(pe):
            rows_linear(k, k.xnT, KT, k.w1_q, k.b1_qo[0:1, 0, :], 3, k.sem("d_q"))
            pe.wait_ge(k.sem("d_masked_sum"), 1)
            nc.tensor.matmul(k.ps[0:1, 6, 0:1], k.ones_sq[:, 0:1], k.masked_f[:, :], start=True, stop=True).then_inc(k.sem("d_total"), 1)
            pe.wait_ge(k.sem("d_q_rows"), QT)
            transpose_rows(k, k.xn, 4, k.sem("d_qT"))


def stage_cross1(k):
    nc = k.nc
    groups = 2 * GROUPS
    m_blocks = S2 // 512
    n_m = QT * m_blocks
    m_beside = [3, 3, 2, 2, 2, 2, 2, 0]
    assert sum(m_beside) == n_m
    probs = k.probs[:, :, :, :].rearrange("p b (g c) q -> p (b g) c q", c=GROUP_CH)
    s = {n: k.sem("d_" + n) for n in (
        "scores", "exp", "pv", "q_staged", "v_staged", "m_scores", "m_read", "m_ops", "m_parts",
        "m_turned", "m_rows", "acc_copied", "sel", "rec", "o_read")}
    k_in = [k.sem(f"d_k_in{j}") for j in range(4)]
    qm_in = [k.sem(f"d_qm_in{b}") for b in range(2)]

    def scores_bank(g):
        return k.ps[:, 2 * (g % 2):2 * (g % 2) + 2, :].rearrange("p b (c q) -> p (b c) q", q=S)

    def pairs_of_heads(eng, body):
        body(0, True, False)
        with eng.Fori(1, H // 2 - 1) as it:
            body(it, False, False)
        body(H // 2 - 1, False, True)

    with nc.Block() as block:
        @block.sync
        def _(sp):
            def load_q(h, b):
                sp.dma_start(k.q_m[0:MAXROW, b, :], k.q_all[0:MAXROW, h, :]).then_inc(qm_in[b], 16)

            for b in range(2):
                load_q(b, b)
                for j in (2 * b, 2 * b + 1):
                    load_k_unit(k, sp, k.kd1, b, j % 2, j, k_in[j])
            load_late_weights(k, sp)
            with sp.Fori(1, H // 2) as it:
                for b in range(2):
                    sp.wait_ge(s["m_read"], n_m * 2 * it + n_m * (b - 1))
                    load_q(2 * it + b, b)
                    for j in (2 * b, 2 * b + 1):
                        sp.wait_ge(s["scores"], 16 * it - 16 + 4 * (j + 1))
                        load_k_unit(k, sp, k.kd1, 2 * it + b, j % 2, j, k_in[j])

        @block.gpsimd
        def _(pool):
            g = nc.gpsimd

            def stage(h, b, fresh):
                if not fresh:
                    pool.wait_ge(s["scores"], groups * h - groups)
                g.tensor_copy(k.q_st[0:STACK, b, :], k.q_all[0:STACK, h, :]).then_inc(s["q_staged"], 1)
                if not fresh:
                    pool.wait_ge(s["pv"], groups * h - groups)
                g.tensor_copy(k.v_st[:, b, :, 0:DH], k.v_proj[:, :, bass.ds(h * DH, DH)]).then_inc(s["v_staged"], 1)

            stage(0, 0, True)
            stage(1, 1, True)
            with pool.Fori(1, H // 2) as it:
                stage(2 * it, 0, False)
                stage(2 * it + 1, 1, False)

        @block.scalar
        def _(act):
            def body(it, first, last):
                for b in range(2):
                    for g in range(groups):
                        n = 16 * it + 8 * b + g
                        act.wait_ge(s["scores"], n + 1)
                        if not (first and b == 0):
                            act.wait_ge(s["pv"], n - groups + 1)
                        nc.scalar.activation(probs[:, g], scores_bank(g), ACT.Exp).then_inc(s["exp"], 1)

            pairs_of_heads(act, body)

        @block.tensor
        def _(pe):
            t = nc.tensor

            def m_scores(it, b, idx, masked, first):
                h = 2 * it + b
                blk, q = divmod(idx, QT)
                half = blk // (m_blocks // 2)
                if idx == 0:
                    pe.wait_ge(qm_in[b], 16 * (it + 1))
                if idx % (n_m // 2) == 0:
                    pe.wait_ge(k_in[2 * b + half], 16 * K_LOADS * (it + 1))
                if not (first and b == 0 and idx < 2):
                    pe.wait_ge(s["m_read"], n_m * h + idx - 1)
                if idx == 0 and not (first and b == 0):
                    pe.wait_ge(s["m_rows"], h)
                o = k.ps[:, 6 + idx % 2, :]
                key0 = (blk % (m_blocks // 2)) * 512
                last = t.matmul(o, k.q_m[0:MAXROW, b, q * P:(q + 1) * P], k.k_st[0:MAXROW, 2 * b + half, key0:key0 + 512],
                                start=True, stop=not masked)
                if masked:
                    last = t.matmul(o, k.ident_bf[:, :], k.mask_bias[:, q, blk * 512:(blk + 1) * 512], start=False, stop=True)
                last.then_inc(s["m_scores"], 1)

            def m_turn(it, b):
                pe.wait_ge(s["m_parts"], 2 * it + b + 1)
                for q in range(QT):
                    last = t.matmul(k.ps[MAXROW:LOROW, 6, q * P:(q + 1) * P], k.m_parts[:, q, :], k.ident_bf[:, :],
                                    start=True, stop=True)
                last.then_inc(s["m_turned"], 1)

            def qk(it, b, g, masked, first):
                h, j = 2 * it + b, 2 * b + g // GROUPS
                n = groups * h + g
                if g == 0:
                    pe.wait_ge(s["m_rows"], h + 1)
                if g % GROUPS == 0:
                    pe.wait_ge(k_in[j], 16 * K_LOADS * (it + 1))
                if not (first and b == 0 and g < 2):
                    pe.wait_ge(s["exp"], n - 1)
                out = scores_bank(g)
                for c in range(GROUP_CH):
                    ch = GROUP_CH * (g % GROUPS) + c
                    last = t.matmul(out[:, c, :], k.k_st[0:STACK, j, ch * P:(ch + 1) * P], k.q_st[0:STACK, b, :],
                                    start=True, stop=not masked)
                    if masked:
                        ch = GROUP_CH * g + c
                        for q in range(QT):
                            last = t.matmul(out[:, c, q * P:(q + 1) * P], k.mask_bias[:, q, ch * P:(ch + 1) * P],
                                            k.ident_bf[:, :], start=False, stop=(q == QT - 1))
                last.then_inc(s["scores"], 1)

            def pv(it, b, g, first):
                h = 2 * it + b
                pe.wait_ge(s["exp"], groups * h + g + 1)
                if g == 0:
                    pe.wait_ge(s["v_staged"], h + 1)
                    if not first:
                        pe.wait_ge(s["o_read"], h - 1)
                for m in range(GROUP_CH):
                    last = t.matmul(k.ps[32 * m:32 * m + 32, 4 + b, 0:S], k.v_st[:, b, GROUP_CH * g + m, :], probs[:, g, m, :],
                                    start=(g == 0), stop=(g == groups - 1))
                last.then_inc(s["pv"], 1)

            def sel(h, b):
                pe.wait_ge(s["acc_copied"], h + 1)
                for q in range(QT):
                    last = t.matmul(k.ps[:, 4 + b, S + 32 * q:S + 32 * (q + 1)], k.acc_sb[:, b, q * P:(q + 1) * P],
                                    k.quad_sum[:, :], start=True, stop=True)
                last.then_inc(s["sel"], 1)

            def all_heads(masked):
                for idx in range(n_m):
                    m_scores(0, 0, idx, masked, True)
                m_turn(0, 0)

                def body(it, first, last):
                    for b in range(2):
                        nit, nb = (it, 1) if b == 0 else (it + 1, 0)
                        more = not (last and b == 1)
                        idx = 0
                        for g in range(groups):
                            qk(it, b, g, masked, first)
                            if g >= 1:
                                pv(it, b, g - 1, first)
                            if more:
                                for _ in range(m_beside[g]):
                                    m_scores(nit, nb, idx, masked, False)
                                    idx += 1
                            if g == 2 and not (first and b == 0):
                                sel(2 * it + b - 1, 1 - b)
                        pv(it, b, groups - 1, first)
                        if more:
                            m_turn(nit, nb)

                pairs_of_heads(pe, body)
                sel(H - 1, 1)

            masked = pe.value_load(k.masked_i[0:1, 0:1], min_val=0, max_val=1)
            with pe.If(masked):
                all_heads(True)
            with pe.Else():
                all_heads(False)

        @block.vector
        def _(dve):
            v = nc.vector

            def m_read(h, idx):
                blk, q = divmod(idx, QT)
                dve.wait_ge(s["m_scores"], n_m * h + idx + 1)
                v.tensor_reduce(k.m_blk[:, q, blk:blk + 1], k.ps[:, 6 + idx % 2, :], AX.X, ALU.max).then_inc(s["m_read"], 1)

            def m_parts(h):
                ops = 4 * h
                dve.wait_ge(s["m_read"], n_m * h + n_m)
                v.tensor_reduce(k.m_neg[:, :], k.m_blk[:, :, :], AX.X, ALU.max, negate=True).then_inc(s["m_ops"], 1)
                dve.wait_ge(s["m_ops"], ops + 1)
                v.tensor_copy(k.m_parts[:, :, 0], k.m_neg[:, :]).then_inc(s["m_ops"], 1)
                dve.wait_ge(s["m_ops"], ops + 2)
                v.tensor_tensor(k.m_res[:, 0, :], k.m_neg[:, :], k.m_parts[:, :, 0], ALU.subtract).then_inc(s["m_ops"], 1)
                dve.wait_ge(s["m_ops"], ops + 3)
                v.tensor_copy(k.m_parts[:, :, 1], k.m_res[:, 0, :]).then_inc(s["m_ops"], 1)
                dve.wait_ge(s["m_ops"], ops + 4)
                v.tensor_tensor(k.m_parts[:, :, 2], k.m_res[:, 0, :], k.m_parts[:, :, 1], ALU.subtract).then_inc(s["m_parts"], 1)

            def m_rows(h, b):
                dve.wait_ge(s["m_turned"], h + 1)
                dve.wait_ge(s["q_staged"], h + 1)
                v.tensor_copy(k.q_st[MAXROW:LOROW, b, :], k.ps[MAXROW:LOROW, 6, 0:S]).then_inc(s["m_rows"], 1)

            def copy_acc(h, b):
                dve.wait_ge(s["pv"], groups * h + groups)
                v.tensor_copy(k.acc_sb[:, b, :], k.ps[:, 4 + b, 0:S]).then_inc(s["acc_copied"], 1)

            def normalise(h, b):
                o = k.ps[:, 4 + b, S:S + 32 * QT].rearrange("p (q n) -> p q n", q=QT)
                dve.wait_ge(s["sel"], h + 1)
                v.reciprocal(k.rec[:, b, :], o[:, :, DH]).then_inc(s["rec"], 1)
                dve.wait_ge(s["rec"], h + 1)
                v.tensor_tensor(k.o_nat[:, :, bass.ds(h * DH, DH)], o[:, :, 0:DH],
                                k.rec[:, b, :].unsqueeze(2).to_broadcast([P, QT, DH]), ALU.mult).then_inc(s["o_read"], 1)

            for idx in range(n_m):
                m_read(0, idx)
            m_parts(0)
            m_rows(0, 0)

            def body(it, first, last):
                for b in range(2):
                    h = 2 * it + b
                    if not (last and b == 1):
                        for idx in range(m_beside[0]):
                            m_read(h + 1, idx)
                    if not (first and b == 0):
                        copy_acc(h - 1, 1 - b)
                    if not (last and b == 1):
                        for idx in range(m_beside[0], sum(m_beside[0:4])):
                            m_read(h + 1, idx)
                    if not (first and b == 0):
                        normalise(h - 1, 1 - b)
                    if not (last and b == 1):
                        for idx in range(sum(m_beside[0:4]), n_m):
                            m_read(h + 1, idx)
                        m_parts(h + 1)
                        m_rows(h + 1, 1 - b)

            pairs_of_heads(dve, body)
            copy_acc(H - 1, 1)
            normalise(H - 1, 1)


def load_late_weights(k, sp):
    i = k.i
    done = k.sem("e_w_in")
    for n, name in enumerate(("Wq", "Wk", "Wv")):
        sp.dma_start(k.e_w[:, n], i[f"L1_attn_{name}T"].rearrange("(t p) n -> p t n", p=P)).then_inc(done, 16)
    sp.dma_start(k.e_proj, i["L1_attn_proj"].rearrange("(t p) n -> p t n", p=P)).then_inc(done, 16)
    sp.dma_start(k.e_bqk[:, 0, :], i["L1_attn_bq_cols"]).then_inc(done, 16)
    sp.dma_start(k.e_bqk[:, 1, :], i["L1_attn_bk_cols"]).then_inc(done, 16)
    sp.dma_start(k.e_bv, i["L1_attn_bv_row"]).then_inc(done, 16)
    done = k.sem("f_w_in")
    sp.dma_start(k.f_wq, i["L1_ffn_WqT"].rearrange("(t p) n -> p t n", p=P)).then_inc(done, 16)
    sp.dma_start(k.f_wo, i["L1_ffn_WoT"].rearrange("(t p) n -> p t n", p=P)).then_inc(done, 16)
    for half in range(2):
        sp.dma_start(k.f_wkc[:, :, half * E_DH:(half + 1) * E_DH],
                     i["L1_ffn_WkcT"].rearrange("(t p) n -> p t n", p=P)).then_inc(done, 16)
    sp.dma_start(k.f_wvc, i["L1_ffn_WvcT"].rearrange("(t p) n -> p t n", p=P)).then_inc(done, 16)
    sp.dma_start(k.f_wr, i["L1_ffn_WrT"].rearrange("(t p) n -> p t n", p=P)).then_inc(done, 16)
    for n in range(2):
        sp.dma_start(k.f_g[:, n, :], i[f"L1_ffn_g{n + 1}_cols"]).then_inc(done, 16)
    sp.dma_start(k.f_be, i["L1_ffn_expert_bias"].unsqueeze(0)).then_inc(done, 16)


def rms_norm(k, dve, link, src, done):
    v = k.nc.vector
    for t in range(QT):
        link(v.bn_stats(k.ln_stats[:, t, :], src[:, t, :]))
        link(v.bn_aggr(k.ln_mv[:, t, :], k.ln_stats[:, t, :]))
    link(v.tensor_tensor(k.rs_t[:, 0:QT], k.ln_mv[:, :, 0], k.ln_mv[:, :, 0], ALU.mult))
    link(v.scalar_tensor_tensor(out=k.rs_v[:, 0:QT], in0=k.rs_t[:, 0:QT], scalar=1e-6, in1=k.ln_mv[:, :, 1],
                                op0=ALU.add, op1=ALU.add))
    rsqrt(k, link, QT)
    for t in range(QT):
        v.tensor_scalar(k.xn[:, t, :], src[:, t, :], k.rs_y[:, t:t + 1], None, ALU.mult).then_inc(done, 1)


def weigh_turned(k, dve, which, ready, done):
    dve.wait_ge(ready, 1)
    for c in range(KT):
        k.nc.vector.tensor_scalar(k.xnT[:, c, :], k.ps[:, 2, c * S:(c + 1) * S], k.f_g[:, which, c:c + 1], None,
                                  ALU.mult).then_inc(done, 1)


def stage_self1(k):
    nc, i = k.nc, k.i
    v, sc, t = nc.vector, nc.scalar, nc.tensor
    causal = Small(k, 2 * E_T, 2, True,
                   q_of=lambda h, q: k.e_qT[64 * (h % 2):64 * (h % 2) + 64, h // 2, q * P:(q + 1) * P],
                   k_of=lambda h, nk: k.e_kT[64 * (h % 2):64 * (h % 2) + 64, h // 2, 0:nk],
                   v_of=lambda h, c: k.e_v[:, c, h * E_DH:(h + 1) * E_DH],
                   out_of=lambda h, q, r: k.ps[64 * r:64 * r + 64, 4 + h // 4, (h % 4) * P + q * 64:(h % 4) * P + (q + 1) * 64],
                   interleave=2)
    latent = Small(k, F_H, 2, False,
                   q_of=lambda h, q: k.f_qT[64 * (h % 2):64 * (h % 2) + 64, h // 2, q * P:(q + 1) * P],
                   k_of=lambda h, nk: k.f_kT[64 * (h % 2):64 * (h % 2) + 64, 0:nk],
                   v_of=lambda h, c: k.f_v[:, c, :],
                   out_of=lambda h, q, r: k.ps[64 * (h % 2):64 * (h % 2) + 64, 4, (h // 2) * S + q * P:(h // 2) * S + (q + 1) * P])
    experts = [N_EXP] + list(range(N_EXP))
    jobs = [(w, n) for w in range(3) for n in range(4)]
    by_dve = [n for n, (w, m) in enumerate(jobs) if w == 0 or (w == 2 and m % 2 == 0)]
    by_act = [n for n in range(len(jobs)) if n not in by_dve]

    def wait_evacuated(pe, n):
        m = n - 4
        if m in by_dve:
            pe.wait_ge(k.sem("e_dve"), by_dve.index(m) + 1)
        else:
            pe.wait_ge(k.sem("e_act"), by_act.index(m) + 1)

    with nc.Block() as block:
        @block.sync
        def _(sp):
            for n, e in enumerate(experts):
                names = ("eW1T", "eW3T", "eW2T") if e < N_EXP else ("sW1T", "sW3T", "sW2T")
                for w, name in enumerate(names):
                    a = i["L1_ffn_" + name]
                    a = a[e] if e < N_EXP else a
                    sp.dma_start(k.f_exp[e][w], a.rearrange("(t p) n -> p t n", p=P)).then_inc(k.sem(f"f_exp_in{n}"), 16)
            sp.wait_ge(k.sem("f_x"), 2 * (N_EXP + 1))
            sp.dma_start(k.out.rearrange("a (t p) d -> p (a t) d", p=P), k.x[:, :, :]).then_inc(k.sem("out"), 16)
            sp.wait_ge(k.sem("out"), 16)

        @block.gpsimd
        def _(pool):
            g = nc.gpsimd
            link = Order(pool, k.sem("pool_order"), k.pool_ordered).link
            link(g.memset(k.causal[:, :], 0.0))
            link(g.affine_select(out=k.causal[:, :], in_=k.causal[:, :], compare_op=ALU.is_ge, fill=-1e30, base=0,
                                 pattern=[[-1, P]], channel_multiplier=1))
            link(g.memset(k.f_low[:, :, :], 1.0))
            link(g.affine_select(out=k.f_low[:, :, :], in_=k.f_low[:, :, :], compare_op=ALU.is_gt, fill=0.0, base=0,
                                 pattern=[[1, N_EXP], [-1, N_EXP]], channel_multiplier=0))
            link(g.memset(k.f_comb[:, :, :], 1.0))

        @block.tensor
        def _(pe):
            update_pe(k, pe, "d", k.oT, KT, k.w1_o, k.b1_qo[0:1, 1, :], True)
            pe.wait_ge(k.sem("d_xnT"), 1)
            pe.wait_ge(k.sem("e_w_in"), 16 * 7)
            for n, (w, m) in enumerate(jobs):
                if n >= 4:
                    wait_evacuated(pe, n)
                if w < 2:
                    for half in range(2):
                        tile = 2 * m + half
                        for c in range(KT):
                            last = t.matmul(k.ps[:, 4 + n % 4, half * S:(half + 1) * S], k.e_w[:, w, c, tile * P:(tile + 1) * P],
                                            k.xnT[:, c, :], start=(c == 0), stop=(c == KT - 1))
                else:
                    cols = slice((m % 2) * 512, (m % 2 + 1) * 512)
                    for c in range(KT):
                        t.matmul(k.ps[:, 4 + n % 4, :], k.xnT[:, c, (m // 2) * P:(m // 2 + 1) * P], k.e_w[:, w, c, cols],
                                 start=(c == 0), stop=False)
                    last = t.matmul(k.ps[:, 4 + n % 4, :], k.ones_row[0:1, 0:P], k.e_bv[0:1, cols], start=False, stop=True)
                last.then_inc(k.sem("e_job"), 1)
            pe.wait_ge(k.sem("e_dve"), len(by_dve))
            pe.wait_ge(k.sem("e_act"), len(by_act))
            pe.wait_ge(k.sem("pool_order"), k.pool_ordered[0] - 3)
            small_pe(k, pe, causal)
            pe.wait_ge(k.sem("e_oT"), 1)
            for q in range(QT):
                for c in range(E_T):
                    last = t.matmul(k.ps[:, 1, q * D:(q + 1) * D], k.e_oT[:, q * 8:(q + 1) * 8, :, c], k.e_proj[:, c, :],
                                    start=(c == 0), stop=(c == E_T - 1))
            last.then_inc(k.sem("e_y"), 1)
            pe.wait_ge(k.sem("f_xn"), QT)
            transpose_rows(k, k.xn, 2, k.sem("f_xnT_ps"))
            pe.wait_ge(k.sem("f_xnT"), KT)
            pe.wait_ge(k.sem("f_w_in"), 16 * 9)
            for m in range(KT):
                for c in range(KT):
                    t.matmul(k.ps[:, 3, m * S:(m + 1) * S], k.f_wq[:, c, m * P:(m + 1) * P], k.xnT[:, c, :],
                             start=(c == 0), stop=(c == KT - 1))
            for c in range(KT):
                t.matmul(k.ps[:, 5, 0:S], k.f_wkc[:, c, :], k.xnT[:, c, :], start=(c == 0), stop=(c == KT - 1))
            for m in range(KT):
                for c in range(KT):
                    last = t.matmul(k.ps[:, 6, m * E_DH:(m + 1) * E_DH], k.xnT[:, c, m * P:(m + 1) * P], k.f_wvc[:, c, :],
                                    start=(c == 0), stop=(c == KT - 1))
            last.then_inc(k.sem("f_proj"), 1)
            pe.wait_ge(k.sem("f_qkv"), 3)
            small_pe(k, pe, latent)
            pe.wait_ge(k.sem("f_oT"), 1)
            rows_linear(k, k.oT, KT, k.f_wo, None, 1, k.sem("f_y"))
            pe.wait_ge(k.sem("g_xn"), QT)
            transpose_rows(k, k.xn, 2, k.sem("g_xnT_ps"))
            pe.wait_ge(k.sem("g_xnT"), KT)
            for q in range(QT):
                o = k.ps[:, 7, q * N_EXP:(q + 1) * N_EXP]
                for c in range(KT):
                    t.matmul(o, k.xnT[:, c, q * P:(q + 1) * P], k.f_wr[:, c, :], start=(c == 0), stop=False)
                last = t.matmul(o, k.ones_row[0:1, 0:P], k.f_be, start=False, stop=True)
            last.then_inc(k.sem("g_logits"), 1)

            def hidden(n):
                e = experts[n]
                pe.wait_ge(k.sem(f"f_exp_in{n}"), 48)
                if n >= 2:
                    pe.wait_ge(k.sem("g_h"), n - 1)
                for w in range(2):
                    for m in range(KT):
                        for c in range(KT):
                            last = t.matmul(k.ps[:, 2 * w + n % 2, m * S:(m + 1) * S], k.f_exp[e][w][:, c, m * P:(m + 1) * P],
                                            k.xnT[:, c, :], start=(c == 0), stop=(c == KT - 1))
                last.then_inc(k.sem("g_hidden"), 1)

            def down(n):
                pe.wait_ge(k.sem("g_h"), n + 1)
                if n >= 2:
                    pe.wait_ge(k.sem("f_x"), 2 * (n - 1))
                rows_linear(k, k.f_hT[:, n % 2], KT, k.f_exp[experts[n]][2], None, 4 + n % 2, k.sem("g_rows"))

            hidden(0)
            for n in range(N_EXP + 1):
                if n < N_EXP:
                    hidden(n + 1)
                down(n)

        @block.scalar
        def _(act):
            for n in by_act:
                w, m = jobs[n]
                act.wait_ge(k.sem("e_job"), n + 1)
                if w == 1:
                    for half in range(2):
                        ins = sc.activation(k.e_kT[:, 2 * m + half, :], k.ps[:, 4 + n % 4, half * S:(half + 1) * S], ACT.Identity,
                                            bias=k.e_bqk[:, 1, 2 * m + half:2 * m + half + 1])
                else:
                    ins = sc.activation(k.e_v[:, m // 2, (m % 2) * 512:(m % 2 + 1) * 512], k.ps[:, 4 + n % 4, :], ACT.Copy,
                                        scale=1.0 / np.sqrt(E_DH))
                ins.then_inc(k.sem("e_act"), 1)
            small_act(k, act, causal)
            act.wait_ge(k.sem("f_proj"), 1)
            sc.activation(k.f_kT, k.ps[:, 5, 0:S], ACT.Copy).then_inc(k.sem("f_qkv"), 1)
            sc.activation(k.f_v, k.ps[:, 6, 0:2 * E_DH].rearrange("p (t n) -> p t n", t=KT), ACT.Copy).then_inc(k.sem("f_qkv"), 1)
            small_act(k, act, latent)

            def gate(n):
                act.wait_ge(k.sem("g_hidden"), n + 1)
                if n >= 2:
                    act.wait_ge(k.sem("g_h"), n - 1)
                sc.activation(k.f_tanh[:, n % 2, :], k.ps[:, n % 2, :], ACT.Tanh, scale=0.5).then_inc(k.sem("g_tanh"), 1)

            act.wait_ge(k.sem("g_lg"), 1)
            sc.activation(k.f_rw[:, :, :], k.f_lg[:, :, :], ACT.Exp).then_inc(k.sem("g_rexp"), 1)
            gate(0)
            act.wait_ge(k.sem("g_diff"), 1)
            sc.activation(k.f_w[:, 1, :], k.f_w[:, 0, :], ACT.Exp).then_inc(k.sem("g_wexp"), 1)
            for n in range(1, N_EXP + 1):
                gate(n)

        @block.vector
        def _(dve):
            link = Order(dve, k.sem("dve_order"), k.dve_ordered).link
            update_dve(k, dve, link, "d", True)
            dve.wait_ge(k.sem("e_w_in"), 16 * 7)
            for n in by_dve:
                w, m = jobs[n]
                dve.wait_ge(k.sem("e_job"), n + 1)
                if w == 0:
                    for half in range(2):
                        ins = v.tensor_scalar(k.e_qT[:, 2 * m + half, :], k.ps[:, 4 + n % 4, half * S:(half + 1) * S],
                                              k.e_bqk[:, 0, 2 * m + half:2 * m + half + 1], 1.0 / np.sqrt(E_DH), ALU.add, ALU.mult)
                else:
                    ins = v.tensor_scalar(k.e_v[:, m // 2, (m % 2) * 512:(m % 2 + 1) * 512], k.ps[:, 4 + n % 4, :],
                                          1.0 / np.sqrt(E_DH), None, ALU.mult)
                ins.then_inc(k.sem("e_dve"), 1)
            small_dve(k, dve, causal)
            dve.wait_ge(k.sem("small_out"), causal.base + len(causal.pairs))
            v.tensor_copy(k.e_oT.rearrange("p (b g) i c -> p b (g i c)", b=4), k.ps[:, 4:8, :]).then_inc(k.sem("e_oT"), 1)
            xf = k.x[:, :, :].rearrange("p t d -> p (t d)")
            dve.wait_ge(k.sem("e_y"), 1)
            link(v.tensor_tensor(xf, xf, k.ps[:, 1, :], ALU.add))
            layer_norm(k, dve, link, k.x, k.x_ffn, k.sem("f_x0"))
            dve.wait_ge(k.sem("f_x0"), QT)
            rms_norm(k, dve, link, k.x_ffn, k.sem("f_xn"))
            dve.wait_ge(k.sem("f_w_in"), 16 * 9)
            weigh_turned(k, dve, 0, k.sem("f_xnT_ps"), k.sem("f_xnT"))
            dve.wait_ge(k.sem("f_proj"), 1)
            v.tensor_scalar(k.f_qT.rearrange("p t q -> p (t q)"), k.ps[:, 3, :], 1.0 / np.sqrt(E_DH), None, ALU.mult).then_inc(k.sem("f_qkv"), 1)
            small_dve(k, dve, latent)
            dve.wait_ge(k.sem("small_out"), latent.base + len(latent.pairs))
            v.tensor_copy(k.oT[:, :, :].rearrange("p c q -> p (c q)"), k.ps[:, 4, :]).then_inc(k.sem("f_oT"), 1)
            dve.wait_ge(k.sem("f_y"), 1)
            x_ffn = k.x_ffn[:, :, :].rearrange("p t d -> p (t d)")
            link(v.tensor_tensor(x_ffn, x_ffn, k.ps[:, 1, :], ALU.add))
            rms_norm(k, dve, link, k.x_ffn, k.sem("g_xn"))
            link(v.tensor_tensor(xf, xf, x_ffn, ALU.add))
            weigh_turned(k, dve, 1, k.sem("g_xnT_ps"), k.sem("g_xnT"))
            dve.wait_ge(k.sem("g_logits"), 1)
            link(v.tensor_copy(k.f_lg[:, :, :], k.ps[:, 7, 0:QT * N_EXP].rearrange("p (q e) -> p q e", q=QT)))
            link(v.tensor_reduce(k.f_w[:, 3, :], k.f_lg[:, :, :], AX.X, ALU.max))
            of_row = lambda a: a.unsqueeze(2).to_broadcast([P, QT, N_EXP])
            v.tensor_tensor(k.f_lg[:, :, :], k.f_lg[:, :, :], of_row(k.f_w[:, 3, :]), ALU.subtract).then_inc(k.sem("g_lg"), 1)
            dve.wait_ge(k.sem("g_rexp"), 1)
            link(v.tensor_reduce(k.f_w[:, 3, :], k.f_rw[:, :, :], AX.X, ALU.add))
            link(v.reciprocal(k.f_w[:, 3, :], k.f_w[:, 3, :]))
            link(v.tensor_tensor(k.f_rw[:, :, :], k.f_rw[:, :, :], of_row(k.f_w[:, 3, :]), ALU.mult))
            for q in range(QT):
                others = k.f_rw[:, q, :].unsqueeze(1).to_broadcast([P, N_EXP, N_EXP])
                own = k.f_rw[:, q, :].unsqueeze(2).to_broadcast([P, N_EXP, N_EXP])
                link(v.tensor_tensor(k.f_gt[:, q], others, own, ALU.is_gt))
                link(v.tensor_tensor(k.f_eq[:, q], others, own, ALU.is_equal))
            dve.wait_ge(k.sem("pool_order"), k.pool_ordered[0])
            link(v.tensor_tensor(k.f_eq[:, :, :, :], k.f_eq[:, :, :, :], k.f_low[:, :, :].unsqueeze(1).to_broadcast([P, QT, N_EXP, N_EXP]), ALU.mult))
            link(v.tensor_tensor(k.f_gt[:, :, :, :], k.f_gt[:, :, :, :], k.f_eq[:, :, :, :], ALU.add))
            link(v.tensor_reduce(k.f_rank[:, :, :], k.f_gt[:, :, :, :], AX.X, ALU.add))
            for n in range(2):
                link(v.tensor_scalar(k.f_sel[:, n], k.f_rank[:, :, :], float(n), None, ALU.is_equal))
                link(v.tensor_tensor(k.f_pick[:, n], k.f_sel[:, n], k.f_rw[:, :, :], ALU.mult))
            link(v.tensor_reduce(k.f_p[:, :, :], k.f_pick[:, :, :, :], AX.X, ALU.add))
            v.tensor_tensor(k.f_w[:, 0, :], k.f_p[:, 1, :], k.f_p[:, 0, :], ALU.subtract).then_inc(k.sem("g_diff"), 1)

            def hidden(n):
                b = n % 2
                dve.wait_ge(k.sem("g_tanh"), n + 1)
                if n >= 2:
                    dve.wait_ge(k.sem("g_rows"), n - 1)
                link(v.scalar_tensor_tensor(out=k.f_gate[:, b, :], in0=k.f_tanh[:, b, :], scalar=1.0, in1=k.ps[:, b, :],
                                            op0=ALU.add, op1=ALU.mult))
                v.scalar_tensor_tensor(out=k.f_hT[:, b].rearrange("p t q -> p (t q)"), in0=k.f_gate[:, b, :], scalar=0.5,
                                       in1=k.ps[:, 2 + b, :], op0=ALU.mult, op1=ALU.mult).then_inc(k.sem("g_h"), 1)

            hidden(0)
            dve.wait_ge(k.sem("g_wexp"), 1)
            link(v.tensor_scalar(k.f_w[:, 2, :], k.f_w[:, 1, :], 1.0, None, ALU.add))
            link(v.reciprocal(k.f_w[:, 2, :], k.f_w[:, 2, :]))
            link(v.tensor_tensor(k.f_w[:, 3, :], k.f_w[:, 1, :], k.f_w[:, 2, :], ALU.mult))
            for n in range(2):
                link(v.tensor_tensor(k.f_sel[:, n], k.f_sel[:, n], of_row(k.f_w[:, 2 + n, :]), ALU.mult))
            link(v.tensor_tensor(k.f_comb[:, :, 0:N_EXP], k.f_sel[:, 0], k.f_sel[:, 1], ALU.add))
            for n in range(N_EXP + 1):
                if n < N_EXP:
                    hidden(n + 1)
                dve.wait_ge(k.sem("g_rows"), n + 1)
                if n >= 1:
                    dve.wait_ge(k.sem("f_x"), 2 * n)
                for q in range(QT):
                    v.scalar_tensor_tensor(out=k.x[:, q, :], in0=k.ps[:, 4 + n % 2, q * D:(q + 1) * D],
                                           scalar=k.f_comb[:, q, experts[n]:experts[n] + 1], in1=k.x[:, q, :],
                                           op0=ALU.mult, op1=ALU.add).then_inc(k.sem("f_x"), 1)


def program(nc, ins, out):
    with ExitStack() as ctx:
        k = Kern(nc, ctx, ins, out)
        allocate(k)
        stage_prepare(k)
        stage_cross0(k)
        stage_self0(k)
        stage_cross1_prepare(k)
        stage_cross1(k)
        stage_self1(k)


def _t(a):
    return np.ascontiguousarray(np.swapaxes(a, -1, -2))


def lay_out(inputs):
    a = {n: np.asarray(v) for n, v in inputs.items()}
    out = {n: a[n] for n in ("x", "ctx_1024", "L1_xattn_bk", "L1_xattn_bv")}
    out["L0_xattn_scale"] = a["L0_xattn_scale"].reshape(1, 1)
    out["L0_xattn_log_C"] = a["L0_xattn_log_C"].reshape(1, 1)
    out["mask_bk0_by_chunk"] = a["mask_Bx1xS2_bk0"].reshape(NCH, P).T
    out["ctxT"] = _t(a["ctx_1024"][0])
    for n in ("L0_attn_b_qkv", "L0_attn_b_proj", "L0_attn_qn_w", "L0_attn_kn_w", "L1_xattn_bq", "L1_xattn_bo",
              "mask_Bx1xSxS2_bf1"):
        out[n] = a[n]
    for n, c in (("bq", "cols"), ("bk", "cols"), ("bv", "row")):
        b = a["L1_attn_" + n].reshape(-1)
        out[f"L1_attn_{n}_{c}"] = b.reshape(E_T, P).T if c == "cols" else b[None]
    for n in ("Wq", "Wk", "Wv"):
        out[f"L1_attn_{n}T"] = _t(a["L1_attn_" + n].reshape(2 * E_T * E_DH, D))
    for n in ("g1", "g2"):
        out[f"L1_ffn_{n}_cols"] = a["L1_ffn_" + n].reshape(KT, P).T
    for n in ("Wq", "Wkc", "Wvc", "Wo", "Wr", "sW1", "sW2", "sW3", "eW1", "eW2", "eW3"):
        out[f"L1_ffn_{n}T"] = _t(a["L1_ffn_" + n])
    for n in ("L1_attn_proj", "L1_ffn_expert_bias"):
        out[n] = a[n]
    for n in ("L0_attn_w_qkv", "L0_attn_w_proj", "L0_ffn_weight", "L0_xattn_W_out", "L1_xattn_Wk", "L1_xattn_Wv", "L1_xattn_Wq", "L1_xattn_Wo"):
        out[n + "T"] = _t(a[n])
    return out


def kernel(**inputs):
    import concourse.bacc as bacc
    from concourse.bass_utils import run_bass_kernel_spmd

    nc = bacc.Bacc("TRN2", target_bir_lowering=False, num_devices=1)
    arrays, ins = {}, {}
    for name, a in lay_out(inputs).items():
        a = np.ascontiguousarray(a)
        arrays[name] = a
        ins[name] = nc.dram_tensor(name, a.shape, mybir.dt.from_np(a.dtype), kind="ExternalInput").ap()
    out = nc.dram_tensor("out", (1, S, D), F32, kind="ExternalOutput").ap()
    program(nc, ins, out)
    r = run_bass_kernel_spmd(nc, [arrays], core_ids=[0])
    return r.results[0]["out"]
```

```python
from contextlib import ExitStack

import numpy as np

import concourse.bass as bass
from concourse import mybir

F32 = mybir.dt.float32
BF16 = mybir.dt.bfloat16
I32 = mybir.dt.int32
U8 = mybir.dt.uint8
ALU = mybir.AluOpType
ACT = mybir.ActivationFunctionType
AX = mybir.AxisListType

P = 128
S = 256
D = 256
S2 = 4096
H = 16
DH = D // H
QT = S // P
KT = D // P
NCH = S2 // P
UNIT_CH = NCH // 2
UNIT_KEYS = UNIT_CH * P
GROUP_CH = 4
GROUPS = UNIT_CH // GROUP_CH
PARTS = 3
MAXROW = 96
LOROW = MAXROW + PARTS
STACK = LOROW + DH
KSPLIT = 1024
SPLITS = S2 // KSPLIT
CBLK = 512
E_T = 8
E_DH = 64
N_EXP = 8
F_H = 4
MASKED = -float(2 ** 30)
ROUND = 12582912.0
RSQRT_MAGIC = float(0x5F3759DF)


class Kern:

    def __init__(self, nc, ctx, ins, out):
        self.nc, self.ctx, self.i, self.out = nc, ctx, ins, out
        self.sems = {}
        self.dve_ordered = [0]
        self.pool_ordered = [0]
        self.small_pairs = 0

    def sb(self, name, shape, dt=F32):
        t = self.ctx.enter_context(self.nc.sbuf_tensor("sb_" + name, shape, dt))
        return t

    def sem(self, name):
        if name not in self.sems:
            self.sems[name] = self.ctx.enter_context(self.nc.semaphore(name))
        return self.sems[name]


class Order:

    def __init__(self, eng, sem, count):
        self.eng, self.sem, self.count = eng, sem, count

    def link(self, *several):
        for ins in several:
            self.count[0] += 1
            ins.then_inc(self.sem, 1)
        self.eng.wait_ge(self.sem, self.count[0])


def allocate(k):
    nc = k.nc
    k.kd0 = nc.dram_tensor("k_parts_l0", [H, PARTS * DH, S2], BF16, kind="Internal").ap()
    k.kd1 = nc.dram_tensor("k_parts_l1", [H, PARTS * DH, S2], BF16, kind="Internal").ap()
    k.qd = nc.dram_tensor("q_parts", [2, PARTS, D, S], BF16, kind="Internal").ap()

    k.ps = k.ctx.enter_context(nc.psum_tensor("ps", [P, 8, 512], F32))

    k.x = k.sb("x", [P, QT, D])
    k.ident = k.sb("ident", [P, P])
    k.ident_bf = k.sb("ident_bf", [P, P], BF16)
    k.quad_sum = k.sb("quad_sum", [P, 32])
    k.ones_row = k.sb("ones_row", [1, CBLK])
    k.ln_stats = k.sb("ln_stats", [P, QT, 6])
    k.ln_mv = k.sb("ln_mv", [P, QT, 2])
    k.rs_v = k.sb("rs_v", [P, 64])
    k.rs_y = k.sb("rs_y", [P, 64])
    k.rs_t = k.sb("rs_t", [P, 64])
    k.xn = k.sb("xn", [P, QT, D])
    k.xnT = k.sb("xnT", [P, KT, S])
    k.o_nat = k.sb("o_nat", [P, QT, D])
    k.oT = k.sb("oT", [P, KT, S])
    k.q_f = k.sb("q_f", [P, KT, S])
    k.q_r = k.sb("q_r", [P, KT, S])
    k.q_p = k.sb("q_p", [P, PARTS, KT, S], BF16)
    k.q_all = k.sb("q_all", [P, H, S], BF16)
    k.q_st = k.sb("q_st", [P, 2, S], BF16)
    k.k_st = k.sb("k_st", [P, 4, UNIT_KEYS], BF16)
    k.v_st = k.sb("v_st", [P, 2, NCH, 32])
    k.v_rows = k.sb("v_rows", [P, NCH, D])
    k.v_proj = k.sb("v_proj", [P, NCH, D])
    k.probs = k.sb("probs", [P, 2, UNIT_KEYS // P, S])
    k.acc_sb = k.sb("acc_sb", [P, 2, S])
    k.rec = k.sb("rec", [P, 2, QT])
    k.keep = k.sb("keep", [P, NCH])
    k.keep_u8 = k.sb("keep_u8", [P, NCH], U8)
    k.l0_scale = k.sb("l0_scale", [P, 1])
    k.l0_logc = k.sb("l0_logc", [P, 1])
    k.cap = k.sb("cap", [P, 1])
    k.neg_cap = k.sb("neg_cap", [P, 1])
    k.bkv1 = k.sb("bkv1", [1, 2, D])
    k.w1_q = k.sb("w1_q", [P, KT, D])
    k.w1_o = k.sb("w1_o", [P, KT, D])
    k.b1_qo = k.sb("b1_qo", [P, 2, D])
    k.any_keep = k.sb("any_keep", [P, QT])
    k.mask_sum = k.sb("mask_sum", [P, QT])
    k.masked_f = k.sb("masked_f", [P, 1])
    k.masked_i = k.sb("masked_i", [1, 1], I32)
    k.m_blk = k.sb("m_blk", [P, QT, S2 // 512])
    k.m_neg = k.sb("m_neg", [P, QT])
    k.m_res = k.sb("m_res", [P, 2, QT])
    k.m_parts = k.sb("m_parts", [P, QT, PARTS], BF16)
    k.q_m = k.sb("q_m", [P, 2, S], BF16)
    vf = k.v_rows[:, :, :].rearrange("p c d -> p (c d)")
    k.mask_bias = vf[:, 0:4096].bitcast(BF16).rearrange("p (t n) -> p t n", t=QT)
    k.mask_u8 = vf[:, 4096:6144].bitcast(U8).rearrange("p (t n) -> p t n", t=QT)
    k.early = k.sb("early", [P, 8192])
    k.bias_rows = k.sb("bias_rows", [P, 4 * D])
    at = [0]

    def carve(n):
        at[0] += n
        return k.early[:, at[0] - n:at[0]]

    k.w_out0, k.wk1, k.wv1, k.w_ffn0 = [carve(KT * D).rearrange("p (t n) -> p t n", t=KT) for _ in range(4)]
    k.w_qkv0 = carve(KT * 3 * D).rearrange("p (t n) -> p t n", t=KT)
    k.w_proj0 = carve(H // 4 * D).rearrange("p (t n) -> p t n", t=H // 4)
    k.ctx_blk = carve(KT * CBLK).rearrange("p (t n) -> p t n", t=KT)
    k.kd_r = carve(2 * CBLK).rearrange("p (t n) -> p t n", t=2)
    k.kd_bf = carve(PARTS * CBLK).bitcast(BF16).rearrange("p (b s n) -> p b s n", b=2, s=PARTS)
    k.b_qkv0, k.b_proj0 = k.bias_rows[:, 0:3 * D], k.bias_rows[:, 3 * D:4 * D]
    k.e_w = k.early[:, 0:6144].rearrange("p (s t n) -> p s t n", s=3, t=KT)
    k.e_proj = k.early[:, 6144:8192].rearrange("p (t n) -> p t n", t=E_T)
    k.e_bv = k.bias_rows[:, :]
    k.e_bqk = k.sb("e_bqk", [P, 2, E_T])
    k.causal = k.sb("causal", [P, P], BF16)
    k.f_comb = k.sb("f_comb", [P, QT, N_EXP + 1])
    k.f_lg = k.sb("f_lg", [P, QT, N_EXP])
    k.f_rw = k.sb("f_rw", [P, QT, N_EXP])
    k.f_gt = k.sb("f_gt", [P, QT, N_EXP, N_EXP])
    k.f_eq = k.sb("f_eq", [P, QT, N_EXP, N_EXP])
    k.f_low = k.sb("f_low", [P, N_EXP, N_EXP])
    k.f_rank = k.sb("f_rank", [P, QT, N_EXP])
    k.f_sel = k.sb("f_sel", [P, 2, QT, N_EXP])
    k.f_pick = k.sb("f_pick", [P, 2, QT, N_EXP])
    k.f_p = k.sb("f_p", [P, 2, QT])
    k.f_w = k.sb("f_w", [P, 4, QT])
    k.head_mask = k.sb("head_mask", [P, P // DH])
    k.ones_sq = k.sb("ones_sq", [P, P])
    k.w_qkn = k.sb("w_qkn", [P, 2, DH])
    k.nmax = k.sb("nmax", [P, 2 * H])
    k.sums = k.sb("sums", [P, 2 * H])
    k.inv = k.sb("inv", [P, 2 * H])
    k.w_tern = k.sb("w_tern", [P, KT, D], BF16)
    k.w_sum = k.sb("w_sum", [P, 1])
    k.w_scale = k.sb("w_scale", [P, 1])
    k.w_inv = k.sb("w_inv", [P, 1])
    k.a_scale = k.sb("a_scale", [P, QT])
    k.a_inv = k.sb("a_inv", [P, QT])
    k.a_q = k.sb("a_q", [P, QT, D], BF16)
    k.a_qT = k.sb("a_qT", [P, KT, S], BF16)
    flat = lambda t, dims: t.rearrange(f"p {dims} -> p ({dims})")
    pf = flat(k.probs[:, :, :, :], "b c q")
    k.q_mask = pf[:, 0:H * S].rearrange("p (h q) -> p h q", q=S)
    k.qk = pf[:, 4096:5120].rearrange("p (t n) -> p t n", t=QT)
    k.qk_sq = pf[:, 5120:6144].rearrange("p (t n) -> p t n", t=QT)
    k.kT_self = pf[:, 6144:6656].rearrange("p (t n) -> p t n", t=KT)
    k.v_self = pf[:, 6656:7680].rearrange("p (t h n) -> p t h n", t=KT, h=H)
    qa = flat(k.q_all[:, :, :], "h q").bitcast(F32)
    k.sp_rows = qa[:, 0:1024].rearrange("p (b e n) -> p b e n", b=2, e=2)
    k.sp_T = qa[:, 1024:2048].rearrange("p (b n) -> p b n", b=2)
    k.e_qT = pf[:, 0:2048].rearrange("p (t q) -> p t q", t=E_T)
    k.e_kM = k.k_st[:, :, :].rearrange("p s n -> p (s n)").bitcast(F32).rearrange("p (h q) -> p h q", q=S)
    k.e_v = pf[:, 4096:6144].rearrange("p (t n) -> p t n", t=KT)
    k.e_oT = pf[:, 6144:8192].rearrange("p (h i c) -> p h i c", h=2 * E_T, c=E_T)
    k.x_ffn = k.o_nat
    k.f_qT = pf[:, 0:512].rearrange("p (t q) -> p t q", t=KT)
    k.f_v = pf[:, 768:896].rearrange("p (t n) -> p t n", t=KT)
    k.f_tanh = pf[:, 1024:2048].rearrange("p (b n) -> p b n", b=2)
    k.f_gate = pf[:, 2048:3072].rearrange("p (b n) -> p b n", b=2)
    k.f_hT = pf[:, 3072:4096].rearrange("p (b t q) -> p b t q", b=2, t=KT)
    fs = vf[:, 6144:8192]
    k.f_wq = fs[:, 0:512].rearrange("p (t n) -> p t n", t=KT)
    k.f_wo = fs[:, 512:1024].rearrange("p (t n) -> p t n", t=KT)
    k.f_wkc = fs[:, 1024:1280].rearrange("p (t n) -> p t n", t=KT)
    k.f_wvc = fs[:, 1280:1408].rearrange("p (t n) -> p t n", t=KT)
    k.f_wr = fs[:, 1408:1424].rearrange("p (t n) -> p t n", t=KT)
    k.f_g = fs[:, 1424:1428].rearrange("p (s t) -> p s t", s=2)
    k.f_be = fs[0:1, 1428:1436]
    vp = k.v_proj[:, :, :].rearrange("p c d -> p (c d)")
    place = [vp[:, n * 512:(n + 1) * 512] for n in range(16)] + [vf[:, n * 512:(n + 1) * 512] for n in range(11)]
    k.f_exp = [[place[3 * e + w].rearrange("p (t n) -> p t n", t=KT) for w in range(3)] for e in range(N_EXP + 1)]
    k.oT_pad = flat(k.v_st[:, :, :, :], "b c n")[:, 0:1024].rearrange("p (g q) -> p g q", g=4)


def layer_norm(k, dve, link, src, dst, done):
    v = k.nc.vector
    link(*[v.bn_stats(k.ln_stats[:, t, :], src[:, t, :]) for t in range(QT)])
    link(*[v.bn_aggr(k.ln_mv[:, t, :], k.ln_stats[:, t, :]) for t in range(QT)])
    link(v.tensor_scalar(k.rs_v[:, 0:QT], k.ln_mv[:, :, 1], 1e-5, None, ALU.add))
    rsqrt(k, link, QT)
    for t in range(QT):
        v.tensor_scalar(dst[:, t, :], src[:, t, :], k.ln_mv[:, t, 0:1], k.rs_y[:, t:t + 1],
                        ALU.subtract, ALU.mult).then_inc(done, 1)


def rsqrt(k, link, n):
    v, y, t = k.rs_v[:, 0:n], k.rs_y[:, 0:n], k.rs_t[:, 0:n]
    vec = k.nc.vector
    link(vec.tensor_scalar(y.bitcast(I32), v.bitcast(I32), -0.5, RSQRT_MAGIC, ALU.mult, ALU.add))
    for _ in range(3):
        link(vec.tensor_tensor(t, y, y, ALU.mult))
        link(vec.scalar_tensor_tensor(out=t, in0=t, scalar=-0.5, in1=v, op0=ALU.mult, op1=ALU.mult))
        link(vec.scalar_tensor_tensor(out=y, in0=t, scalar=1.5, in1=y, op0=ALU.add, op1=ALU.mult))


def transpose_rows(k, src, banks, done):
    for t in range(QT):
        for c in range(KT):
            last = k.nc.tensor.transpose(k.ps[:, banks, c * S + t * P:c * S + (t + 1) * P],
                                         src[:, t, c * P:(c + 1) * P], k.ident[:, :])
    last.then_inc(done, 1)


def split_q(k, link):
    v = k.nc.vector
    link(v.tensor_copy(k.q_p[:, 0], k.q_f[:, :, :]))
    link(v.tensor_tensor(k.q_r[:, :, :], k.q_f[:, :, :], k.q_p[:, 0], ALU.subtract))
    link(v.tensor_copy(k.q_p[:, 1], k.q_r[:, :, :]))
    return v.tensor_tensor(k.q_p[:, 2], k.q_r[:, :, :], k.q_p[:, 1], ALU.subtract)


def store_q_parts(k, sp, layer):
    split, stored = k.sem("q_split"), k.sem("q_stored")
    sp.wait_ge(split, layer + 1)
    for p in range(PARTS):
        sp.dma_start(k.qd[layer, p].rearrange("(t r) q -> r t q", t=KT), k.q_p[:, p]).then_inc(stored, 16)


Q_LOADS = 2 * PARTS + 1


def load_q_stack(k, sp, layer):
    stored, loaded = k.sem("q_stored"), k.sem("q_loaded")
    sp.wait_ge(stored, 16 * PARTS * (layer + 1))
    rows = [(r * DH, r // 2) for r in range(2 * PARTS)] + [(LOROW, 0)]
    for row, p in rows:
        sp.dma_start(k.q_all[row:row + DH, :, :],
                     k.qd[layer, p].rearrange("(h d) q -> d h q", d=DH)).then_inc(loaded, 16)
    assert len(rows) == Q_LOADS


def load_k_unit(k, sp, kd, h, half, slot, loaded):
    ks = slice(half * UNIT_KEYS, (half + 1) * UNIT_KEYS)
    for r in range(PARTS):
        sp.dma_start(k.k_st[2 * DH * r:2 * DH * (r + 1), slot, :], kd[h, 0:2 * DH, ks]).then_inc(loaded, 16)
    sp.dma_start(k.k_st[LOROW:STACK, slot, :], kd[h, 2 * DH:3 * DH, ks]).then_inc(loaded, 16)


K_LOADS = PARTS + 1


def store_k_parts(k, sp, n, parts):
    t, b = divmod(n, SPLITS)
    sp.wait_ge(k.sem("k0_split"), n + 1)
    for p in range(PARTS):
        sp.dma_start(k.kd0[t * 8:(t + 1) * 8, p * DH:(p + 1) * DH, b * KSPLIT:(b + 1) * KSPLIT],
                     parts[:, p, :]).then_inc(k.sem(f"k0_stored{n % 2}"), 16)


def load_ctx_rows(k, eng, half):
    cols = slice(half * D // 2, (half + 1) * D // 2)
    eng.dma_start(k.v_rows[:, :, cols], k.i["ctx_1024"].rearrange("a (c p) d -> p (a c) d", p=P)[:, :, cols]
                  ).then_inc(k.sem(f"ctx_in{half}"), 16)


def load_early_weights(k, sp):
    i, w2 = k.i, k.sem("w2_in")
    sp.dma_start(k.w_out0[:, :, :], i["L0_xattn_W_outT"].rearrange("(t p) n -> p t n", p=P)).then_inc(w2, 16)
    sp.dma_start(k.w_qkv0[:, :, :], i["L0_attn_w_qkvT"].rearrange("(t p) n -> p t n", p=P)).then_inc(w2, 16)
    sp.dma_start(k.b_qkv0[:, :], i["L0_attn_b_qkv"].unsqueeze(0).to_broadcast([P, 3 * D])).then_inc(w2, 16)
    sp.dma_start(k.b_proj0[:, :], i["L0_attn_b_proj"].unsqueeze(0).to_broadcast([P, D])).then_inc(w2, 16)
    sp.dma_start(k.w_qkn[:, 0, :], i["L0_attn_qn_w"].unsqueeze(0).to_broadcast([P, DH])).then_inc(w2, 16)
    sp.dma_start(k.w_qkn[:, 1, :], i["L0_attn_kn_w"].unsqueeze(0).to_broadcast([P, DH])).then_inc(w2, 16)
    sp.dma_start(k.w_ffn0[:, :, :], i["L0_ffn_weightT"].rearrange("(t p) n -> p t n", p=P)).then_inc(w2, 16)
    sp.dma_start(k.w1_q[:, :, :], i["L1_xattn_WqT"].rearrange("(t p) n -> p t n", p=P)).then_inc(w2, 16)
    sp.dma_start(k.w1_o[:, :, :], i["L1_xattn_WoT"].rearrange("(t p) n -> p t n", p=P)).then_inc(w2, 16)
    sp.dma_start(k.b1_qo[:, 0, :], i["L1_xattn_bq"].unsqueeze(0).to_broadcast([P, D])).then_inc(w2, 16)
    sp.dma_start(k.b1_qo[:, 1, :], i["L1_xattn_bo"].unsqueeze(0).to_broadcast([P, D])).then_inc(w2, 16)
    for m in range(4):
        sp.dma_start(k.w_proj0[32 * m:32 * m + DH, :, :],
                     i["L0_attn_w_projT"].rearrange("(g m d) n -> m d g n", m=4, d=DH)[m]).then_inc(w2, 16)


def stage_prepare(k):
    nc, i = k.nc, k.i
    n_blk = SPLITS
    blk = k.probs[:, 0].rearrange("p c q -> p (c q)").rearrange("p (b n) -> p b n", n=KSPLIT)
    res = k.probs[:, 1].rearrange("p c q -> p (c q)")[:, 0:2 * KSPLIT].rearrange("p (b n) -> p b n", n=KSPLIT)
    parts = k.v_proj[:, 0:24].rearrange("p c q -> p (c q)").bitcast(BF16).rearrange("p (b s n) -> p b s n", b=SPLITS, s=PARTS)

    with nc.Block() as block:
        @block.sync
        def _(sp):
            sp.dma_start(k.x[:, :, :], i["x"].rearrange("a (t p) d -> p (a t) d", p=P)).then_inc(k.sem("x_in"), 16)
            for n in range(n_blk):
                sp.dma_start(blk[:, n], i["ctxT"][0:P, n * KSPLIT:(n + 1) * KSPLIT]).then_inc(k.sem(f"ctxT_in{n}"), 16)
            store_q_parts(k, sp, 0)
            store_k_parts(k, sp, 0, parts[:, 0])
            load_q_stack(k, sp, 0)
            for n in range(1, n_blk):
                store_k_parts(k, sp, n, parts[:, n])
            sp.wait_ge(k.sem("q_loaded"), 16 * Q_LOADS)
            for b in range(2):
                sp.wait_ge(k.sem(f"k0_stored{b}"), 16 * PARTS * n_blk // 2)

        @block.gpsimd
        def _(pool):
            g = nc.gpsimd
            link = Order(pool, k.sem("pool_order"), k.pool_ordered).link
            link(g.memset(k.ident[:, :], 0.0))
            link(g.affine_select(out=k.ident[:, :], in_=k.ident[:, :], compare_op=ALU.not_equal, fill=1.0, base=0,
                                 pattern=[[-1, P]], channel_multiplier=1))
            link(g.memset(k.w_proj0[:, :, :], 0.0))
            link(g.memset(k.ones_row[:, :], 1.0))
            link(g.memset(k.ones_sq[:, :], 1.0))
            link(g.memset(k.v_st[:, :, :, :], 0.0))
            link(g.memset(k.k_st[MAXROW:LOROW, :, :], 1.0))
            link(g.memset(k.q_all[MAXROW:LOROW, :, :], 0.0))

        @block.scalar
        def _(act):
            a = nc.scalar
            one = k.sem("small_in")
            act.dma_start(k.l0_scale[:, :], i["L0_xattn_scale"].to_broadcast([P, 1])).then_inc(one, 16)
            act.dma_start(k.l0_logc[:, :], i["L0_xattn_log_C"].to_broadcast([P, 1])).then_inc(one, 16)
            act.dma_start(k.keep_u8[:, :], i["mask_bk0_by_chunk"]).then_inc(one, 16)
            load_ctx_rows(k, act, 0)
            act.dma_start(k.wk1[:, :, :], i["L1_xattn_WkT"].rearrange("(t p) n -> p t n", p=P)).then_inc(k.sem("w1_in"), 16)
            act.dma_start(k.wv1[:, :, :], i["L1_xattn_WvT"].rearrange("(t p) n -> p t n", p=P)).then_inc(k.sem("w1_in"), 16)
            act.dma_start(k.bkv1[0:1, 0, :], i["L1_xattn_bk"].unsqueeze(0)).then_inc(k.sem("w1_in"), 16)
            act.dma_start(k.bkv1[0:1, 1, :], i["L1_xattn_bv"].unsqueeze(0)).then_inc(k.sem("w1_in"), 16)
            act.wait_ge(one, 48)
            a.activation(k.cap[:, :], k.l0_logc[:, :], ACT.Exp).then_inc(k.sem("cap"), 1)
            act.wait_ge(k.sem("cap"), 1)
            a.activation(k.neg_cap[:, :], k.cap[:, :], ACT.Copy, scale=-1.0).then_inc(k.sem("cap"), 1)
            for n in range(n_blk + 1):
                if n < n_blk:
                    act.wait_ge(k.sem(f"ctxT_in{n}"), 16)
                    a.activation(parts[:, n, 0, :], blk[:, n], ACT.Copy).then_inc(k.sem("k0_hi"), 1)
                if n >= 1:
                    act.wait_ge(k.sem("k0_res"), n)
                    a.activation(parts[:, n - 1, 1, :], res[:, (n - 1) % 2], ACT.Copy).then_inc(k.sem("k0_mid"), 1)

        @block.vector
        def _(dve):
            v = nc.vector
            link = Order(dve, k.sem("dve_order"), k.dve_ordered).link
            dve.wait_ge(k.sem("x_in"), 16)
            layer_norm(k, dve, link, k.x, k.xn, k.sem("xn0"))
            dve.wait_ge(k.sem("xnT_ps"), 1)
            dve.wait_ge(k.sem("small_in"), 48)
            link(v.tensor_scalar(k.q_f[:, :, :].rearrange("p c q -> p (c q)"), k.ps[:, 0, :], k.l0_scale[:, 0:1],
                                 1.0 / np.sqrt(DH), ALU.mult, ALU.mult))
            split_q(k, link).then_inc(k.sem("q_split"), 1)
            for n in range(n_blk + 1):
                if n < n_blk:
                    dve.wait_ge(k.sem("k0_hi"), n + 1)
                    if n >= 2:
                        dve.wait_ge(k.sem("k0_split"), n - 1)
                    v.tensor_tensor(res[:, n % 2], blk[:, n], parts[:, n, 0, :], ALU.subtract
                                    ).then_inc(k.sem("k0_res"), 1)
                if n >= 1:
                    dve.wait_ge(k.sem("k0_mid"), n)
                    v.tensor_tensor(parts[:, n - 1, 2, :], res[:, (n - 1) % 2], parts[:, n - 1, 1, :], ALU.subtract
                                    ).then_inc(k.sem("k0_split"), 1)
            dve.wait_ge(k.sem("pool_order"), 2)
            link(v.tensor_copy(k.ident_bf[:, :], k.ident[:, :]))
            link(v.tensor_reduce(k.quad_sum[:, :], k.ident[:, :].rearrange("p (g j) -> p j g", g=4), AX.X, ALU.add))
            link(v.tensor_reduce(k.head_mask[:, :], k.ident[:, :].rearrange("p (j d) -> p j d", d=DH), AX.X, ALU.add))
            link(v.tensor_scalar(k.keep[:, :], k.keep_u8[:, :], -1.0, 1.0, ALU.mult, ALU.add))
            dve.wait_ge(k.sem("pool_order"), 6)
            for b in range(2):
                link(v.tensor_copy(k.v_st[:, b, :, DH], k.keep[:, :]))

        @block.tensor
        def _(pe):
            pe.wait_ge(k.sem("pool_order"), 2)
            pe.wait_ge(k.sem("xn0"), QT)
            transpose_rows(k, k.xn, 0, k.sem("xnT_ps"))


def stage_cross0(k):
    nc, i = k.nc, k.i
    probs = k.probs[:, :, :, :]
    s = {n: k.sem("a_" + n) for n in (
        "scores", "tanh", "exp", "pv", "staged", "acc_copied", "sel", "o_read", "rec", "blk_in",
        "proj", "v_copied", "kd_ops", "kd_split")}
    k_in = [k.sem(f"a_k_in{j}") for j in range(4)]
    kd_out = [k.sem(f"a_kd_out{j}") for j in range(2)]

    late = k.v_proj[:, 8:NCH].rearrange("p c q -> p (c q)")
    late_parts = late[:, 0:PARTS * KSPLIT].bitcast(BF16).rearrange("p (b s n) -> p b s n", b=2, s=PARTS)
    late_blk = late[:, PARTS * KSPLIT:2 * PARTS * KSPLIT].rearrange("p (b n) -> p b n", n=KSPLIT)

    def scores_bank(g):
        return k.ps[:, 2 * (g % 2):2 * (g % 2) + 2, :].rearrange("p b (c q) -> p (b c) q", q=S)

    with nc.Block() as block:
        @block.sync
        def _(sp):
            ctx_blocks = i["ctxT"].rearrange("(t p) n -> p t n", p=P)

            def body(it, more):
                for j in range(4):
                    if more:
                        sp.wait_ge(s["scores"], it * 16 + 4 * (j + 1))
                        load_k_unit(k, sp, k.kd0, 2 * it + 2 + j // 2, j % 2, j, k_in[j])
                    if j < 2:
                        sp.wait_ge(s["kd_split"], 2 * it + j + 1)
                        for p in (1, 2, 0):
                            sp.dma_start(k.kd1[8 * j:8 * j + 8, p * DH:(p + 1) * DH, bass.ds(sp.snap(it * CBLK), CBLK)],
                                         k.kd_bf[:, j, p, :]).then_inc(kd_out[j], 16)
                if more:
                    sp.wait_ge(s["proj"], 4 * it + 4)
                    sp.dma_start(k.ctx_blk[:, :, :], ctx_blocks[:, :, bass.ds(sp.snap(it * CBLK + CBLK), CBLK)]
                                 ).then_inc(s["blk_in"], 16)

            def load_split(n):
                sp.dma_start(late_blk[:, n % 3], i["ctxT"][P:2 * P, n * KSPLIT:(n + 1) * KSPLIT]).then_inc(k.sem(f"ctxT_in{n}"), 16)

            for j in range(4):
                load_k_unit(k, sp, k.kd0, j // 2, j % 2, j, k_in[j])
            sp.dma_start(k.ctx_blk[:, :, :], ctx_blocks[:, :, 0:CBLK]).then_inc(s["blk_in"], 16)
            for n in range(3):
                load_split(n)
            load_ctx_rows(k, sp, 1)
            for n in range(2):
                store_k_parts(k, sp, SPLITS + n, late_parts[:, n])
            load_split(3)
            load_early_weights(k, sp)
            body(0, True)
            for n in range(2, SPLITS):
                store_k_parts(k, sp, SPLITS + n, late_parts[:, n % 2])
            for b in range(2):
                sp.wait_ge(k.sem(f"k0_stored{b}"), 16 * PARTS * SPLITS)
            with sp.Fori(1, H // 2 - 1) as it:
                body(it, True)
            body(H // 2 - 1, False)
            for j in range(2):
                sp.wait_ge(kd_out[j], 16 * PARTS * (H // 2))
            sp.wait_ge(k.sem("w2_in"), 16 * 15)

        @block.gpsimd
        def _(pool):
            g = nc.gpsimd

            def stage(h, b, fresh):
                if not fresh:
                    pool.wait_ge(s["pv"], 2 * h - 2)
                g.tensor_tensor(k.v_st[:, b, :, 0:DH], k.v_rows[:, :, bass.ds(h * DH, DH)],
                                k.keep[:, :].unsqueeze(2).to_broadcast([P, NCH, DH]), ALU.mult).then_inc(s["staged"], 1)
                g.tensor_copy(k.q_st[0:STACK, b, :], k.q_all[0:STACK, h, :]).then_inc(s["staged"], 1)

            pool.wait_ge(k.sem("ctx_in0"), 16)
            stage(0, 0, True)
            stage(1, 1, True)
            pool.wait_ge(k.sem("ctx_in1"), 16)
            with pool.Fori(1, H // 2) as it:
                stage(2 * it, 0, False)
                stage(2 * it + 1, 1, False)

        @block.scalar
        def _(act):
            a = nc.scalar

            def body(it, first):
                for j in range(4):
                    u = 4 * it + j
                    for g in range(GROUPS):
                        act.wait_ge(s["scores"], 4 * u + g + 1)
                        if g == 0 and not (first and j < 2):
                            act.wait_ge(s["pv"], u - 1)
                        a.activation(probs[:, j % 2, 4 * g:4 * g + 4, :], scores_bank(g), ACT.Tanh).then_inc(s["tanh"], 1)
                    act.wait_ge(s["tanh"], 4 * u + 4)
                    a.activation(probs[:, j % 2], probs[:, j % 2], ACT.Exp, bias=k.neg_cap[:, 0:1], scale=k.cap[:, 0:1]
                                 ).then_inc(s["exp"], 1)

            body(0, True)
            with act.Fori(1, H // 2) as it:
                body(it, False)

        @block.tensor
        def _(pe):
            t = nc.tensor

            def qk(it, j, g, first):
                u = 4 * it + j
                if g == 0:
                    pe.wait_ge(k_in[j], 16 * K_LOADS * (it + 1))
                    if j % 2 == 0:
                        pe.wait_ge(s["staged"], u + 2)
                if not (first and j == 0 and g < 2):
                    pe.wait_ge(s["tanh"], 4 * u + g - 1)
                out = scores_bank(g)
                for c in range(GROUP_CH):
                    n = GROUP_CH * g + c
                    last = t.matmul(out[:, c, :], k.k_st[0:STACK, j, n * P:(n + 1) * P], k.q_st[0:STACK, j // 2, :],
                                    start=True, stop=True)
                last.then_inc(s["scores"], 1)

            def pv(it, j, c, first):
                b = j // 2
                if c == 0:
                    pe.wait_ge(s["exp"], 4 * it + j + 1)
                    if j % 2 == 0 and not first:
                        pe.wait_ge(s["o_read"], 2 * it + b - 1)
                for m in range(4):
                    ch = 4 * c + m
                    last = t.matmul(k.ps[32 * m:32 * m + 32, 4 + b, 0:S], k.v_st[:, b, (j % 2) * UNIT_CH + ch, :],
                                    probs[:, j % 2, ch, :], start=(j % 2 == 0 and c == 0), stop=(j % 2 == 1 and c == 3))
                if c == 3:
                    last.then_inc(s["pv"], 1)

            def sel(h, b):
                pe.wait_ge(s["acc_copied"], h + 1)
                for q in range(QT):
                    last = t.matmul(k.ps[:, 4 + b, S + 32 * q:S + 32 * (q + 1)], k.acc_sb[:, b, q * P:(q + 1) * P],
                                    k.quad_sum[:, :], start=True, stop=True)
                last.then_inc(s["sel"], 1)

            def project(it, j, first):
                if j == 0:
                    pe.wait_ge(s["blk_in"], 16 * (it + 1))
                if j >= 2:
                    pe.wait_ge(s["kd_split"], 2 * it + j - 1)
                elif not first:
                    pe.wait_ge(s["v_copied"], 2 * it + j - 1)
                bank = 6 + j % 2
                if j < 2:
                    o = k.ps[:, bank, :]
                    for c in range(KT):
                        t.matmul(o, k.wk1[:, c, j * P:(j + 1) * P], k.ctx_blk[:, c, :], start=(c == 0), stop=False)
                    last = t.matmul(o, k.bkv1[0:1, 0, j * P:(j + 1) * P], k.ones_row[0:1, 0:CBLK], start=False, stop=True)
                else:
                    for m in range(2):
                        ch = 2 * (j - 2) + m
                        o = k.ps[:, bank, m * D:(m + 1) * D]
                        for c in range(KT):
                            t.matmul(o, k.ctx_blk[:, c, ch * P:(ch + 1) * P], k.wv1[:, c, :], start=(c == 0), stop=False)
                        last = t.matmul(o, k.ones_row[0:1, 0:P], k.bkv1[0:1, 1, :], start=False, stop=True)
                last.then_inc(s["proj"], 1)

            def body(it, first):
                for j in range(4):
                    pit, pj = (it - 1, 3) if j == 0 else (it, j - 1)
                    for g, cs in enumerate([[], [0, 1], [2], [3]]):
                        qk(it, j, g, first)
                        for c in cs:
                            if not (first and j == 0):
                                pv(pit, pj, c, first)
                    if j == 1 and not first:
                        sel(2 * it - 1, 1)
                    if j == 3:
                        sel(2 * it, 0)
                    project(it, j, first)

            pe.wait_ge(k.sem("w1_in"), 64)
            body(0, True)
            with pe.Fori(1, H // 2) as it:
                body(it, False)
            for c in range(4):
                pv(H // 2 - 1, 3, c, False)
            sel(H - 1, 1)

        @block.vector
        def _(dve):
            v = nc.vector

            def split_k(it, j, first):
                n = 4 * it + j
                base = 6 * it + 3 * j
                src = k.ps[:, 6 + j, :]
                dve.wait_ge(s["proj"], n + 1)
                if not first:
                    dve.wait_ge(kd_out[j], 16 * PARTS * it)
                v.tensor_copy(k.kd_bf[:, j, 0, :], src).then_inc(s["kd_ops"], 1)
                dve.wait_ge(s["kd_ops"], base + 1)
                v.tensor_tensor(k.kd_r[:, j, :], src, k.kd_bf[:, j, 0, :], ALU.subtract).then_inc(s["kd_ops"], 1)
                dve.wait_ge(s["kd_ops"], base + 2)
                v.tensor_copy(k.kd_bf[:, j, 1, :], k.kd_r[:, j, :]).then_inc(s["kd_ops"], 1)
                dve.wait_ge(s["kd_ops"], base + 3)
                v.tensor_tensor(k.kd_bf[:, j, 2, :], k.kd_r[:, j, :], k.kd_bf[:, j, 1, :], ALU.subtract).then_inc(s["kd_split"], 1)

            def body(it, first):
                for j in range(4):
                    if j % 2 == 0 and not (first and j == 0):
                        copy_acc(2 * it - 1 + j // 2, (j // 2 + 1) % 2)
                    if j == 1 and not first:
                        normalise(2 * it - 1, 1)
                    if j == 3:
                        normalise(2 * it, 0)
                    if j < 2:
                        split_k(it, j, first)
                    else:
                        dve.wait_ge(s["proj"], 4 * it + j + 1)
                        v.tensor_copy(k.v_proj[:, bass.ds(4 * it + 2 * (j - 2), 2), :],
                                      k.ps[:, 6 + j % 2, :].rearrange("p (c d) -> p c d", d=D)).then_inc(s["v_copied"], 1)

            def copy_acc(h, b):
                dve.wait_ge(s["pv"], 2 * h + 2)
                v.tensor_copy(k.acc_sb[:, b, :], k.ps[:, 4 + b, 0:S]).then_inc(s["acc_copied"], 1)

            def normalise(h, b):
                o = k.ps[:, 4 + b, S:S + 32 * QT].rearrange("p (q n) -> p q n", q=QT)
                dve.wait_ge(s["sel"], h + 1)
                v.reciprocal(k.rec[:, b, :], o[:, :, DH]).then_inc(s["rec"], 1)
                dve.wait_ge(s["rec"], h + 1)
                v.tensor_tensor(k.o_nat[:, :, bass.ds(h * DH, DH)], o[:, :, 0:DH],
                                k.rec[:, b, :].unsqueeze(2).to_broadcast([P, QT, DH]), ALU.mult).then_inc(s["o_read"], 1)

            link = Order(dve, k.sem("dve_order"), k.dve_ordered).link

            def split_late(n):
                x, parts = late_blk[:, n % 3], late_parts[:, n % 2]
                dve.wait_ge(k.sem(f"ctxT_in{n}"), 32)
                if n >= 2:
                    dve.wait_ge(k.sem(f"k0_stored{n % 2}"), 16 * PARTS * (SPLITS // 2 + n // 2))
                link(v.tensor_copy(parts[:, 0], x))
                link(v.tensor_tensor(x, x, parts[:, 0], ALU.subtract))
                link(v.tensor_copy(parts[:, 1], x))
                v.tensor_tensor(parts[:, 2], x, parts[:, 1], ALU.subtract).then_inc(k.sem("k0_split"), 1)

            for n in range(2):
                split_late(n)
            body(0, True)
            for n in range(2, SPLITS):
                split_late(n)
            for b in range(2):
                dve.wait_ge(k.sem(f"k0_stored{b}"), 16 * PARTS * SPLITS)
            with dve.Fori(1, H // 2) as it:
                body(it, False)
            copy_acc(H - 1, 1)
            normalise(H - 1, 1)



def rows_linear(k, src, n_k, w, bias, bank, done):
    t = k.nc.tensor
    for q in range(QT):
        o = k.ps[:, bank, q * D:(q + 1) * D]
        for c in range(n_k):
            last = t.matmul(o, src[:, c, q * P:(q + 1) * P], w[:, c, :], start=(c == 0),
                            stop=(bias is None and c == n_k - 1))
        if bias is not None:
            last = t.matmul(o, k.ones_row[0:1, 0:P], bias, start=False, stop=True)
    last.then_inc(done, 1)


def update_pe(k, pe, tag, src, n_k, w, turn, norm=True):
    if turn:
        transpose_rows(k, k.o_nat, 0, k.sem(tag + "_oT_ps"))
    pe.wait_ge(k.sem(tag + "_oT"), 1)
    rows_linear(k, src, n_k, w, None, 1, k.sem(tag + "_y"))
    if norm:
        pe.wait_ge(k.sem(tag + "_xn"), QT)
        transpose_rows(k, k.xn, 2, k.sem(tag + "_xnT_ps"))


def update_dve(k, dve, link, tag, bias, turn, norm=True):
    v = k.nc.vector
    if turn:
        dve.wait_ge(k.sem(tag + "_oT_ps"), 1)
        v.tensor_copy(k.oT[:, :, :].rearrange("p c q -> p (c q)"), k.ps[:, 0, :]).then_inc(k.sem(tag + "_oT"), 1)
    if bias is not None:
        link(v.tensor_tensor(k.x[:, :, :], k.x[:, :, :], bias.unsqueeze(1).to_broadcast([P, QT, D]), ALU.add))
    dve.wait_ge(k.sem(tag + "_y"), 1)
    xf = k.x[:, :, :].rearrange("p t d -> p (t d)")
    link(v.tensor_tensor(xf, xf, k.ps[:, 1, :], ALU.add))
    if norm:
        layer_norm(k, dve, link, k.x, k.xn, k.sem(tag + "_xn"))
        dve.wait_ge(k.sem(tag + "_xnT_ps"), 1)
        v.tensor_copy(k.xnT[:, :, :].rearrange("p c q -> p (c q)"), k.ps[:, 2, :]).then_inc(k.sem(tag + "_xnT"), 1)


class Small:

    def __init__(self, k, heads, causal, q_of, k_of, v_of, out_of, interleave=1):
        self.causal = causal
        self.interleave = interleave
        self.q_of, self.k_of, self.v_of, self.out_of = q_of, k_of, v_of, out_of
        self.base = k.small_pairs
        self.pairs = [(h0, q) for h0 in range(0, heads, 2) for q in range(QT)]
        k.small_pairs += len(self.pairs)

    def tiles(self, q):
        return q + 1 if self.causal else QT


def small_pe(k, pe, a):
    t = k.nc.tensor
    s = {n: k.sem("small_" + n) for n in ("S", "exp", "pn", "PT", "PT_copied", "out")}

    def scores(n):
        h0, q = a.pairs[n]
        nk = a.tiles(q) * P
        if n >= 2:
            pe.wait_ge(s["exp"], 2 * (a.base + n - 1))
        for e in range(2):
            o = k.ps[:, n % 2, e * S:e * S + nk]
            last = t.matmul(o, a.q_of(h0 + e, q), a.k_of(h0 + e, nk), start=True, stop=not a.causal)
            if a.causal:
                last = t.matmul(o[:, nk - P:nk], k.ident_bf[:, :], k.causal[:, :], start=False, stop=True)
        last.then_inc(s["S"], 1)

    def turn(n):
        h0, q = a.pairs[n]
        pe.wait_ge(s["pn"], 2 * (a.base + n + 1))
        if n >= 2:
            pe.wait_ge(s["PT_copied"], a.base + n - 1)
        for e in range(2):
            for c in range(a.tiles(q)):
                last = t.transpose(k.ps[:, 2 + n % 2, (2 * e + c) * P:(2 * e + c + 1) * P],
                                   k.sp_rows[:, n % 2, e, c * P:(c + 1) * P], k.ident[:, :])
        last.then_inc(s["PT"], 1)

    def values(n):
        h0, q = a.pairs[n]
        pe.wait_ge(s["PT_copied"], a.base + n + 1)
        for e in range(2):
            for r in range(a.interleave):
                for c in range(a.tiles(q)):
                    cols = k.sp_T[:, n % 2, (2 * e + c) * P:(2 * e + c + 1) * P].rearrange("p (m r) -> p m r", r=a.interleave)
                    last = t.matmul(a.out_of(h0 + e, q, r), a.v_of(h0 + e, c), cols[:, :, r],
                                    start=(c == 0), stop=(c == a.tiles(q) - 1))
        last.then_inc(s["out"], 1)

    n_pairs = len(a.pairs)
    scores(0)
    scores(1)
    for n in range(n_pairs):
        if n + 2 < n_pairs:
            scores(n + 2)
        turn(n)
        if n >= 1:
            values(n - 1)
    values(n_pairs - 1)


def small_act(k, act, a):
    sc = k.nc.scalar
    s = {n: k.sem("small_" + n) for n in ("max", "exp", "PT", "PT_copied", "out")}

    def copy_turned(n):
        q = a.pairs[n][1]
        nk = a.tiles(q) * P
        act.wait_ge(s["PT"], a.base + n + 1)
        if n >= 2:
            act.wait_ge(s["out"], a.base + n - 1)
        sc.activation(k.sp_T[:, n % 2, :].rearrange("p (e m) -> p e m", e=2)[:, :, 0:nk],
                      k.ps[:, 2 + n % 2, :].rearrange("p (e m) -> p e m", e=2)[:, :, 0:nk], ACT.Copy).then_inc(s["PT_copied"], 1)

    for n, (h0, q) in enumerate(a.pairs):
        nk = a.tiles(q) * P
        act.wait_ge(s["max"], a.base + n + 1)
        if n >= 2:
            act.wait_ge(s["PT"], a.base + n - 1)
        for e in range(2):
            sc.activation(k.sp_rows[:, n % 2, e, 0:nk], k.ps[:, n % 2, e * S:e * S + nk], ACT.Exp,
                          bias=k.nmax[:, 2 * n + e:2 * n + e + 1],
                          accum_out=k.sums[:, 2 * n + e:2 * n + e + 1]).then_inc(s["exp"], 1)
        if n >= 1:
            copy_turned(n - 1)
    copy_turned(len(a.pairs) - 1)


def small_dve(k, dve, a):
    v = k.nc.vector
    s = {n: k.sem("small_" + n) for n in ("S", "max", "exp", "pn", "inv")}

    def row_max(n):
        q = a.pairs[n][1]
        nk = a.tiles(q) * P
        dve.wait_ge(s["S"], a.base + n + 1)
        v.tensor_reduce(k.nmax[:, 2 * n:2 * n + 2], k.ps[:, n % 2, :].rearrange("p (e m) -> p e m", e=2)[:, :, 0:nk],
                        AX.X, ALU.max, negate=True).then_inc(s["max"], 1)

    row_max(0)
    row_max(1)
    for n, (h0, q) in enumerate(a.pairs):
        nk = a.tiles(q) * P
        dve.wait_ge(s["exp"], 2 * (a.base + n + 1))
        v.reciprocal(k.inv[:, 2 * n:2 * n + 2], k.sums[:, 2 * n:2 * n + 2]).then_inc(s["inv"], 1)
        dve.wait_ge(s["inv"], a.base + n + 1)
        for e in range(2):
            v.tensor_scalar(k.sp_rows[:, n % 2, e, 0:nk], k.sp_rows[:, n % 2, e, 0:nk],
                            k.inv[:, 2 * n + e:2 * n + e + 1], None, ALU.mult).then_inc(s["pn"], 1)
        if n + 2 < len(a.pairs):
            row_max(n + 2)


def stage_self0(k):
    nc = k.nc
    vec, sc, t = nc.vector, nc.scalar, nc.tensor
    att = Small(k, H, False,
                q_of=lambda h, q: k.q_mask[:, h, q * P:(q + 1) * P],
                k_of=lambda h, nk: k.kT_self[:, h // 8, 0:nk],
                v_of=lambda h, c: k.v_self[:, c, h, :],
                out_of=lambda h, q, r: k.ps[32 * (h % 4):32 * (h % 4) + 32, 4 + h // 8, (h // 4 % 2) * S + q * P:(h // 4 % 2) * S + (q + 1) * P])
    with nc.Block() as block:
        @block.sync
        def _(sp):
            sp.dma_start(k.mask_u8, k.i["mask_Bx1xSxS2_bf1"].rearrange("a b (t p) n -> p (a b t) n", p=P)).then_inc(k.sem("d_mask_in"), 16)

        @block.gpsimd
        def _(pool):
            nc.gpsimd.memset(k.v_self[:, :, :, :], 0.0).then_inc(k.sem("b_v_z"), 1)

        @block.tensor
        def _(pe):
            update_pe(k, pe, "a", k.oT, KT, k.w_out0, True)
            pe.wait_ge(k.sem("a_xnT"), 1)
            for q in range(QT):
                for c in range(KT):
                    last = t.matmul(k.ps[:, 3 + q, :], k.xnT[:, c, q * P:(q + 1) * P], k.w_qkv0[:, c, 0:2 * D],
                                    start=(c == 0), stop=(c == KT - 1))
            last.then_inc(k.sem("b_qk"), 1)
            rows_linear(k, k.xnT, KT, k.w_qkv0[:, :, 2 * D:3 * D], None, 5, k.sem("b_v"))
            pe.wait_ge(k.sem("c_w_sum"), 1)
            t.matmul(k.ps[:, 7, 0:1], k.ones_sq[:, :], k.w_sum[:, :], start=True, stop=True).then_inc(k.sem("c_w_total"), 1)
            pe.wait_ge(k.sem("b_qkn"), QT)
            for q in range(QT):
                for half in range(2):
                    for c in range(KT):
                        bank, col = (2 * c, 0) if half == 0 else (1, c * S)
                        last = t.transpose(k.ps[:, bank, col + q * P:col + (q + 1) * P],
                                           k.qk[:, q, half * D + c * P:half * D + (c + 1) * P], k.ident[:, :])
            last.then_inc(k.sem("b_qkT"), 1)
            pe.wait_ge(k.sem("b_kT"), 1)
            pe.wait_ge(k.sem("b_qm_dve"), H // 2)
            pe.wait_ge(k.sem("b_qm_act"), H // 2)
            pe.wait_ge(k.sem("b_v_in"), QT)
            small_pe(k, pe, att)
            update_pe(k, pe, "b", k.oT_pad, 4, k.w_proj0, False, norm=False)
            pe.wait_ge(k.sem("c_aq"), 1)
            o = k.ps[:, 2, :].bitcast(BF16)
            for q in range(QT):
                for c in range(KT):
                    last = t.transpose(o[:, c * S + q * P:c * S + (q + 1) * P], k.a_q[:, q, c * P:(c + 1) * P], k.ident_bf[:, :])
            last.then_inc(k.sem("c_aqT_ps"), 1)
            pe.wait_ge(k.sem("c_aqT"), 1)
            rows_linear(k, k.a_qT, KT, k.w_tern, None, 3, k.sem("c_y"))
            pe.wait_ge(k.sem("c_xn"), QT)
            transpose_rows(k, k.xn, 2, k.sem("c_xnT_ps"))

        @block.scalar
        def _(act):
            act.wait_ge(k.sem("d_mask_in"), 16)
            for q in range(QT):
                sc.activation(k.mask_bias[:, q, :], k.mask_u8[:, q, :], ACT.Copy, scale=-MASKED, bias=MASKED,
                                     accum_out=k.mask_sum[:, q:q + 1]).then_inc(k.sem("d_bias"), 1)

            act.wait_ge(k.sem("b_qk_rows"), 1)
            sc.activation(k.qk_sq[:, :, :], k.qk[:, :, :], ACT.Square).then_inc(k.sem("b_sq"), 1)
            act.wait_ge(k.sem("b_qkT"), 1)
            for h in range(8, H):
                sc.activation(k.q_mask[:, h, :], k.ps[:, 2, 0:S], ACT.Copy, scale=k.head_mask[:, h - 8:h - 7]).then_inc(k.sem("b_qm_act"), 1)
            small_act(k, act, att)

        @block.vector
        def _(dve):
            link = Order(dve, k.sem("dve_order"), k.dve_ordered).link
            update_dve(k, dve, link, "a", None, True)
            vec.tensor_reduce(k.w_sum[:, :], k.w_ffn0[:, :, :].rearrange("p t n -> p (t n)"), AX.X, ALU.add,
                              apply_absolute_value=True).then_inc(k.sem("c_w_sum"), 1)
            dve.wait_ge(k.sem("b_qk"), 1)
            vec.tensor_tensor(k.qk[:, :, :], k.ps[:, 3:5, :], k.b_qkv0[:, 0:2 * D].unsqueeze(1).to_broadcast([P, QT, 2 * D]), ALU.add).then_inc(k.sem("b_qk_rows"), 1)
            dve.wait_ge(k.sem("b_v"), 1)
            dve.wait_ge(k.sem("b_v_z"), 1)
            b_v = k.b_qkv0[:, 2 * D:3 * D].rearrange("p (h d) -> p h d", d=DH)
            for q in range(QT):
                vec.tensor_tensor(k.v_self[:, q, :, 0:DH], k.ps[:, 5, q * D:(q + 1) * D].rearrange("p (h d) -> p h d", d=DH), b_v,
                                  ALU.add).then_inc(k.sem("b_v_in"), 1)
            dve.wait_ge(k.sem("b_sq"), 1)
            link(vec.tensor_reduce(k.rs_v[:, :], k.qk_sq[:, :, :].rearrange("p t (h d) -> p (t h) d", d=DH), AX.X, ALU.add))
            link(vec.tensor_scalar(k.rs_v[:, :], k.rs_v[:, :], 1.0 / DH, 1e-6, ALU.mult, ALU.add))
            rsqrt(k, link, 64)
            link(vec.tensor_scalar(k.w_qkn[:, 0, :], k.w_qkn[:, 0, :], 1.0 / np.sqrt(DH), None, ALU.mult))
            heads = k.qk[:, :, :].rearrange("p t (h d) -> p (t h) d", d=DH)
            link(vec.tensor_tensor(heads, heads, k.rs_y[:, :].unsqueeze(2).to_broadcast([P, 4 * H, DH]), ALU.mult))
            for q in range(QT):
                row = k.qk[:, q, :].rearrange("p (s h d) -> p s h d", s=2, d=DH)
                vec.tensor_tensor(row, row, k.w_qkn[:, :, :].unsqueeze(2).to_broadcast([P, 2, H, DH]), ALU.mult).then_inc(k.sem("b_qkn"), 1)
            dve.wait_ge(k.sem("c_w_total"), 1)
            link(vec.tensor_scalar(k.w_scale[:, :], k.ps[:, 7, 0:1], 1.0 / (D * D), 1e-8, ALU.mult, ALU.add))
            link(vec.reciprocal(k.w_inv[:, :], k.w_scale[:, :]))
            link(vec.tensor_scalar(k.w_ffn0[:, :, :], k.w_ffn0[:, :, :], k.w_inv[:, 0:1], ROUND, ALU.mult, ALU.add))
            link(vec.tensor_scalar(k.w_ffn0[:, :, :], k.w_ffn0[:, :, :], -ROUND, 1.0, ALU.add, ALU.min))
            link(vec.tensor_scalar(k.w_tern[:, :, :], k.w_ffn0[:, :, :], -1.0, None, ALU.max))
            dve.wait_ge(k.sem("b_qkT"), 1)
            vec.tensor_copy(k.kT_self[:, :, :].rearrange("p t n -> p (t n)"), k.ps[:, 1, :]).then_inc(k.sem("b_kT"), 1)
            for h in range(8):
                vec.tensor_scalar(k.q_mask[:, h, :], k.ps[:, 0, 0:S], k.head_mask[:, h:h + 1], None, ALU.mult).then_inc(k.sem("b_qm_dve"), 1)
            small_dve(k, dve, att)
            dve.wait_ge(k.sem("small_out"), att.base + len(att.pairs))
            vec.tensor_copy(k.oT_pad[:, :, :].rearrange("p (b g) q -> p b (g q)", b=2), k.ps[:, 4:6, :]).then_inc(k.sem("b_oT"), 1)
            update_dve(k, dve, link, "b", k.b_proj0, False, norm=False)
            layer_norm(k, dve, link, k.x, k.xn, k.sem("c_xn0"))
            dve.wait_ge(k.sem("c_xn0"), QT)
            link(vec.tensor_reduce(k.a_scale[:, :], k.xn[:, :, :], AX.X, ALU.max, apply_absolute_value=True))
            link(vec.tensor_scalar(k.a_scale[:, :], k.a_scale[:, :], 1e-8, None, ALU.add))
            link(vec.reciprocal(k.a_inv[:, :], k.a_scale[:, :]))
            for q in range(QT):
                link(vec.tensor_scalar(k.xn[:, q, :], k.xn[:, q, :], k.a_inv[:, q:q + 1], 127.0, ALU.mult, ALU.mult))
            link(vec.tensor_scalar(k.xn[:, :, :], k.xn[:, :, :], 127.0, -128.0, ALU.min, ALU.max))
            vec.tensor_scalar(k.a_q[:, :, :], k.xn[:, :, :], ROUND, -ROUND, ALU.add, ALU.add).then_inc(k.sem("c_aq"), 1)
            dve.wait_ge(k.sem("c_aqT_ps"), 1)
            vec.tensor_copy(k.a_qT[:, :, :].rearrange("p c q -> p (c q)"), k.ps[:, 2, :].bitcast(BF16)[:, 0:KT * S]).then_inc(k.sem("c_aqT"), 1)
            link(vec.tensor_scalar(k.a_scale[:, :], k.a_scale[:, :], k.w_scale[:, 0:1], 1.0 / 127.0, ALU.mult, ALU.mult))
            dve.wait_ge(k.sem("c_y"), 1)
            for q in range(QT):
                link(vec.scalar_tensor_tensor(out=k.x[:, q, :], in0=k.ps[:, 3, q * D:(q + 1) * D], scalar=k.a_scale[:, q:q + 1],
                                              in1=k.x[:, q, :], op0=ALU.mult, op1=ALU.add))
            layer_norm(k, dve, link, k.x, k.xn, k.sem("c_xn"))
            dve.wait_ge(k.sem("c_xnT_ps"), 1)
            vec.tensor_copy(k.xnT[:, :, :].rearrange("p c q -> p (c q)"), k.ps[:, 2, :]).then_inc(k.sem("c_xnT"), 1)


def stage_cross1_prepare(k):
    nc = k.nc
    with nc.Block() as block:
        @block.sync
        def _(sp):
            for j in range(4):
                load_k_unit(k, sp, k.kd1, j // 2, j % 2, j, k.sem(f"d_k_in{j}"))
            store_q_parts(k, sp, 1)
            load_q_stack(k, sp, 1)
            sp.wait_ge(k.sem("q_loaded"), 16 * Q_LOADS * 2)

        @block.gpsimd
        def _(pool):
            g = nc.gpsimd
            link = Order(pool, k.sem("pool_order"), k.pool_ordered).link
            link(g.memset(k.q_all[MAXROW:LOROW, :, :], 0.0))
            link(g.memset(k.v_st[:, :, :, :], 0.0))
            link(g.memset(k.v_st[:, :, :, DH], 1.0))

        @block.vector
        def _(dve):
            v = nc.vector
            link = Order(dve, k.sem("dve_order"), k.dve_ordered).link
            dve.wait_ge(k.sem("d_bias"), QT)
            link(v.tensor_scalar(k.any_keep[:, :], k.mask_sum[:, :], MASKED * (S2 - 0.5), 1.0 / np.sqrt(DH), ALU.is_gt, ALU.mult))
            v.tensor_reduce(k.masked_f[:, :], k.mask_sum[:, :], AX.X, ALU.add).then_inc(k.sem("d_masked_sum"), 1)
            dve.wait_ge(k.sem("d_total"), 1)
            v.tensor_scalar(k.masked_i[:, :], k.ps[0:1, 6, 0:1], 0.0, None, ALU.is_lt).then_inc(k.sem("d_masked"), 1)
            dve.wait_ge(k.sem("d_q"), 1)
            for q in range(QT):
                v.tensor_scalar(k.xn[:, q, :], k.ps[:, 3, q * D:(q + 1) * D], k.any_keep[:, q:q + 1], None, ALU.mult).then_inc(k.sem("d_q_rows"), 1)
            dve.wait_ge(k.sem("d_qT"), 1)
            link(v.tensor_copy(k.q_f[:, :, :].rearrange("p c q -> p (c q)"), k.ps[:, 4, :]))
            split_q(k, link).then_inc(k.sem("q_split"), 1)

        @block.tensor
        def _(pe):
            rows_linear(k, k.xnT, KT, k.w1_q, k.b1_qo[0:1, 0, :], 3, k.sem("d_q"))
            pe.wait_ge(k.sem("d_masked_sum"), 1)
            nc.tensor.matmul(k.ps[0:1, 6, 0:1], k.ones_sq[:, 0:1], k.masked_f[:, :], start=True, stop=True).then_inc(k.sem("d_total"), 1)
            pe.wait_ge(k.sem("d_q_rows"), QT)
            transpose_rows(k, k.xn, 4, k.sem("d_qT"))


def stage_cross1(k):
    nc = k.nc
    groups = 2 * GROUPS
    m_blocks = S2 // 512
    n_m = QT * m_blocks
    M_EARLY = 2
    m_beside = [2, 2, 2, 2, 2, 2, 2, 0]
    assert M_EARLY + sum(m_beside) == n_m
    MT0 = S + 32 * QT
    PV_LAG = 2
    probs = k.probs[:, :, :, :].rearrange("p b (g c) q -> p (b g) c q", c=GROUP_CH)
    s = {n: k.sem("d_" + n) for n in (
        "scores", "exp", "pv", "q_staged", "v_staged", "m_scores", "m_read", "m_ops", "m_parts",
        "m_turned", "m_rows", "acc_copied", "sel", "rec", "o_read")}
    k_in = [k.sem(f"d_k_in{j}") for j in range(4)]
    qm_in = [k.sem(f"d_qm_in{b}") for b in range(2)]

    def scores_bank(g):
        return k.ps[:, 2 * (g % 2):2 * (g % 2) + 2, :].rearrange("p b (c q) -> p (b c) q", q=S)

    def pairs_of_heads(eng, body):
        body(0, True, False)
        with eng.Fori(1, H // 2 - 1) as it:
            body(it, False, False)
        body(H // 2 - 1, False, True)

    with nc.Block() as block:
        @block.sync
        def _(sp):
            def load_q(h, b):
                sp.dma_start(k.q_m[0:MAXROW, b, :], k.q_all[0:MAXROW, h, :]).then_inc(qm_in[b], 16)

            for b in range(2):
                load_q(b, b)
            load_late_weights(k, sp)
            with sp.Fori(1, H // 2) as it:
                for b in range(2):
                    sp.wait_ge(s["m_read"], n_m * 2 * it + n_m * (b - 1))
                    load_q(2 * it + b, b)
                    for j in (2 * b, 2 * b + 1):
                        sp.wait_ge(s["scores"], 16 * it - 16 + 4 * (j + 1))
                        load_k_unit(k, sp, k.kd1, 2 * it + b, j % 2, j, k_in[j])

        @block.gpsimd
        def _(pool):
            g = nc.gpsimd

            def stage(h, b, fresh):
                if not fresh:
                    pool.wait_ge(s["scores"], groups * h - groups)
                g.tensor_copy(k.q_st[0:STACK, b, :], k.q_all[0:STACK, h, :]).then_inc(s["q_staged"], 1)
                if not fresh:
                    pool.wait_ge(s["pv"], groups * h - groups)
                g.tensor_copy(k.v_st[:, b, :, 0:DH], k.v_proj[:, :, bass.ds(h * DH, DH)]).then_inc(s["v_staged"], 1)

            stage(0, 0, True)
            stage(1, 1, True)
            with pool.Fori(1, H // 2) as it:
                stage(2 * it, 0, False)
                stage(2 * it + 1, 1, False)

        @block.scalar
        def _(act):
            def body(it, first, last):
                for b in range(2):
                    for g in range(groups):
                        n = 16 * it + 8 * b + g
                        act.wait_ge(s["scores"], n + 1)
                        if not (first and b == 0):
                            act.wait_ge(s["pv"], n - groups + 1)
                        nc.scalar.activation(probs[:, g], scores_bank(g), ACT.Exp).then_inc(s["exp"], 1)
                        if g == 1 and not (first and b == 0):
                            copy_acc(2 * it + b - 1, 1 - b)
                    if not (last and b == 1):
                        m_rows(2 * it + b + 1, 1 - b)

            def m_rows(h, b):
                act.wait_ge(s["m_turned"], h + 1)
                act.wait_ge(s["q_staged"], h + 1)
                nc.scalar.activation(k.q_st[MAXROW:LOROW, b, :].rearrange("p (t n) -> p t n", t=QT),
                                     k.ps[MAXROW:LOROW, 4:4 + QT, MT0:MT0 + P], ACT.Copy).then_inc(s["m_rows"], 1)

            def copy_acc(h, b):
                act.wait_ge(s["pv"], groups * h + groups)
                nc.scalar.activation(k.acc_sb[:, b, :], k.ps[:, 4 + b, 0:S], ACT.Copy).then_inc(s["acc_copied"], 1)

            m_rows(0, 0)
            pairs_of_heads(act, body)
            copy_acc(H - 1, 1)

        @block.tensor
        def _(pe):
            t = nc.tensor

            def m_scores(it, b, idx, masked, first):
                h = 2 * it + b
                blk, q = divmod(idx, QT)
                half = blk // (m_blocks // 2)
                if idx == 0:
                    pe.wait_ge(qm_in[b], 16 * (it + 1))
                if idx % (n_m // 2) == 0:
                    pe.wait_ge(k_in[2 * b + half], 16 * K_LOADS * (it + 1))
                if not (first and b == 0 and idx < 2):
                    pe.wait_ge(s["m_read"], n_m * h + idx - 1)
                o = k.ps[:, 6 + idx % 2, :]
                key0 = (blk % (m_blocks // 2)) * 512
                last = t.matmul(o, k.q_m[0:MAXROW, b, q * P:(q + 1) * P], k.k_st[0:MAXROW, 2 * b + half, key0:key0 + 512],
                                start=True, stop=not masked)
                if masked:
                    last = t.matmul(o, k.ident_bf[:, :], k.mask_bias[:, q, blk * 512:(blk + 1) * 512], start=False, stop=True)
                last.then_inc(s["m_scores"], 1)

            def m_turn(it, b):
                pe.wait_ge(s["m_parts"], 2 * it + b + 1)
                for q in range(QT):
                    last = t.matmul(k.ps[MAXROW:LOROW, 4 + q, MT0:MT0 + P], k.m_parts[:, q, :], k.ident_bf[:, :],
                                    start=True, stop=True)
                last.then_inc(s["m_turned"], 1)

            def qk(it, b, g, masked, first):
                h, j = 2 * it + b, 2 * b + g // GROUPS
                n = groups * h + g
                if g == 0:
                    pe.wait_ge(s["m_rows"], h + 1)
                if g % GROUPS == 0:
                    pe.wait_ge(k_in[j], 16 * K_LOADS * (it + 1))
                if not (first and b == 0 and g < 2):
                    pe.wait_ge(s["exp"], n - 1)
                out = scores_bank(g)
                for c in range(GROUP_CH):
                    ch = GROUP_CH * (g % GROUPS) + c
                    last = t.matmul(out[:, c, :], k.k_st[0:STACK, j, ch * P:(ch + 1) * P], k.q_st[0:STACK, b, :],
                                    start=True, stop=not masked)
                    if masked:
                        ch = GROUP_CH * g + c
                        for q in range(QT):
                            last = t.matmul(out[:, c, q * P:(q + 1) * P], k.mask_bias[:, q, ch * P:(ch + 1) * P],
                                            k.ident_bf[:, :], start=False, stop=(q == QT - 1))
                last.then_inc(s["scores"], 1)

            def pv(it, b, g, first):
                h = 2 * it + b
                pe.wait_ge(s["exp"], groups * h + g + 1)
                if g == 0:
                    pe.wait_ge(s["v_staged"], h + 1)
                    if not first:
                        pe.wait_ge(s["o_read"], h - 1)
                for m in range(GROUP_CH):
                    last = t.matmul(k.ps[32 * m:32 * m + 32, 4 + b, 0:S], k.v_st[:, b, GROUP_CH * g + m, :], probs[:, g, m, :],
                                    start=(g == 0), stop=(g == groups - 1))
                last.then_inc(s["pv"], 1)

            def sel(h, b):
                pe.wait_ge(s["acc_copied"], h + 1)
                for q in range(QT):
                    last = t.matmul(k.ps[:, 4 + b, S + 32 * q:S + 32 * (q + 1)], k.acc_sb[:, b, q * P:(q + 1) * P],
                                    k.quad_sum[:, :], start=True, stop=True)
                last.then_inc(s["sel"], 1)

            def all_heads(masked):
                for idx in range(n_m):
                    m_scores(0, 0, idx, masked, True)
                for idx in range(M_EARLY):
                    m_scores(0, 1, idx, masked, True)
                m_turn(0, 0)

                def body(it, first, last):
                    for b in range(2):
                        nit, nb = (it, 1) if b == 0 else (it + 1, 0)
                        more = not (last and b == 1)
                        for g in range(groups):
                            m_now = [M_EARLY + sum(m_beside[:g]) + n for n in range(m_beside[g])] if more else []
                            qk(it, b, g, masked, first)
                            for idx in m_now[:1]:
                                m_scores(nit, nb, idx, masked, False)
                            if g >= PV_LAG:
                                pv(it, b, g - PV_LAG, first)
                            for idx in m_now[1:]:
                                m_scores(nit, nb, idx, masked, False)
                            if g == 2 and not (first and b == 0):
                                sel(2 * it + b - 1, 1 - b)
                        for g in range(groups - PV_LAG, groups):
                            pv(it, b, g, first)
                        if not last:
                            for idx in range(M_EARLY):
                                m_scores(it + 1, b, idx, masked, False)
                        if more:
                            m_turn(nit, nb)

                pairs_of_heads(pe, body)
                sel(H - 1, 1)

            masked = pe.value_load(k.masked_i[0:1, 0:1], min_val=0, max_val=1)
            with pe.If(masked):
                all_heads(True)
            with pe.Else():
                all_heads(False)

        @block.vector
        def _(dve):
            v = nc.vector

            def m_read(h, idx):
                blk, q = divmod(idx, QT)
                dve.wait_ge(s["m_scores"], n_m * h + idx + 1)
                v.tensor_reduce(k.m_blk[:, q, blk:blk + 1], k.ps[:, 6 + idx % 2, :], AX.X, ALU.max).then_inc(s["m_read"], 1)

            def m_parts(h):
                ops = 4 * h
                dve.wait_ge(s["m_read"], n_m * h + n_m)
                v.tensor_reduce(k.m_neg[:, :], k.m_blk[:, :, :], AX.X, ALU.max, negate=True).then_inc(s["m_ops"], 1)
                dve.wait_ge(s["m_ops"], ops + 1)
                v.tensor_copy(k.m_parts[:, :, 0], k.m_neg[:, :]).then_inc(s["m_ops"], 1)
                dve.wait_ge(s["m_ops"], ops + 2)
                v.tensor_tensor(k.m_res[:, 0, :], k.m_neg[:, :], k.m_parts[:, :, 0], ALU.subtract).then_inc(s["m_ops"], 1)
                dve.wait_ge(s["m_ops"], ops + 3)
                v.tensor_copy(k.m_parts[:, :, 1], k.m_res[:, 0, :]).then_inc(s["m_ops"], 1)
                dve.wait_ge(s["m_ops"], ops + 4)
                v.tensor_tensor(k.m_parts[:, :, 2], k.m_res[:, 0, :], k.m_parts[:, :, 1], ALU.subtract).then_inc(s["m_parts"], 1)

            def normalise(h, b):
                o = k.ps[:, 4 + b, S:S + 32 * QT].rearrange("p (q n) -> p q n", q=QT)
                dve.wait_ge(s["sel"], h + 1)
                v.reciprocal(k.rec[:, b, :], o[:, :, DH]).then_inc(s["rec"], 1)
                dve.wait_ge(s["rec"], h + 1)
                v.tensor_tensor(k.o_nat[:, :, bass.ds(h * DH, DH)], o[:, :, 0:DH],
                                k.rec[:, b, :].unsqueeze(2).to_broadcast([P, QT, DH]), ALU.mult).then_inc(s["o_read"], 1)

            for idx in range(n_m):
                m_read(0, idx)
            m_parts(0)

            def body(it, first, last):
                for b in range(2):
                    h = 2 * it + b
                    if not (last and b == 1):
                        for idx in range(M_EARLY + sum(m_beside[0:4])):
                            m_read(h + 1, idx)
                    if not (first and b == 0):
                        normalise(h - 1, 1 - b)
                    if not (last and b == 1):
                        for idx in range(M_EARLY + sum(m_beside[0:4]), n_m):
                            m_read(h + 1, idx)
                        m_parts(h + 1)

            pairs_of_heads(dve, body)
            normalise(H - 1, 1)


def load_late_weights(k, sp):
    i = k.i
    done = k.sem("e_w_in")
    for n, name in enumerate(("Wq", "Wk", "Wv")):
        sp.dma_start(k.e_w[:, n], i[f"L1_attn_{name}T"].rearrange("(t p) n -> p t n", p=P)).then_inc(done, 16)
    sp.dma_start(k.e_proj, i["L1_attn_proj"].rearrange("(t p) n -> p t n", p=P)).then_inc(done, 16)
    sp.dma_start(k.e_bqk[:, 0, :], i["L1_attn_bq_cols"]).then_inc(done, 16)
    sp.dma_start(k.e_bqk[:, 1, :], i["L1_attn_bk_cols"]).then_inc(done, 16)
    sp.dma_start(k.e_bv, i["L1_attn_bv_row"].to_broadcast([P, 2 * E_T * E_DH])).then_inc(done, 16)
    done = k.sem("f_w_in")
    sp.dma_start(k.f_wq, i["L1_ffn_WqT"].rearrange("(t p) n -> p t n", p=P)).then_inc(done, 16)
    sp.dma_start(k.f_wo, i["L1_ffn_WoT"].rearrange("(t p) n -> p t n", p=P)).then_inc(done, 16)
    for half in range(2):
        sp.dma_start(k.f_wkc[:, :, half * E_DH:(half + 1) * E_DH],
                     i["L1_ffn_WkcT"].rearrange("(t p) n -> p t n", p=P)).then_inc(done, 16)
    sp.dma_start(k.f_wvc, i["L1_ffn_WvcT"].rearrange("(t p) n -> p t n", p=P)).then_inc(done, 16)
    sp.dma_start(k.f_wr, i["L1_ffn_WrT"].rearrange("(t p) n -> p t n", p=P)).then_inc(done, 16)
    for n in range(2):
        sp.dma_start(k.f_g[:, n, :], i[f"L1_ffn_g{n + 1}_cols"]).then_inc(done, 16)
    sp.dma_start(k.f_be, i["L1_ffn_expert_bias"].unsqueeze(0)).then_inc(done, 16)


def rms_norm(k, dve, link, src, done):
    v = k.nc.vector
    link(*[v.bn_stats(k.ln_stats[:, t, :], src[:, t, :]) for t in range(QT)])
    link(*[v.bn_aggr(k.ln_mv[:, t, :], k.ln_stats[:, t, :]) for t in range(QT)])
    link(v.tensor_tensor(k.rs_t[:, 0:QT], k.ln_mv[:, :, 0], k.ln_mv[:, :, 0], ALU.mult))
    link(v.scalar_tensor_tensor(out=k.rs_v[:, 0:QT], in0=k.rs_t[:, 0:QT], scalar=1e-6, in1=k.ln_mv[:, :, 1],
                                op0=ALU.add, op1=ALU.add))
    rsqrt(k, link, QT)
    for t in range(QT):
        v.tensor_scalar(k.xn[:, t, :], src[:, t, :], k.rs_y[:, t:t + 1], None, ALU.mult).then_inc(done, 1)


def weigh_turned(k, dve, which, ready, done):
    dve.wait_ge(ready, 1)
    for c in range(KT):
        k.nc.vector.tensor_scalar(k.xnT[:, c, :], k.ps[:, 2, c * S:(c + 1) * S], k.f_g[:, which, c:c + 1], None,
                                  ALU.mult).then_inc(done, 1)


def stage_self1(k):
    nc, i = k.nc, k.i
    v, sc, t = nc.vector, nc.scalar, nc.tensor
    causal = Small(k, 2 * E_T, True,
                   q_of=lambda h, q: k.e_qT[:, h // 2, q * P:(q + 1) * P],
                   k_of=lambda h, nk: k.e_kM[:, h, 0:nk],
                   v_of=lambda h, c: k.e_v[:, c, h * E_DH:(h + 1) * E_DH],
                   out_of=lambda h, q, r: k.ps[64 * r:64 * r + 64, 4 + h // 4, (h % 4) * P + q * 64:(h % 4) * P + (q + 1) * 64],
                   interleave=2)
    latent = Small(k, F_H, False,
                   q_of=lambda h, q: k.f_qT[:, h // 2, q * P:(q + 1) * P],
                   k_of=lambda h, nk: k.e_kM[:, h % 2, 0:nk],
                   v_of=lambda h, c: k.f_v[:, c, :],
                   out_of=lambda h, q, r: k.ps[64 * (h % 2):64 * (h % 2) + 64, 4, (h // 2) * S + q * P:(h // 2) * S + (q + 1) * P])
    experts = [N_EXP] + list(range(N_EXP))
    jobs = [(w, n) for w in range(3) for n in range(4)]
    by_dve = [n for n, (w, m) in enumerate(jobs) if w != 1]
    by_act = [n for n in range(len(jobs)) if n not in by_dve]

    def wait_evacuated(pe, n):
        m = n - 4
        if m in by_dve:
            pe.wait_ge(k.sem("e_dve"), by_dve.index(m) + 1)
        else:
            pe.wait_ge(k.sem("e_act"), by_act.index(m) + 1)

    with nc.Block() as block:
        @block.sync
        def _(sp):
            for n, e in enumerate(experts):
                names = ("eW1T", "eW3T", "eW2T") if e < N_EXP else ("sW1T", "sW3T", "sW2T")
                for w, name in enumerate(names):
                    a = i["L1_ffn_" + name]
                    a = a[e] if e < N_EXP else a
                    sp.dma_start(k.f_exp[e][w], a.rearrange("(t p) n -> p t n", p=P)).then_inc(k.sem(f"f_exp_in{n}"), 16)
            sp.wait_ge(k.sem("f_x"), 2 * (N_EXP + 1))
            sp.dma_start(k.out.rearrange("a (t p) d -> p (a t) d", p=P), k.x[:, :, :]).then_inc(k.sem("out"), 16)
            sp.wait_ge(k.sem("out"), 16)

        @block.gpsimd
        def _(pool):
            g = nc.gpsimd
            link = Order(pool, k.sem("pool_order"), k.pool_ordered).link
            link(g.memset(k.causal[:, :], 0.0))
            link(g.affine_select(out=k.causal[:, :], in_=k.causal[:, :], compare_op=ALU.is_ge, fill=-1e30, base=0,
                                 pattern=[[-1, P]], channel_multiplier=1))
            for e in range(2):
                link(g.memset(k.e_kM[(1 - e) * E_DH:(2 - e) * E_DH, :, :].rearrange("p (t e) q -> p t e q", e=2)[:, :, e, :], 0.0))
            link(g.memset(k.f_low[:, :, :], 1.0))
            link(g.affine_select(out=k.f_low[:, :, :], in_=k.f_low[:, :, :], compare_op=ALU.is_gt, fill=0.0, base=0,
                                 pattern=[[1, N_EXP], [-1, N_EXP]], channel_multiplier=0))
            link(g.memset(k.f_comb[:, :, :], 1.0))

        @block.tensor
        def _(pe):
            update_pe(k, pe, "d", k.oT, KT, k.w1_o, True)
            pe.wait_ge(k.sem("d_xnT"), 1)
            pe.wait_ge(k.sem("e_w_in"), 16 * 7)
            for n, (w, m) in enumerate(jobs):
                if n >= 4:
                    wait_evacuated(pe, n)
                if w < 2:
                    for half in range(2):
                        tile = 2 * m + half
                        for c in range(KT):
                            last = t.matmul(k.ps[:, 4 + n % 4, half * S:(half + 1) * S], k.e_w[:, w, c, tile * P:(tile + 1) * P],
                                            k.xnT[:, c, :], start=(c == 0), stop=(c == KT - 1))
                else:
                    cols = slice((m % 2) * 512, (m % 2 + 1) * 512)
                    for c in range(KT):
                        last = t.matmul(k.ps[:, 4 + n % 4, :], k.xnT[:, c, (m // 2) * P:(m // 2 + 1) * P], k.e_w[:, w, c, cols],
                                        start=(c == 0), stop=(c == KT - 1))
                last.then_inc(k.sem("e_job"), 1)
            pe.wait_ge(k.sem("e_dve"), len(by_dve))
            pe.wait_ge(k.sem("e_act"), len(by_act))
            pe.wait_ge(k.sem("pool_order"), k.pool_ordered[0])
            small_pe(k, pe, causal)
            pe.wait_ge(k.sem("e_oT"), 1)
            for q in range(QT):
                for c in range(E_T):
                    last = t.matmul(k.ps[:, 1, q * D:(q + 1) * D], k.e_oT[:, q * 8:(q + 1) * 8, :, c], k.e_proj[:, c, :],
                                    start=(c == 0), stop=(c == E_T - 1))
            last.then_inc(k.sem("e_y"), 1)
            pe.wait_ge(k.sem("f_xn"), QT)
            transpose_rows(k, k.xn, 2, k.sem("f_xnT_ps"))
            pe.wait_ge(k.sem("f_xnT"), KT)
            pe.wait_ge(k.sem("f_w_in"), 16 * 9)
            for m in range(KT):
                for c in range(KT):
                    t.matmul(k.ps[:, 3, m * S:(m + 1) * S], k.f_wq[:, c, m * P:(m + 1) * P], k.xnT[:, c, :],
                             start=(c == 0), stop=(c == KT - 1))
            for c in range(KT):
                t.matmul(k.ps[:, 5, 0:S], k.f_wkc[:, c, :], k.xnT[:, c, :], start=(c == 0), stop=(c == KT - 1))
            for m in range(KT):
                for c in range(KT):
                    last = t.matmul(k.ps[:, 6, m * E_DH:(m + 1) * E_DH], k.xnT[:, c, m * P:(m + 1) * P], k.f_wvc[:, c, :],
                                    start=(c == 0), stop=(c == KT - 1))
            last.then_inc(k.sem("f_proj"), 1)
            pe.wait_ge(k.sem("f_qkv"), 4)
            small_pe(k, pe, latent)
            pe.wait_ge(k.sem("f_oT"), 1)
            rows_linear(k, k.oT, KT, k.f_wo, None, 1, k.sem("f_y"))
            pe.wait_ge(k.sem("g_xn"), QT)
            transpose_rows(k, k.xn, 2, k.sem("g_xnT_ps"))
            pe.wait_ge(k.sem("g_xnT"), KT)
            for q in range(QT):
                o = k.ps[:, 7, q * N_EXP:(q + 1) * N_EXP]
                for c in range(KT):
                    t.matmul(o, k.xnT[:, c, q * P:(q + 1) * P], k.f_wr[:, c, :], start=(c == 0), stop=False)
                last = t.matmul(o, k.ones_row[0:1, 0:P], k.f_be, start=False, stop=True)
            last.then_inc(k.sem("g_logits"), 1)

            def hidden(n):
                e = experts[n]
                pe.wait_ge(k.sem(f"f_exp_in{n}"), 48)
                if n >= 2:
                    pe.wait_ge(k.sem("g_h"), n - 1)
                for w in range(2):
                    for m in range(KT):
                        for c in range(KT):
                            last = t.matmul(k.ps[:, 2 * w + n % 2, m * S:(m + 1) * S], k.f_exp[e][w][:, c, m * P:(m + 1) * P],
                                            k.xnT[:, c, :], start=(c == 0), stop=(c == KT - 1))
                last.then_inc(k.sem("g_hidden"), 1)

            def down(n):
                pe.wait_ge(k.sem("g_h"), n + 1)
                if n >= 2:
                    pe.wait_ge(k.sem("f_x"), 2 * (n - 1))
                rows_linear(k, k.f_hT[:, n % 2], KT, k.f_exp[experts[n]][2], None, 4 + n % 2, k.sem("g_rows"))

            hidden(0)
            for n in range(N_EXP + 1):
                if n < N_EXP:
                    hidden(n + 1)
                down(n)

        @block.scalar
        def _(act):
            for n in by_act:
                w, m = jobs[n]
                act.wait_ge(k.sem("e_job"), n + 1)
                for half in range(2):
                    tile = 2 * m + half
                    for e in range(2):
                        rows = slice(e * E_DH, (e + 1) * E_DH)
                        ins = sc.activation(k.e_kM[rows, 2 * tile + e, :], k.ps[rows, 4 + n % 4, half * S:(half + 1) * S],
                                            ACT.Identity, bias=k.e_bqk[rows, 1, tile:tile + 1])
                ins.then_inc(k.sem("e_act"), 1)
            small_act(k, act, causal)
            act.wait_ge(k.sem("f_proj"), 1)
            for e in range(2):
                rows = slice(e * E_DH, (e + 1) * E_DH)
                sc.activation(k.e_kM[rows, e, :], k.ps[rows, 5, 0:S], ACT.Copy).then_inc(k.sem("f_qkv"), 1)
            sc.activation(k.f_v, k.ps[:, 6, 0:2 * E_DH].rearrange("p (t n) -> p t n", t=KT), ACT.Copy).then_inc(k.sem("f_qkv"), 1)
            small_act(k, act, latent)

            def gate(n):
                act.wait_ge(k.sem("g_hidden"), n + 1)
                if n >= 2:
                    act.wait_ge(k.sem("g_h"), n - 1)
                sc.activation(k.f_tanh[:, n % 2, :], k.ps[:, n % 2, :], ACT.Tanh, scale=0.5).then_inc(k.sem("g_tanh"), 1)

            act.wait_ge(k.sem("g_lg"), 1)
            sc.activation(k.f_rw[:, :, :], k.f_lg[:, :, :], ACT.Exp).then_inc(k.sem("g_rexp"), 1)
            gate(0)
            act.wait_ge(k.sem("g_diff"), 1)
            sc.activation(k.f_w[:, 1, :], k.f_w[:, 0, :], ACT.Exp).then_inc(k.sem("g_wexp"), 1)
            for n in range(1, N_EXP + 1):
                gate(n)

        @block.vector
        def _(dve):
            link = Order(dve, k.sem("dve_order"), k.dve_ordered).link
            update_dve(k, dve, link, "d", k.b1_qo[:, 1, :], True)
            dve.wait_ge(k.sem("e_w_in"), 16 * 7)
            for n in by_dve:
                w, m = jobs[n]
                dve.wait_ge(k.sem("e_job"), n + 1)
                if w == 0:
                    for half in range(2):
                        ins = v.tensor_scalar(k.e_qT[:, 2 * m + half, :], k.ps[:, 4 + n % 4, half * S:(half + 1) * S],
                                              k.e_bqk[:, 0, 2 * m + half:2 * m + half + 1], 1.0 / np.sqrt(E_DH), ALU.add, ALU.mult)
                else:
                    cols = slice((m % 2) * 512, (m % 2 + 1) * 512)
                    ins = v.tensor_tensor(k.e_v[:, m // 2, cols], k.ps[:, 4 + n % 4, :], k.e_bv[:, cols], ALU.add)
                ins.then_inc(k.sem("e_dve"), 1)
            small_dve(k, dve, causal)
            dve.wait_ge(k.sem("small_out"), causal.base + len(causal.pairs))
            v.tensor_copy(k.e_oT.rearrange("p (b g) i c -> p b (g i c)", b=4), k.ps[:, 4:8, :]).then_inc(k.sem("e_oT"), 1)
            xf = k.x[:, :, :].rearrange("p t d -> p (t d)")
            dve.wait_ge(k.sem("e_y"), 1)
            link(v.scalar_tensor_tensor(out=xf, in0=k.ps[:, 1, :], scalar=1.0 / np.sqrt(E_DH), in1=xf, op0=ALU.mult, op1=ALU.add))
            layer_norm(k, dve, link, k.x, k.x_ffn, k.sem("f_x0"))
            dve.wait_ge(k.sem("f_x0"), QT)
            rms_norm(k, dve, link, k.x_ffn, k.sem("f_xn"))
            dve.wait_ge(k.sem("f_w_in"), 16 * 9)
            weigh_turned(k, dve, 0, k.sem("f_xnT_ps"), k.sem("f_xnT"))
            dve.wait_ge(k.sem("f_proj"), 1)
            v.tensor_scalar(k.f_qT.rearrange("p t q -> p (t q)"), k.ps[:, 3, :], 1.0 / np.sqrt(E_DH), None, ALU.mult).then_inc(k.sem("f_qkv"), 1)
            small_dve(k, dve, latent)
            dve.wait_ge(k.sem("small_out"), latent.base + len(latent.pairs))
            v.tensor_copy(k.oT[:, :, :].rearrange("p c q -> p (c q)"), k.ps[:, 4, :]).then_inc(k.sem("f_oT"), 1)
            dve.wait_ge(k.sem("f_y"), 1)
            x_ffn = k.x_ffn[:, :, :].rearrange("p t d -> p (t d)")
            link(v.tensor_tensor(x_ffn, x_ffn, k.ps[:, 1, :], ALU.add))
            rms_norm(k, dve, link, k.x_ffn, k.sem("g_xn"))
            link(v.tensor_tensor(xf, xf, x_ffn, ALU.add))
            weigh_turned(k, dve, 1, k.sem("g_xnT_ps"), k.sem("g_xnT"))
            dve.wait_ge(k.sem("g_logits"), 1)
            link(v.tensor_copy(k.f_lg[:, :, :], k.ps[:, 7, 0:QT * N_EXP].rearrange("p (q e) -> p q e", q=QT)))
            link(v.tensor_reduce(k.f_w[:, 3, :], k.f_lg[:, :, :], AX.X, ALU.max))
            of_row = lambda a: a.unsqueeze(2).to_broadcast([P, QT, N_EXP])
            v.tensor_tensor(k.f_lg[:, :, :], k.f_lg[:, :, :], of_row(k.f_w[:, 3, :]), ALU.subtract).then_inc(k.sem("g_lg"), 1)
            dve.wait_ge(k.sem("g_rexp"), 1)
            link(v.tensor_reduce(k.f_w[:, 3, :], k.f_rw[:, :, :], AX.X, ALU.add))
            link(v.reciprocal(k.f_w[:, 3, :], k.f_w[:, 3, :]))
            link(v.tensor_tensor(k.f_rw[:, :, :], k.f_rw[:, :, :], of_row(k.f_w[:, 3, :]), ALU.mult))
            for q in range(QT):
                others = k.f_rw[:, q, :].unsqueeze(1).to_broadcast([P, N_EXP, N_EXP])
                own = k.f_rw[:, q, :].unsqueeze(2).to_broadcast([P, N_EXP, N_EXP])
                link(v.tensor_tensor(k.f_gt[:, q], others, own, ALU.is_gt))
                link(v.tensor_tensor(k.f_eq[:, q], others, own, ALU.is_equal))
            dve.wait_ge(k.sem("pool_order"), k.pool_ordered[0])
            link(v.tensor_tensor(k.f_eq[:, :, :, :], k.f_eq[:, :, :, :], k.f_low[:, :, :].unsqueeze(1).to_broadcast([P, QT, N_EXP, N_EXP]), ALU.mult))
            link(v.tensor_tensor(k.f_gt[:, :, :, :], k.f_gt[:, :, :, :], k.f_eq[:, :, :, :], ALU.add))
            link(v.tensor_reduce(k.f_rank[:, :, :], k.f_gt[:, :, :, :], AX.X, ALU.add))
            for n in range(2):
                link(v.tensor_scalar(k.f_sel[:, n], k.f_rank[:, :, :], float(n), None, ALU.is_equal))
                link(v.tensor_tensor(k.f_pick[:, n], k.f_sel[:, n], k.f_rw[:, :, :], ALU.mult))
            link(v.tensor_reduce(k.f_p[:, :, :], k.f_pick[:, :, :, :], AX.X, ALU.add))
            v.tensor_tensor(k.f_w[:, 0, :], k.f_p[:, 1, :], k.f_p[:, 0, :], ALU.subtract).then_inc(k.sem("g_diff"), 1)

            def hidden(n):
                b = n % 2
                dve.wait_ge(k.sem("g_tanh"), n + 1)
                if n >= 2:
                    dve.wait_ge(k.sem("g_rows"), n - 1)
                link(v.scalar_tensor_tensor(out=k.f_gate[:, b, :], in0=k.f_tanh[:, b, :], scalar=1.0, in1=k.ps[:, b, :],
                                            op0=ALU.add, op1=ALU.mult))
                v.scalar_tensor_tensor(out=k.f_hT[:, b].rearrange("p t q -> p (t q)"), in0=k.f_gate[:, b, :], scalar=0.5,
                                       in1=k.ps[:, 2 + b, :], op0=ALU.mult, op1=ALU.mult).then_inc(k.sem("g_h"), 1)

            hidden(0)
            dve.wait_ge(k.sem("g_wexp"), 1)
            link(v.tensor_scalar(k.f_w[:, 2, :], k.f_w[:, 1, :], 1.0, None, ALU.add))
            link(v.reciprocal(k.f_w[:, 2, :], k.f_w[:, 2, :]))
            link(v.tensor_tensor(k.f_w[:, 3, :], k.f_w[:, 1, :], k.f_w[:, 2, :], ALU.mult))
            for n in range(2):
                link(v.tensor_tensor(k.f_sel[:, n], k.f_sel[:, n], of_row(k.f_w[:, 2 + n, :]), ALU.mult))
            link(v.tensor_tensor(k.f_comb[:, :, 0:N_EXP], k.f_sel[:, 0], k.f_sel[:, 1], ALU.add))
            for n in range(N_EXP + 1):
                if n < N_EXP:
                    hidden(n + 1)
                dve.wait_ge(k.sem("g_rows"), n + 1)
                if n >= 1:
                    dve.wait_ge(k.sem("f_x"), 2 * n)
                for q in range(QT):
                    v.scalar_tensor_tensor(out=k.x[:, q, :], in0=k.ps[:, 4 + n % 2, q * D:(q + 1) * D],
                                           scalar=k.f_comb[:, q, experts[n]:experts[n] + 1], in1=k.x[:, q, :],
                                           op0=ALU.mult, op1=ALU.add).then_inc(k.sem("f_x"), 1)


def program(nc, ins, out):
    with ExitStack() as ctx:
        k = Kern(nc, ctx, ins, out)
        allocate(k)
        stage_prepare(k)
        stage_cross0(k)
        stage_self0(k)
        stage_cross1_prepare(k)
        stage_cross1(k)
        stage_self1(k)


def _t(a):
    return np.ascontiguousarray(np.swapaxes(a, -1, -2))


def lay_out(inputs):
    a = {n: np.asarray(v) for n, v in inputs.items()}
    out = {n: a[n] for n in ("x", "ctx_1024", "L1_xattn_bk", "L1_xattn_bv")}
    out["L0_xattn_scale"] = a["L0_xattn_scale"].reshape(1, 1)
    out["L0_xattn_log_C"] = a["L0_xattn_log_C"].reshape(1, 1)
    out["mask_bk0_by_chunk"] = a["mask_Bx1xS2_bk0"].reshape(NCH, P).T
    out["ctxT"] = _t(a["ctx_1024"][0])
    for n in ("L0_attn_b_qkv", "L0_attn_b_proj", "L0_attn_qn_w", "L0_attn_kn_w", "L1_xattn_bq", "L1_xattn_bo",
              "mask_Bx1xSxS2_bf1"):
        out[n] = a[n]
    for n, c in (("bq", "cols"), ("bk", "cols"), ("bv", "row")):
        b = a["L1_attn_" + n].reshape(-1)
        out[f"L1_attn_{n}_{c}"] = b.reshape(E_T, P).T if c == "cols" else b[None]
    for n in ("Wq", "Wk", "Wv"):
        out[f"L1_attn_{n}T"] = _t(a["L1_attn_" + n].reshape(2 * E_T * E_DH, D))
    for n in ("g1", "g2"):
        out[f"L1_ffn_{n}_cols"] = a["L1_ffn_" + n].reshape(KT, P).T
    for n in ("Wq", "Wkc", "Wvc", "Wo", "Wr", "sW1", "sW2", "sW3", "eW1", "eW2", "eW3"):
        out[f"L1_ffn_{n}T"] = _t(a["L1_ffn_" + n])
    for n in ("L1_attn_proj", "L1_ffn_expert_bias"):
        out[n] = a[n]
    for n in ("L0_attn_w_qkv", "L0_attn_w_proj", "L0_ffn_weight", "L0_xattn_W_out", "L1_xattn_Wk", "L1_xattn_Wv", "L1_xattn_Wq", "L1_xattn_Wo"):
        out[n + "T"] = _t(a[n])
    return out


def kernel(**inputs):
    import concourse.bacc as bacc
    from concourse.bass_utils import run_bass_kernel_spmd

    nc = bacc.Bacc("TRN2", target_bir_lowering=False, num_devices=1)
    arrays, ins = {}, {}
    for name, a in lay_out(inputs).items():
        a = np.ascontiguousarray(a)
        arrays[name] = a
        ins[name] = nc.dram_tensor(name, a.shape, mybir.dt.from_np(a.dtype), kind="ExternalInput").ap()
    out = nc.dram_tensor("out", (1, S, D), F32, kind="ExternalOutput").ap()
    program(nc, ins, out)
    r = run_bass_kernel_spmd(nc, [arrays], core_ids=[0])
    return r.results[0]["out"]
```
